# Optimizing a Trainium2 kernel written in Bass

```python
import numpy as np
import jax
import jax.numpy as jnp

def _softmax(x, axis=-1):
    return jax.nn.softmax(x, axis=axis)

def _gelu(x):
    return jax.nn.gelu(x, approximate=True)

def _silu(x):
    return jax.nn.silu(x)

def _sigmoid(x):
    return jax.nn.sigmoid(x)

def _layernorm(x, axis=-1, eps=1e-05):
    m = jnp.mean(x, axis=axis, keepdims=True)
    v = jnp.var(x, axis=axis, keepdims=True)
    return (x - m) / jnp.sqrt(v + eps)

def _scatter_add(tgt, idx, src, axis=0):
    return tgt.at[idx].add(src)

def _segment_sum(src, seg, n):
    return jax.ops.segment_sum(src, seg, n)
kernel_name = 'mk_prb_d2_jaxref_r8_79cd21'

def setup_inputs(seed: int=0):
    np.random.seed(seed)
    _w = jnp.asarray

    def _L0_attn_setup():
        import jax, jax.numpy as jnp
        import numpy as np
        B, L, D, H, DK, DV = (2, 128, 128, 16, 64, 64)
        EPS = 1e-05

        def _silu(x):
            return x * jax.nn.sigmoid(x)
        key = jax.random.key(seed)
        ks = jax.random.split(key, 16)
        w = lambda k, shp: jax.random.normal(k, shp, dtype=jnp.float32) * 0.02
        return {'hidden_states': jax.random.normal(ks[0], (B, L, D), jnp.float32), 'Wq': w(ks[1], (D, H * DK)), 'bq': jnp.zeros((H * DK,), jnp.float32), 'Wk': w(ks[2], (D, H * DK)), 'bk': jnp.zeros((H * DK,), jnp.float32), 'Wv': w(ks[3], (D, H * DV)), 'bv': jnp.zeros((H * DV,), jnp.float32), 'Wb': w(ks[4], (D, H)), 'bb': jnp.zeros((H,), jnp.float32), 'Wfd': w(ks[5], (D, H)), 'bfd': jnp.zeros((H,), jnp.float32), 'fast_decay_bias': jnp.full((H,), -1.0, jnp.float32), 'Wsd': w(ks[6], (D, H)), 'bsd': jnp.zeros((H,), jnp.float32), 'slow_decay_bias': jnp.full((H,), 2.0, jnp.float32), 'Wfg': w(ks[7], (D, H)), 'bfg': jnp.zeros((H,), jnp.float32), 'Wsg': w(ks[8], (D, H)), 'bsg': jnp.zeros((H,), jnp.float32), 'Wg': w(ks[9], (D, H * DV)), 'bg': jnp.zeros((H * DV,), jnp.float32), 'onorm_w': jnp.ones((DV,), jnp.float32), 'Wo': w(ks[10], (H * DV, D)), 'bo': jnp.zeros((D,), jnp.float32), 'resonance_flux': jnp.float32(0.05)}
    _L0_attn_in = _L0_attn_setup()

    def _L0_ffn_setup():
        import jax, jax.numpy as jnp
        import numpy as np
        BLOCK = 16
        _GRID = jnp.array([0.0, 0.5, 1.0, 1.5, 2.0, 3.0, 4.0, 6.0], dtype=jnp.float32)
        _MID = jnp.array([0.25, 0.75, 1.25, 1.75, 2.5, 3.5, 5.0], dtype=jnp.float32)

        def fp4_quant_dequant(x):
            shape = x.shape
            xb = x.reshape(shape[:-1] + (shape[-1] // BLOCK, BLOCK))
            scale = jnp.max(jnp.abs(xb), axis=-1, keepdims=True) / 6.0
            scale = jnp.maximum(scale, jnp.float32(1e-12))
            xn = xb / scale
            idx = jnp.searchsorted(_MID, jnp.abs(xn))
            q = _GRID[idx] * jnp.sign(xn) * scale
            return q.reshape(shape)

        def fp4_linear(x, w):
            xq = fp4_quant_dequant(x)
            wq = fp4_quant_dequant(w)
            return jnp.einsum('bsk,nk->bsn', xq, wq)
        key = jax.random.key(seed)
        k1, k2, k3, k4 = jax.random.split(key, 4)
        H, I = (128, 352)
        x = jax.random.normal(k1, (4, 512, H), dtype=jnp.float32)
        w_gate = jax.random.normal(k2, (I, H), dtype=jnp.float32) * 0.02
        w_up = jax.random.normal(k3, (I, H), dtype=jnp.float32) * 0.02
        w_down = jax.random.normal(k4, (H, I), dtype=jnp.float32) * 0.02
        return {'x': x, 'w_gate': w_gate, 'w_up': w_up, 'w_down': w_down}
    _L0_ffn_in = _L0_ffn_setup()

    def _L1_attn_setup():
        import jax, jax.numpy as jnp
        import numpy as np
        DIM = 128
        H = 16
        D = DIM // H
        SCALE = D ** (-0.5)
        key = jax.random.key(seed)
        ks = jax.random.split(key, 7)
        B, N = (2, 256)
        x = jax.random.normal(ks[0], (B, N, DIM), dtype=jnp.float32)
        y = jax.random.normal(ks[1], (B, N, DIM), dtype=jnp.float32)
        s = DIM ** (-0.5)
        Wq = jax.random.normal(ks[2], (DIM, DIM), dtype=jnp.float32) * s
        Wk = jax.random.normal(ks[3], (DIM, DIM), dtype=jnp.float32) * s
        Wv = jax.random.normal(ks[4], (DIM, DIM), dtype=jnp.float32) * s
        Wp = jax.random.normal(ks[5], (DIM, DIM), dtype=jnp.float32) * s
        bp = jnp.zeros((DIM,), dtype=jnp.float32)
        return {'x': x, 'y': y, 'Wq': Wq, 'Wk': Wk, 'Wv': Wv, 'Wp': Wp, 'bp': bp}
    _L1_attn_in = _L1_attn_setup()

    def _L1_ffn_setup():
        import jax, jax.numpy as jnp
        import numpy as np
        D_MODEL = 128
        D_HIDDEN = 512
        NUM_EXPERTS = 8
        B, T = (2, 256)
        key = jax.random.key(seed)
        ks = jax.random.split(key, 8)
        s = 0.02
        x = jax.random.normal(ks[0], (B, T, D_MODEL), dtype=jnp.float32)
        Wg = jax.random.normal(ks[1], (D_MODEL, NUM_EXPERTS), dtype=jnp.float32) * s
        bg = jnp.zeros((NUM_EXPERTS,), dtype=jnp.float32)
        W1 = jax.random.normal(ks[2], (NUM_EXPERTS, D_MODEL, D_HIDDEN), dtype=jnp.float32) * s
        b1 = jnp.zeros((NUM_EXPERTS, D_HIDDEN), dtype=jnp.float32)
        W2 = jax.random.normal(ks[3], (NUM_EXPERTS, D_HIDDEN, D_MODEL), dtype=jnp.float32) * s
        b2 = jnp.zeros((NUM_EXPERTS, D_MODEL), dtype=jnp.float32)
        return {'x': x, 'Wg': Wg, 'bg': bg, 'W1': W1, 'b1': b1, 'W2': W2, 'b2': b2}
    _L1_ffn_in = _L1_ffn_setup()
    _d = {'L0_attn_hidden_states': _L0_attn_in['hidden_states'], 'L0_attn_Wq': _L0_attn_in['Wq'], 'L0_attn_bq': _L0_attn_in['bq'], 'L0_attn_Wk': _L0_attn_in['Wk'], 'L0_attn_bk': _L0_attn_in['bk'], 'L0_attn_Wv': _L0_attn_in['Wv'], 'L0_attn_bv': _L0_attn_in['bv'], 'L0_attn_Wb': _L0_attn_in['Wb'], 'L0_attn_bb': _L0_attn_in['bb'], 'L0_attn_Wfd': _L0_attn_in['Wfd'], 'L0_attn_bfd': _L0_attn_in['bfd'], 'L0_attn_fast_decay_bias': _L0_attn_in['fast_decay_bias'], 'L0_attn_Wsd': _L0_attn_in['Wsd'], 'L0_attn_bsd': _L0_attn_in['bsd'], 'L0_attn_slow_decay_bias': _L0_attn_in['slow_decay_bias'], 'L0_attn_Wfg': _L0_attn_in['Wfg'], 'L0_attn_bfg': _L0_attn_in['bfg'], 'L0_attn_Wsg': _L0_attn_in['Wsg'], 'L0_attn_bsg': _L0_attn_in['bsg'], 'L0_attn_Wg': _L0_attn_in['Wg'], 'L0_attn_bg': _L0_attn_in['bg'], 'L0_attn_onorm_w': _L0_attn_in['onorm_w'], 'L0_attn_Wo': _L0_attn_in['Wo'], 'L0_attn_bo': _L0_attn_in['bo'], 'L0_attn_resonance_flux': _L0_attn_in['resonance_flux'], 'L0_ffn_w_gate': _L0_ffn_in['w_gate'], 'L0_ffn_w_up': _L0_ffn_in['w_up'], 'L0_ffn_w_down': _L0_ffn_in['w_down'], 'L1_attn_y': _L1_attn_in['y'], 'L1_attn_Wq': _L1_attn_in['Wq'], 'L1_attn_Wk': _L1_attn_in['Wk'], 'L1_attn_Wv': _L1_attn_in['Wv'], 'L1_attn_Wp': _L1_attn_in['Wp'], 'L1_attn_bp': _L1_attn_in['bp'], 'L1_ffn_Wg': _L1_ffn_in['Wg'], 'L1_ffn_bg': _L1_ffn_in['bg'], 'L1_ffn_W1': _L1_ffn_in['W1'], 'L1_ffn_b1': _L1_ffn_in['b1'], 'L1_ffn_W2': _L1_ffn_in['W2'], 'L1_ffn_b2': _L1_ffn_in['b2']}
    _x0 = _d['L0_attn_hidden_states']
    _d['L0_attn_hidden_states'] = jax.random.normal(jax.random.fold_in(jax.random.key(seed), 1), (4, 1024, 128), dtype=_x0.dtype)
    del _x0
    return _d

def reference(L0_attn_hidden_states, L0_attn_Wq, L0_attn_bq, L0_attn_Wk, L0_attn_bk, L0_attn_Wv, L0_attn_bv, L0_attn_Wb, L0_attn_bb, L0_attn_Wfd, L0_attn_bfd, L0_attn_fast_decay_bias, L0_attn_Wsd, L0_attn_bsd, L0_attn_slow_decay_bias, L0_attn_Wfg, L0_attn_bfg, L0_attn_Wsg, L0_attn_bsg, L0_attn_Wg, L0_attn_bg, L0_attn_onorm_w, L0_attn_Wo, L0_attn_bo, L0_attn_resonance_flux, L0_ffn_w_gate, L0_ffn_w_up, L0_ffn_w_down, L1_attn_y, L1_attn_Wq, L1_attn_Wk, L1_attn_Wv, L1_attn_Wp, L1_attn_bp, L1_ffn_Wg, L1_ffn_bg, L1_ffn_W1, L1_ffn_b1, L1_ffn_W2, L1_ffn_b2):

    def _L0_attn_ref(hidden_states, Wq, bq, Wk, bk, Wv, bv, Wb, bb, Wfd, bfd, fast_decay_bias, Wsd, bsd, slow_decay_bias, Wfg, bfg, Wsg, bsg, Wg, bg, onorm_w, Wo, bo, resonance_flux):
        import jax, jax.numpy as jnp
        import numpy as np
        B, L, D, H, DK, DV = (2, 128, 128, 16, 64, 64)
        EPS = 1e-05

        def _silu(x):
            return x * jax.nn.sigmoid(x)
        Bn, Ln, Dn = hidden_states.shape
        hs = hidden_states
        q = _silu(hs @ Wq + bq).reshape(Bn, Ln, H, DK).transpose(0, 2, 1, 3)
        k = _silu(hs @ Wk + bk).reshape(Bn, Ln, H, DK).transpose(0, 2, 1, 3)
        v = _silu(hs @ Wv + bv).reshape(Bn, Ln, H, DV).transpose(0, 2, 1, 3)
        beta = jax.nn.sigmoid(hs @ Wb + bb).transpose(0, 2, 1)
        fd = jax.nn.sigmoid(hs @ Wfd + bfd + fast_decay_bias).transpose(0, 2, 1)
        sd = jax.nn.sigmoid(hs @ Wsd + bsd + slow_decay_bias).transpose(0, 2, 1)
        fg = jax.nn.sigmoid(hs @ Wfg + bfg).transpose(0, 2, 1)
        sg = jax.nn.sigmoid(hs @ Wsg + bsg).transpose(0, 2, 1)
        q = q * jax.lax.rsqrt(jnp.sum(q * q, axis=-1, keepdims=True) + 1e-06)
        k = k * jax.lax.rsqrt(jnp.sum(k * k, axis=-1, keepdims=True) + 1e-06)
        xs = (q.transpose(2, 0, 1, 3), k.transpose(2, 0, 1, 3), v.transpose(2, 0, 1, 3), beta.transpose(2, 0, 1), fd.transpose(2, 0, 1), sd.transpose(2, 0, 1), fg.transpose(2, 0, 1), sg.transpose(2, 0, 1))
        S0 = jnp.zeros((Bn, H, DK, DV), hs.dtype)
        rf = resonance_flux

        def _cap(S):
            n = jnp.sqrt(jnp.sum(S * S, axis=(-2, -1), keepdims=True))
            return S / jnp.maximum(1.0, n / float(DK))

        def step(carry, x):
            S_f, S_s = carry
            qt, kt, vt, bt, fdt, sdt, fgt, sgt = x
            S_f = fdt[..., None, None] * S_f
            S_s = sdt[..., None, None] * S_s
            err_f = vt - jnp.einsum('bhk,bhkv->bhv', kt, S_f)
            err_s = vt - jnp.einsum('bhk,bhkv->bhv', kt, S_s)
            bkt = bt[..., None, None] * kt[..., :, None]
            S_f = S_f + bkt * err_f[..., None, :]
            S_s = S_s + bkt * err_s[..., None, :]
            S_fc = _cap(S_f + rf * S_s)
            S_sc = _cap(S_s + rf * S_f)
            ot = fgt[..., None] * jnp.einsum('bhk,bhkv->bhv', qt, S_fc) + sgt[..., None] * jnp.einsum('bhk,bhkv->bhv', qt, S_sc)
            return ((S_fc, S_sc), ot)
        _, o = jax.lax.scan(step, (S0, S0), xs)
        o = o.transpose(1, 0, 2, 3)
        g = (hs @ Wg + bg).reshape(Bn, Ln, H, DV)
        o = o * jax.lax.rsqrt(jnp.mean(o * o, axis=-1, keepdims=True) + EPS)
        o = o * onorm_w * _silu(g)
        o = o.reshape(Bn, Ln, H * DV) @ Wo + bo
        return o

    def _L0_ffn_ref(x, w_gate, w_up, w_down):
        import jax, jax.numpy as jnp
        import numpy as np
        BLOCK = 16
        _GRID = jnp.array([0.0, 0.5, 1.0, 1.5, 2.0, 3.0, 4.0, 6.0], dtype=jnp.float32)
        _MID = jnp.array([0.25, 0.75, 1.25, 1.75, 2.5, 3.5, 5.0], dtype=jnp.float32)

        def fp4_quant_dequant(x):
            shape = x.shape
            xb = x.reshape(shape[:-1] + (shape[-1] // BLOCK, BLOCK))
            scale = jnp.max(jnp.abs(xb), axis=-1, keepdims=True) / 6.0
            scale = jnp.maximum(scale, jnp.float32(1e-12))
            xn = xb / scale
            idx = jnp.searchsorted(_MID, jnp.abs(xn))
            q = _GRID[idx] * jnp.sign(xn) * scale
            return q.reshape(shape)

        def fp4_linear(x, w):
            xq = fp4_quant_dequant(x)
            wq = fp4_quant_dequant(w)
            return jnp.einsum('bsk,nk->bsn', xq, wq)
        gate = fp4_linear(x, w_gate)
        y = fp4_linear(x, w_up)
        h = jax.nn.silu(gate) * y
        return fp4_linear(h, w_down)

    def _L1_attn_ref(x, y, Wq, Wk, Wv, Wp, bp):
        import jax, jax.numpy as jnp
        import numpy as np
        DIM = 128
        H = 16
        D = DIM // H
        SCALE = D ** (-0.5)
        B, N, C = x.shape
        q = (x @ Wq.T).reshape(B, N, H, D)
        k = (x @ Wk.T).reshape(B, N, H, D)
        v = (x @ Wv.T).reshape(B, N, H, D)
        attn = jnp.einsum('bnhd,blhd->bhnl', q, k)
        causal = jnp.triu(jnp.ones((N, N), dtype=bool), k=1)
        attn = jnp.where(causal[None, None], -jnp.inf, attn)
        attn = jax.nn.softmax(SCALE * attn, axis=-1)
        out = jnp.einsum('bhnl,blhd->bnhd', attn, v).reshape(B, N, C)
        return out @ Wp.T + bp

    def _L1_ffn_ref(x, Wg, bg, W1, b1, W2, b2):
        import jax, jax.numpy as jnp
        import numpy as np
        D_MODEL = 128
        D_HIDDEN = 512
        NUM_EXPERTS = 8
        B, T = (2, 256)
        gate_logits = jnp.einsum('btd,de->bte', x, Wg) + bg
        gate_scores = jax.nn.softmax(gate_logits, axis=-1)
        top1_idx = jnp.argmax(gate_scores, axis=-1)
        top1_mask = jax.nn.one_hot(top1_idx, NUM_EXPERTS, dtype=x.dtype)
        top1_weight = jnp.sum(gate_scores * top1_mask, axis=-1, keepdims=True)
        h = jax.nn.silu(jnp.einsum('btd,edh->bteh', x, W1) + b1)
        o = jnp.einsum('bteh,ehd->bted', h, W2) + b2
        y = jnp.sum(o * top1_mask[..., None], axis=2) * top1_weight
        return y
    x = L0_attn_hidden_states
    xn = _layernorm(x, axis=-1)
    x = x + _L0_attn_ref(xn, L0_attn_Wq, L0_attn_bq, L0_attn_Wk, L0_attn_bk, L0_attn_Wv, L0_attn_bv, L0_attn_Wb, L0_attn_bb, L0_attn_Wfd, L0_attn_bfd, L0_attn_fast_decay_bias, L0_attn_Wsd, L0_attn_bsd, L0_attn_slow_decay_bias, L0_attn_Wfg, L0_attn_bfg, L0_attn_Wsg, L0_attn_bsg, L0_attn_Wg, L0_attn_bg, L0_attn_onorm_w, L0_attn_Wo, L0_attn_bo, L0_attn_resonance_flux) + _L0_ffn_ref(xn, L0_ffn_w_gate, L0_ffn_w_up, L0_ffn_w_down)
    xn = _layernorm(x, axis=-1)
    x = x + _L1_attn_ref(xn, L1_attn_y, L1_attn_Wq, L1_attn_Wk, L1_attn_Wv, L1_attn_Wp, L1_attn_bp) + _L1_ffn_ref(xn, L1_ffn_Wg, L1_ffn_bg, L1_ffn_W1, L1_ffn_b1, L1_ffn_W2, L1_ffn_b2)
    return x

_drawn_inputs = setup_inputs


def setup_inputs(seed=0):
    import zlib

    import numpy as np

    out = dict(_drawn_inputs(seed))
    spreads = {'L0_attn_bq': (0.0, 0.1),
     'L0_attn_bk': (0.0, 0.1),
     'L0_attn_bv': (0.0, 0.1),
     'L0_attn_bb': (0.0, 2.0),
     'L0_attn_bfd': (0.0, 2.0),
     'L0_attn_fast_decay_bias': (-1.0, 0.6),
     'L0_attn_bsd': (0.0, 2.0),
     'L0_attn_slow_decay_bias': (2.0, 0.6),
     'L0_attn_bfg': (0.0, 2.0),
     'L0_attn_bsg': (0.0, 2.0),
     'L0_attn_bg': (0.0, 0.1),
     'L0_attn_onorm_w': (1.0, 0.6),
     'L0_attn_bo': (0.0, 0.1),
     'L1_attn_bp': (0.0, 0.1),
     'L1_ffn_bg': (0.0, 0.577),
     'L1_ffn_b1': (0.0, 0.8),
     'L1_ffn_b2': (0.0, 0.445)}
    factors = {'L0_attn_Wb': 8.0,
     'L0_attn_Wfd': 8.0,
     'L0_attn_Wsd': 8.0,
     'L0_attn_Wfg': 22.309,
     'L0_attn_Wsg': 22.272,
     'L0_ffn_w_gate': 5.521,
     'L0_ffn_w_up': 5.348,
     'L0_ffn_w_down': 5.38,
     'L1_ffn_Wg': 2.951,
     'L1_ffn_W1': 6.217,
     'L1_ffn_W2': 5.652}
    for name, (base, spread) in spreads.items():
        noise = np.random.default_rng([zlib.crc32(name.encode()), seed]).standard_normal(out[name].shape)
        drawn = base * np.exp(spread * noise) if base else spread * noise
        out[name] = jnp.asarray(drawn.astype(out[name].dtype))
    for name, factor in factors.items():
        out[name] = (out[name] * factor).astype(out[name].dtype)
    return out
```

```python
from contextlib import ExitStack

import concourse.bass as bass
import numpy as np
from concourse import mybir

F32 = mybir.dt.float32
BF16 = mybir.dt.bfloat16
ALU = mybir.AluOpType
ACT = mybir.ActivationFunctionType
AX = mybir.AxisListType.X
ds = bass.ds

P = 128
D = 128
B, L = 4, 1024
T = B * L // P
H0, DK = 16, 64
HD = H0 * DK
INNER = 352
BLOCK = 16
H1, D1 = 16, 8
E1, HID = 8, 512
LN_EPS = 1e-5
TB = L // P
STEPS = 4
MASKED = -1e30


class Count:

    def __init__(self, eng, sem, per=0):
        self.eng, self.sem, self.per, self.base, self.n = eng, sem, per, 0, 0

    def start(self, i):
        self.base, self.n = i * self.per, 0

    def done(self, ins):
        self.n += 1
        ins.then_inc(self.sem, 1)

    def link(self, ins):
        self.done(ins)
        self.eng.wait_ge(self.sem, self.base + self.n)

    def end(self):
        assert self.n == self.per, (self.n, self.per)


def layer_kernel(nc, a, out, stop=9):
    ctx = ExitStack()
    with ctx:
        def sem(name):
            return ctx.enter_context(nc.semaphore(name))

        def sb(name, shape, dt=F32, scope=ctx):
            return scope.enter_context(nc.sbuf_tensor(name, shape, dt))

        def dram(name, shape):
            return nc.dram_tensor(name, shape, F32, kind="Internal").ap()

        proj_s = dram("proj_s", (B * L, 4 * HD))
        gates_s = dram("gates_s", (5 * H0, B * L))
        mem_s = dram("mem_s", (2, B * L, HD))

        banks = ctx.enter_context(nc.psum_tensor("banks", [P, 8 * 512], F32))
        bank = [banks[:, 512 * n:512 * n + 512] for n in range(8)]

        res = sb("res", [P, T, D])
        xn = sb("xn", [P, T, D])
        xnT = sb("xnT", [P, B * L])
        ident = sb("ident", [P, P])
        ones_row = sb("ones_row", [1, P])
        stats = sb("stats", [P, 4, T])

        s1 = ExitStack()
        xq = sb("xq", [P, T, D], scope=s1)
        fa = sb("fa", [P, T * D], scope=s1)
        fc = sb("fc", [P, T * D], scope=s1)
        fsg = sb("fsg", [P, T * D], scope=s1)
        fsc = sb("fsc", [P, 2, T * D // BLOCK], scope=s1)
        NW = 6 * P + INNER
        wraw = sb("wraw", [P, NW], scope=s1)
        wqt = sb("wqt", [P, NW], scope=s1)
        wguT = sb("wguT", [P, 2, 3 * P], scope=s1)
        wdT = sb("wdT", [P, 3, P], scope=s1)
        st_n = sb("st_n", [P, P], scope=s1)
        st_q = sb("st_q", [P, P], scope=s1)
        xqT = sb("xqT", [P, P], scope=s1)
        silu_g = sb("silu_g", [P, INNER], scope=s1)
        hid = sb("hid", [P, INNER], scope=s1)
        hq = sb("hq", [P, INNER], scope=s1)
        hqT = sb("hqT", [P, 3, P], scope=s1)
        s1.close()

        s2 = ExitStack()
        wproj = sb("wproj", [P, 4 * HD], scope=s2)
        bproj = sb("bproj", [1, 4 * HD], scope=s2)
        wgate = sb("wgate", [P, 5 * H0], scope=s2)
        bgate = sb("bgate", [5 * H0, 3], scope=s2)
        gates = sb("gates", [5 * H0, B * L], scope=s2)
        st_p = sb("st_p", [P, P], scope=s2)
        prj = sb("prj", [P, 4 * HD], scope=s2)
        prj_sq = sb("prj_sq", [P, 2 * HD], scope=s2)
        prj_n = sb("prj_n", [P, 2, 2 * H0], scope=s2)
        s2.close()

        s3 = ExitStack()
        S = sb("S", [P, DK, DK], scope=s3)
        prod = sb("prod", [P, DK, DK], scope=s3)
        outer = sb("outer", [P, DK, DK], scope=s3)
        Snew = sb("Snew", [P, DK * DK], scope=s3)
        junk = sb("junk", [P, 8 * 512], BF16, scope=s3)
        qkv = sb("qkv", [P, 2, 3, STEPS, DK], scope=s3)
        obuf = sb("obuf", [P, 2, STEPS, DK], scope=s3)
        gbeta = sb("gbeta", [P, L], scope=s3)
        gdec = sb("gdec", [P, L], scope=s3)
        gndec = sb("gndec", [P, L], scope=s3)
        gout = sb("gout", [P, L], scope=s3)
        mix = sb("mix", [P, P], scope=s3)
        rf_col = sb("rf_col", [P, 1], scope=s3)
        small = sb("small", [P, 4, DK], scope=s3)
        gcur = sb("gcur", [P, 4, 2 * STEPS], scope=s3)
        cap = sb("cap", [P, 6], scope=s3)
        s3.close()

        s4 = ExitStack()
        om = sb("om", [P, 3, HD], scope=s4)
        osq = sb("osq", [P, HD], scope=s4)
        orn = sb("orn", [P, H0], scope=s4)
        og = sb("og", [P, HD], scope=s4)
        ogT = sb("ogT", [P, 8, P], scope=s4)
        wout = sb("wout", [P, 8, D], scope=s4)
        bout = sb("bout", [1, D], scope=s4)
        onw = sb("onw", [P, DK], scope=s4)
        s4.close()

        s5 = ExitStack()
        SLOT = 9
        vaug = sb("vaug", [P, T, H1, SLOT], scope=s5)
        o_all = sb("o_all", [P, T, D], scope=s5)
        route = sb("route", [P, T, E1], scope=s5)
        s6 = ExitStack()
        wq1 = sb("wq1", [P, 4, P], scope=s6)
        wk1 = sb("wk1", [P, 4, P], scope=s6)
        wv1 = sb("wv1", [P, D], scope=s6)
        wg1 = sb("wg1", [P, E1], scope=s6)
        bg1 = sb("bg1", [P, E1], scope=s6)
        logit = sb("logit", [P, T, E1], scope=s6)
        rt = sb("rt", [P, 3, T, E1], scope=s6)
        rs = sb("rs", [P, 2, T], scope=s6)
        number_i = sb("number_i", [P, E1], mybir.dt.int32, scope=s6)
        number = sb("number", [P, E1], scope=s6)
        st_x = sb("st_x", [P, P], scope=s6)
        xt_x = sb("xt_x", [P, P], scope=s6)
        st_wq = sb("st_wq", [P, P], scope=s6)
        st_wk = sb("st_wk", [P, P], scope=s6)
        qpad = sb("qpad", [P, L], scope=s6)
        qaug = sb("qaug", [P, L], scope=s6)
        kaug = sb("kaug", [P, L], scope=s6)
        mxz = sb("mxz", [P, TB, P], scope=s6)
        row_one = sb("row_one", [P, 1], scope=s6)
        ident_b = sb("ident_b", [P, P], BF16, scope=s6)
        above = sb("above", [P, P], BF16, scope=s6)
        below = sb("below", [P, P], BF16, scope=s6)
        TRI = TB * (TB + 1) // 2 * P
        probs = sb("probs", [P, 2, TRI], scope=s6)
        inv_o = sb("inv_o", [P, 4, TB], scope=s6)
        s6.close()
        s7 = ExitStack()
        w1 = sb("w1", [P, E1, HID], scope=s7)
        w2 = sb("w2", [P, E1, HID // P, D], scope=s7)
        b1 = sb("b1", [P, E1, HID // P], scope=s7)
        b2 = sb("b2", [E1, D], scope=s7)
        wp1 = sb("wp1", [P, D], scope=s7)
        bp1 = sb("bp1", [1, D], scope=s7)
        st_o = sb("st_o", [P, P], scope=s7)
        oT1 = sb("oT1", [P, P], scope=s7)
        st_r = sb("st_r", [P, 4 * E1], scope=s7)
        rT = sb("rT", [E1, 4 * P], scope=s7)
        hT1 = sb("hT1", [P, 2, 4, 512], scope=s7)
        s7.close()
        s5.close()

        ld = sem("ld")
        ld1 = sem("ld1")
        const_set = sem("const_set")
        v_seq = sem("v_seq")
        norm_done = sem("norm_done")
        var_done = sem("var_done")
        std_done = sem("std_done")
        sign_done = sem("sign_done")
        wq_done = sem("wq_done")
        wt_done = sem("wt_done")
        wT_done = sem("wT_done")
        xq_done = sem("xq_done")
        staged = sem("staged")
        x_turned = sem("x_turned")
        xT_done = sem("xT_done")
        gu_done = sem("gu_done")
        silu_done = sem("silu_done")
        hid_done = sem("hid_done")
        hsign_done = sem("hsign_done")
        v_ffn = sem("v_ffn")
        hq_done = sem("hq_done")
        h_turned = sem("h_turned")
        hT_done = sem("hT_done")
        down_done = sem("down_done")
        ffn_added = sem("ffn_added")

        phase = sem("phase")
        ld2 = sem("ld2")
        p_staged = sem("p_staged")
        p_mm = sem("p_mm")
        p_silu = sem("p_silu")
        p_var = sem("p_var")
        p_std = sem("p_std")
        v_prj = sem("v_prj")
        p_normed = sem("p_normed")
        p_stored = sem("p_stored")
        g_bias = sem("g_bias")
        g_mm = sem("g_mm")
        g_done = sem("g_done")
        g_stored = sem("g_stored")
        ld3 = sem("ld3")
        swap_set = sem("swap_set")
        v_pre = sem("v_pre")
        r_ready = sem("r_ready")
        v_rec = sem("v_rec")
        qkv_in = [sem(f"qkv_in{n}") for n in range(2)]
        stepped = [sem(f"stepped{n}") for n in range(2)]
        updated = sem("updated")
        mixed = sem("mixed")
        squared = sem("squared")
        ratio_set = sem("ratio_set")
        ratio_root = sem("ratio_root")
        lam_set = sem("lam_set")
        state_set = sem("state_set")
        state_read = sem("state_read")
        o_stored = [sem(f"o_stored{n}") for n in range(2)]
        ld4 = sem("ld4")
        om_in = sem("om_in")
        v_out = sem("v_out")
        o_var = sem("o_var")
        o_std = sem("o_std")
        og_set = sem("og_set")
        og_turned = sem("og_turned")
        ogT_set = sem("ogT_set")
        o_mm = sem("o_mm")
        o_added = sem("o_added")

        ld5 = sem("ld5")
        mask_set = sem("mask_set")
        c_set = sem("c_set")
        x1_staged = sem("x1_staged")
        x1_turned = sem("x1_turned")
        x1T_set = sem("x1T_set")
        v_mm = sem("v_mm")
        v_set = sem("v_set")
        w_staged = sem("w_staged")
        pj_mm = sem("pj_mm")
        v_qk = sem("v_qk")
        qk_set = sem("qk_set")
        a_mm = sem("a_mm")
        mx_read = sem("mx_read")
        mx_turned = sem("mx_turned")
        v_qaug = sem("v_qaug")
        qaug_set = sem("qaug_set")
        b_mm = sem("b_mm")
        exp_done = sem("exp_done")
        c_mm = sem("c_mm")
        v_on = sem("v_on")
        o_norm = sem("o_norm")
        ld6 = sem("ld6")
        o_staged = sem("o_staged")
        o1_turned = sem("o1_turned")
        o1T_set = sem("o1T_set")
        pr_mm = sem("pr_mm")
        pr_added = sem("pr_added")
        v_route = sem("v_route")
        route_set = sem("route_set")
        r_exp = sem("r_exp")
        r_ready1 = sem("r_ready1")
        r_staged = sem("r_staged")
        r_turned = sem("r_turned")
        rT_set = sem("rT_set")
        rb_mm = sem("rb_mm")
        rb_added = sem("rb_added")
        h_mm = sem("h_mm")
        h_silu = sem("h_silu")
        e_mm = sem("e_mm")
        e_added = sem("e_added")
        out_stored = sem("out_stored")
        v_moe = sem("v_moe")

        block = ctx.enter_context(nc.Block())

        def end_phase(eng, n):
            eng.drain().then_inc(phase, 1)
            eng.wait_ge(phase, 5 * n)

        def tile(buf, i):
            return buf[:, ds(i, 1), :].rearrange("p a d -> p (a d)")

        def layernorm(dve, c, src, dst, layer):
            tot, mean, rstd = stats[:, 0, :], stats[:, 1, :], stats[:, 2, :]
            c.link(dve.tensor_reduce(tot, src[:, :, :], AX, ALU.add))
            c.link(dve.tensor_scalar(mean, tot, 1.0 / D, None, ALU.mult))
            c.link(dve.tensor_tensor(dst[:, :, :], src[:, :, :], mean.unsqueeze(2).to_broadcast([P, T, D]), ALU.subtract))
            sq = xnT[:, :].rearrange("p (t d) -> p t d", d=D)
            c.link(dve.tensor_tensor(sq, dst[:, :, :], dst[:, :, :], ALU.mult))
            c.link(dve.tensor_reduce(tot, sq, AX, ALU.add))
            dve.tensor_scalar(mean, tot, 1.0 / D, LN_EPS, ALU.mult, ALU.add).then_inc(var_done, 1)
            dve.wait_ge(std_done, layer + 1)
            c.link(dve.reciprocal(rstd, tot))
            c.link(dve.tensor_tensor(dst[:, :, :], dst[:, :, :], rstd.unsqueeze(2).to_broadcast([P, T, D]), ALU.mult))

        def quantize(dve, c, src, n, a_, acc, sgn, sc, dst, sign_ready):
            def blocks(x):
                return x.rearrange("p (n k) -> p n k", k=BLOCK)
            scale, inv = sc[:, 0, 0:n], sc[:, 1, 0:n]
            c.link(dve.tensor_reduce(scale, blocks(src), AX, ALU.max, apply_absolute_value=True))
            c.link(dve.tensor_scalar(scale, scale, 1.0 / 6.0, 1e-12, ALU.mult, ALU.max))
            c.link(dve.reciprocal(inv, scale))
            sign_ready()
            c.link(dve.tensor_tensor(blocks(a_), blocks(a_), inv.unsqueeze(2).to_broadcast([P, n, BLOCK]), ALU.mult))
            c.link(dve.tensor_scalar(acc, a_, 5.0, 2.0, ALU.is_gt, ALU.mult))
            for mid in (3.5, 2.5):
                c.link(dve.scalar_tensor_tensor(out=acc, in0=a_, scalar=mid, in1=acc, op0=ALU.is_gt, op1=ALU.add))
            c.link(dve.tensor_scalar(acc, acc, 2.0, None, ALU.mult))
            for mid in (1.75, 1.25, 0.75, 0.25):
                c.link(dve.scalar_tensor_tensor(out=acc, in0=a_, scalar=mid, in1=acc, op0=ALU.is_gt, op1=ALU.add))
            c.link(dve.scalar_tensor_tensor(out=acc, in0=acc, scalar=0.5, in1=sgn, op0=ALU.mult, op1=ALU.mult))
            return dve.tensor_tensor(blocks(dst), blocks(acc), scale.unsqueeze(2).to_broadcast([P, n, BLOCK]), ALU.mult)

        @block.sync
        def _(sp):
            xv = a["x"].rearrange("(t p) d -> p t d", p=P)
            for c in range(4):
                sp.dma_start(res[:, 8 * c:8 * c + 8, :], xv[:, 8 * c:8 * c + 8, :]).then_inc(ld, 16)
            sp.wait_ge(const_set, 1)
            for m, w in enumerate(("w_gate", "w_up")):
                for c in range(3):
                    rows = min(P, INNER - P * c)
                    sp.dma_start(wraw[0:rows, (3 * m + c) * P:(3 * m + c + 1) * P],
                                 a[w][P * c:P * c + rows, :]).then_inc(ld1, 16)
            sp.dma_start(wraw[:, 6 * P:NW], a["w_down"]).then_inc(ld1, 16)
            if stop == 1:
                sp.wait_ge(ffn_added, T)
                sp.dma_start(out.rearrange("(t p) d -> p t d", p=P), res[:, :, :]).then_inc(ld, 16)
                sp.wait_ge(ld, 80)
                return
            end_phase(sp, 1)
            for n, w in enumerate(("Wq", "Wk", "Wv", "Wg")):
                sp.dma_start(wproj[:, HD * n:HD * n + HD], a[w]).then_inc(ld2, 16)
            sp.dma_start(bproj[:, :], a["bproj"]).then_inc(ld2, 16)
            sp.dma_start(wgate[:, :], a["wgate"]).then_inc(ld2, 16)
            sp.dma_start(bgate[:, 0:2], a["bgate"]).then_inc(ld2, 16)
            ps_v = proj_s.rearrange("(t p) n -> t p n", p=P)
            with sp.Fori(0, T) as i:
                sp.wait_ge(p_normed, i + 1)
                sp.wait_ge(p_silu, 8 * i + 8)
                sp.dma_start(ps_v[ds(i, 1), :, :].rearrange("a p n -> (a p) n"), prj[:, :]).then_inc(p_stored, 16)
            sp.wait_ge(g_done, 8)
            sp.dma_start(gates_s, gates[:, :]).then_inc(g_stored, 16)
            sp.wait_ge(g_stored, 16)
            sp.wait_ge(p_stored, 16 * T)
            end_phase(sp, 2)
            sp.dma_start(rf_col[:, :], a["rf"].partition_broadcast(P)).then_inc(ld3, 16)
            for j in range(2):
                for b in range(B):
                    p0 = j * B * H0 + b * H0
                    for buf, kind in ((gbeta, 0), (gdec, 1 + j), (gout, 3 + j)):
                        sp.dma_start(buf[p0:p0 + H0, :], gates_s[kind * H0:kind * H0 + H0, b * L:b * L + L]).then_inc(ld3, 16)
            pv = proj_s.rearrange("(b t) (w h d) -> w b h t d", b=B, w=4, h=H0)
            mv = mem_s.rearrange("j (b t) (h d) -> j b h t d", b=B, h=H0)
            with sp.Fori(0, L // (2 * STEPS)) as i:
                for n in range(2):
                    sp.wait_ge(stepped[n], i)
                    for w in range(3):
                        for j in range(2):
                            for b in range(B):
                                p0 = j * B * H0 + b * H0
                                sp.dma_start(qkv[p0:p0 + H0, n, w, :, :], pv[w, b, :, ds(i * (2 * STEPS) + n * STEPS, STEPS), :])\
                                    .then_inc(qkv_in[n], 16)
            end_phase(sp, 3)
            for c in range(8):
                sp.dma_start(wout[:, c, :], a["Wo"][P * c:P * c + P, :]).then_inc(ld4, 16)
            sp.dma_start(bout[:, :], a["bo"]).then_inc(ld4, 16)
            sp.dma_start(onw[:, :], a["onorm_w"].partition_broadcast(P)).then_inc(ld4, 16)
            mt = mem_s.rearrange("j (t p) n -> t p j n", p=P)
            with sp.Fori(0, T) as i:
                sp.wait_ge(og_set, i)
                sp.dma_start(om[:, 0:2, :], mt[ds(i, 1), :, :, :].rearrange("a p j n -> (a p) j n")).then_inc(om_in, 16)
                sp.dma_start(om[:, 2, :], ps_v[ds(i, 1), :, 3 * HD:4 * HD].rearrange("a p n -> (a p) n")).then_inc(om_in, 16)
            if stop == 2:
                sp.wait_ge(o_added, T)
                sp.dma_start(out.rearrange("(t p) d -> p t d", p=P), res[:, :, :]).then_inc(ld, 16)
                sp.wait_ge(ld, 80)
                return
            end_phase(sp, 4)
            sp.dma_start(wq1[:, :, :], a["W1q"]).then_inc(ld5, 16)
            sp.dma_start(wk1[:, :, :], a["W1k"]).then_inc(ld5, 16)
            sp.dma_start(wv1[:, :], a["W1v"]).then_inc(ld5, 16)
            sp.dma_start(wg1[:, :], a["Wg1"]).then_inc(ld5, 16)
            sp.dma_start(bg1[:, :], a["bg1"].partition_broadcast(P)).then_inc(ld5, 16)
            end_phase(sp, 5)
            sp.dma_start(wp1[:, :], a["W1p"]).then_inc(ld6, 16)
            sp.dma_start(bp1[:, :], a["bp1"]).then_inc(ld6, 16)
            sp.dma_start(w1[:, :, :], a["W1"].rearrange("e p n -> p e n")).then_inc(ld6, 16)
            for e in range(E1):
                sp.dma_start(w2[:, e, :, :], a["W2"][e].rearrange("(c p) d -> p c d", p=P)).then_inc(ld6, 16)
            sp.dma_start(b1[:, :, :], a["b1"]).then_inc(ld6, 16)
            sp.dma_start(b2[:, :], a["b2"]).then_inc(ld6, 16)
            ov = out.rearrange("(t p) d -> p t d", p=P)
            with sp.Fori(0, T // 4) as i:
                sp.wait_ge(e_added, (i + 1) * (4 * E1))
                sp.dma_start(ov[:, ds(4 * i, 4), :], res[:, ds(4 * i, 4), :]).then_inc(out_stored, 16)
            sp.wait_ge(out_stored, 16 * (T // 4))

        @block.gpsimd
        def _(pool):
            pool.memset(wraw[:, :], 0.0).then_inc(const_set, 1)
            pool.memset(ident[:, :], 0.0).then_inc(const_set, 1)
            pool.memset(ones_row[:, :], 1.0).then_inc(const_set, 1)
            pool.wait_ge(const_set, 3)
            pool.affine_select(out=ident[:, :], in_=ident[:, :], compare_op=ALU.not_equal, fill=1.0, base=0,
                               pattern=[[-1, P]], channel_multiplier=1).then_inc(const_set, 1)
            pool.wait_ge(xq_done, 1)
            with pool.Fori(0, T) as i:
                pool.wait_ge(x_turned, i)
                pool.tensor_copy(st_n[:, :], tile(xn, i)).then_inc(staged, 1)
                pool.tensor_copy(st_q[:, :], tile(xq, i)).then_inc(staged, 1)
            if stop == 1:
                return
            end_phase(pool, 1)
            with pool.Fori(0, T) as i:
                pool.wait_ge(p_mm, 8 * i)
                pool.tensor_copy(st_p[:, :], xnT[:, ds(i * P, P)]).then_inc(p_staged, 1)
            end_phase(pool, 2)
            pool.memset(mix[:, :], 0.0).then_inc(swap_set, 1)
            for n, off in enumerate((64, -64)):
                pool.wait_ge(swap_set, n + 1)
                pool.affine_select(out=mix[:, :], in_=mix[:, :], compare_op=ALU.not_equal, fill=1.0, base=off,
                                   pattern=[[-1, P]], channel_multiplier=1).then_inc(swap_set, 1)
            mv = mem_s.rearrange("j (b t) (h d) -> j b h t d", b=B, h=H0)
            with pool.Fori(0, L // (2 * STEPS)) as i:
                for n in range(2):
                    pool.wait_ge(stepped[n], i + 1)
                    for j in range(2):
                        for b in range(B):
                            p0 = j * B * H0 + b * H0
                            pool.dma_start(mv[j, b, :, ds(i * (2 * STEPS) + n * STEPS, STEPS), :], obuf[p0:p0 + H0, n, :, :])\
                                .then_inc(o_stored[n], 16)
            for n in range(2):
                pool.wait_ge(o_stored[n], L // (2 * STEPS) * 128)
            end_phase(pool, 3)
            if stop == 2:
                return
            end_phase(pool, 4)
            pool.iota(number_i[:, :], pattern=[[1, E1]], base=0, channel_multiplier=0).then_inc(mask_set, 1)
            for m in (above, below):
                pool.memset(m[:, :], 0.0).then_inc(mask_set, 1)
            pool.memset(vaug[:, :, :, :], 1.0).then_inc(mask_set, 1)
            pool.memset(mxz[:, :, :], 0.0).then_inc(mask_set, 1)
            pool.wait_ge(mask_set, 5)
            for m, (cm, step) in ((above, (1, -1)), (below, (-1, 1))):
                pool.affine_select(out=m[:, :], in_=m[:, :], compare_op=ALU.is_ge, fill=MASKED, base=0,
                                   pattern=[[step, P]], channel_multiplier=cm).then_inc(mask_set, 1)
            pool.wait_ge(norm_done, 2)
            with pool.Fori(0, T) as i:
                pool.wait_ge(x1_turned, i)
                pool.tensor_copy(st_x[:, :], tile(xn, i)).then_inc(x1_staged, 1)
            with pool.Fori(0, B) as b:
                with pool.Fori(0, 4) as r:
                    pool.wait_ge(pj_mm, b * 4 + r)
                    pool.tensor_copy(st_wq[:, :], tile(wq1, r)).then_inc(w_staged, 1)
                    pool.tensor_copy(st_wk[:, :], tile(wk1, r)).then_inc(w_staged, 1)
            end_phase(pool, 5)
            with pool.Fori(0, T) as i:
                pool.wait_ge(o1_turned, i)
                pool.tensor_copy(st_o[:, :], tile(o_all, i)).then_inc(o_staged, 1)
            with pool.Fori(0, T // 4) as i:
                pool.wait_ge(e_added, i * (4 * E1))
                pool.tensor_copy(st_r[:, :], route[:, ds(4 * i, 4), :].rearrange("p t e -> p (t e)")).then_inc(r_staged, 1)

        @block.tensor
        def _(pe):
            pe.wait_ge(const_set, 4)
            pe.wait_ge(wq_done, 1)
            for n in range(6):
                pe.transpose(bank[n // 3][:, P * (n % 3):P * (n % 3 + 1)], wqt[:, P * n:P * (n + 1)], ident[:, :])
            for c in range(3):
                w = min(P, INNER - P * c)
                last = pe.transpose(bank[2][0:w, P * c:P * (c + 1)], wqt[:, 6 * P + P * c:6 * P + P * c + w], ident[:, :])
            last.then_inc(wt_done, 1)
            pe.wait_ge(wT_done, 3)
            with pe.Fori(0, T) as i:
                pe.wait_ge(staged, 2 * i + 2)
                pe.transpose(bank[0][:, 0:P], st_n[:, :], ident[:, :])
                pe.transpose(bank[0][:, P:2 * P], st_q[:, :], ident[:, :]).then_inc(x_turned, 1)
                pe.wait_ge(xT_done, 2 * i + 2)
                pe.wait_ge(hid_done, i)
                pe.matmul(bank[1][:, 0:INNER], xqT[:, :], wguT[:, 0, 0:INNER], start=True, stop=True)
                pe.matmul(bank[2][:, 0:INNER], xqT[:, :], wguT[:, 1, 0:INNER], start=True, stop=True).then_inc(gu_done, 1)
                pe.wait_ge(hq_done, i + 1)
                for c in range(3):
                    w = min(P, INNER - P * c)
                    last = pe.transpose(bank[3][0:w, P * c:P * (c + 1)], hq[:, P * c:P * c + w], ident[:, :])
                last.then_inc(h_turned, 1)
                pe.wait_ge(hT_done, 2 * i + 2)
                pe.wait_ge(ffn_added, i)
                for c in range(3):
                    w = min(P, INNER - P * c)
                    last = pe.matmul(bank[4][:, 0:D], hqT[0:w, c, :], wdT[0:w, c, :], start=(c == 0), stop=(c == 2))
                last.then_inc(down_done, 1)
            if stop == 1:
                return
            end_phase(pe, 1)
            pe.wait_ge(ld2, 112)
            with pe.Fori(0, T) as i:
                pe.wait_ge(p_staged, i + 1)
                pe.wait_ge(p_silu, 8 * i)
                for n in range(8):
                    pe.matmul(bank[n], st_p[:, :], wproj[:, 512 * n:512 * n + 512], start=True, stop=False)
                    pe.matmul(bank[n], ones_row[:, :], bproj[:, 512 * n:512 * n + 512], start=False, stop=True).then_inc(p_mm, 1)
            pe.wait_ge(p_silu, 8 * T)
            for n in range(8):
                pe.matmul(bank[n][0:5 * H0, :], wgate[:, :], xnT[:, 512 * n:512 * n + 512], start=True, stop=True).then_inc(g_mm, 1)
            end_phase(pe, 2)
            pe.wait_ge(r_ready, 1)
            with pe.Fori(0, L // (2 * STEPS)) as i:
                for s in range(2 * STEPS):
                    pe.wait_ge(updated, 2 * STEPS * i + s + 1)
                    for n in range(8):
                        last = pe.matmul(bank[n], mix[:, :], Snew[:, 512 * n:512 * n + 512], start=True, stop=True)
                    last.then_inc(mixed, 1)
            end_phase(pe, 3)
            pe.wait_ge(ld4, 160)
            with pe.Fori(0, T) as i:
                pe.wait_ge(og_set, i + 1)
                for c in range(8):
                    last = pe.transpose(bank[c // 4][:, P * (c % 4):P * (c % 4) + P], og[:, P * c:P * c + P], ident[:, :])
                last.then_inc(og_turned, 1)
                pe.wait_ge(ogT_set, 2 * i + 2)
                pe.wait_ge(o_added, i)
                for c in range(8):
                    pe.matmul(bank[2][:, 0:D], ogT[:, c, :], wout[:, c, :], start=(c == 0), stop=False)
                pe.matmul(bank[2][:, 0:D], ones_row[:, :], bout[:, :], start=False, stop=True).then_inc(o_mm, 1)
            if stop == 2:
                return
            end_phase(pe, 4)
            pe.wait_ge(ld5, 80)
            with pe.Fori(0, T) as i:
                pe.wait_ge(x1_staged, i + 1)
                pe.wait_ge(x1T_set, 2 * i)
                pe.transpose(bank[0][:, 0:P], st_x[:, :], ident[:, :]).then_inc(x1_turned, 1)
                pe.wait_ge(x1T_set, 2 * i + 2)
                pe.wait_ge(v_set, 2 * i)
                pe.matmul(bank[1][:, 0:D], xt_x[:, :], wv1[:, :], start=True, stop=True)
                pe.matmul(bank[2][:, 0:E1], xt_x[:, :], wg1[:, :], start=True, stop=True).then_inc(v_mm, 1)
            pe.wait_ge(c_set, 2)
            pe.wait_ge(v_set, 2 * T)
            with pe.Fori(0, B) as b:
                with pe.Fori(0, 4) as r:
                    i = b * 4 + r
                    pe.wait_ge(w_staged, 2 * i + 2)
                    pe.wait_ge(o_norm, 4 * i)
                    for n in range(2):
                        pe.matmul(bank[4 + n], st_wq[:, :], xnT[:, ds(b * L + 512 * n, 512)], start=True, stop=True)
                    for n in range(2):
                        last = pe.matmul(bank[6 + n], st_wk[:, :], xnT[:, ds(b * L + 512 * n, 512)], start=True, stop=True)
                    last.then_inc(pj_mm, 1)
                    pe.wait_ge(qk_set, 2 * i + 2)
                    pe.wait_ge(exp_done, 32 * i)
                    for u in range(32):
                        g, t = u // TB, u % TB
                        rows = slice(32 * g, 32 * g + 32)
                        if u >= 2:
                            pe.wait_ge(mx_read, 32 * i + u - 1)
                        for n in range((t + 4) // 4):
                            w = min(512, (t + 1) * P - 512 * n)
                            pe.matmul(bank[2 * (u % 2) + n][:, 0:w], qpad[rows, t * P:t * P + P], kaug[rows, 512 * n:512 * n + w],
                                      start=True, stop=(n != t // 4))
                        pe.matmul(bank[2 * (u % 2) + t // 4][:, P * (t % 4):P * (t % 4) + P], ident_b[:, :], above[:, :],
                                  start=False, stop=True).then_inc(a_mm, 1)
                    pe.wait_ge(mx_read, 32 * i + 32)
                    for t in range(TB):
                        last = pe.matmul(bank[4 + t // 4][:, P * (t % 4):P * (t % 4) + P], mxz[:, t, :], ident[:, :], start=True, stop=True)
                    last.then_inc(mx_turned, 1)
                    pe.wait_ge(qaug_set, i + 1)

                    def values(g):
                        pe.wait_ge(exp_done, 32 * i + 8 * g + 8)
                        if g >= 2:
                            pe.wait_ge(o_norm, 4 * i + g - 1)
                        for t in range(TB):
                            for j in range(t + 1):
                                at = sum(TB - x for x in range(j)) * P + (t - j) * P
                                last = pe.matmul(bank[6 + g % 2][:, SLOT * t:SLOT * t + SLOT], probs[:, g % 2, at:at + P],
                                                 vaug[:, ds(b * TB + j, 1), ds(r * 4 + g, 1), :].rearrange("p a h d -> p (a h d)"),
                                                 start=(j == 0), stop=(j == t))
                        last.then_inc(c_mm, 1)

                    for g in range(4):
                        rows = slice(32 * g, 32 * g + 32)
                        for j in range(TB):
                            u = 8 * g + j
                            if u >= 2:
                                pe.wait_ge(exp_done, 32 * i + u - 1)
                            wide = L - P * j
                            for n in range((wide + 511) // 512):
                                w = min(512, wide - 512 * n)
                                last = pe.matmul(bank[2 * (u % 2) + n][:, 0:w], kaug[rows, P * j:P * j + P],
                                                 qaug[rows, P * j + 512 * n:P * j + 512 * n + w], start=True, stop=(n > 0))
                                if n == 0:
                                    last = pe.matmul(bank[2 * (u % 2)][:, 0:P], ident_b[:, :], below[:, :], start=False, stop=True)
                            last.then_inc(b_mm, 1)
                        if g:
                            values(g - 1)
                    values(3)
            end_phase(pe, 5)
            pe.wait_ge(ld6, 16 * 13)
            with pe.Fori(0, T) as i:
                pe.wait_ge(o_staged, i + 1)
                pe.wait_ge(o1T_set, i)
                pe.transpose(bank[0][:, 0:P], st_o[:, :], ident[:, :]).then_inc(o1_turned, 1)
                pe.wait_ge(o1T_set, i + 1)
                pe.wait_ge(pr_added, i)
                pe.matmul(bank[1][:, 0:D], oT1[:, :], wp1[:, :], start=True, stop=False)
                pe.matmul(bank[1][:, 0:D], ones_row[:, :], bp1[:, :], start=False, stop=True).then_inc(pr_mm, 1)
            pe.wait_ge(pr_added, T)
            with pe.Fori(0, T // 4) as i:
                pe.wait_ge(r_staged, i + 1)
                for t in range(4):
                    last = pe.transpose(bank[6][0:E1, P * t:P * t + P], st_r[:, E1 * t:E1 * t + E1], ident[:, :])
                last.then_inc(r_turned, 1)
                pe.wait_ge(rT_set, i + 1)
                for t in range(4):
                    last = pe.matmul(bank[7][:, P * t:P * t + P], rT[:, P * t:P * t + P], b2[:, :], start=True, stop=True)
                last.then_inc(rb_mm, 1)

                def second(e):
                    pe.wait_ge(h_silu, 4 * E1 * i + 4 * e + 4)
                    if e >= 2:
                        pe.wait_ge(e_added, 4 * E1 * i + 4 * (e - 1))
                    for t in range(4):
                        for c in range(4):
                            last = pe.matmul(bank[4 + e % 2][:, P * t:P * t + P], hT1[:, e % 2, c, P * t:P * t + P], w2[:, e, c, :],
                                             start=(c == 0), stop=(c == 3))
                    last.then_inc(e_mm, 1)

                for e in range(E1):
                    for c in range(4):
                        if e or c:
                            pe.wait_ge(h_silu, 4 * E1 * i + max(4 * e + c - 3, 0))
                        pe.matmul(bank[c], w1[:, e, P * c:P * c + P], xnT[:, ds(i * 512, 512)], start=True, stop=True).then_inc(h_mm, 1)
                    if e:
                        second(e - 1)
                second(E1 - 1)

        @block.scalar
        def _(act):
            act.wait_ge(var_done, 1)
            act.activation(stats[:, 0, :], stats[:, 1, :], ACT.Sqrt).then_inc(std_done, 1)
            act.wait_ge(norm_done, 1)
            act.activation(fa[:, :], xn[:, :, :].rearrange("p t d -> p (t d)"), ACT.Abs).then_inc(sign_done, 1)
            act.activation(fsg[:, :], xn[:, :, :].rearrange("p t d -> p (t d)"), ACT.Sign).then_inc(sign_done, 1)
            act.wait_ge(wt_done, 1)
            act.wait_ge(ld1, 112)
            for m in range(2):
                act.copy(wguT[:, m, :], bank[m][:, 0:3 * P]).then_inc(wT_done, 1)
            act.copy(wdT[:, 0:2, :], bank[2][:, 0:2 * P].rearrange("p (c d) -> p c d", c=2))
            act.copy(wdT[0:INNER - 2 * P, 2, :], bank[2][0:INNER - 2 * P, 2 * P:3 * P]).then_inc(wT_done, 1)
            with act.Fori(0, T) as i:
                act.wait_ge(x_turned, i + 1)
                act.copy(xnT[:, ds(i * P, P)], bank[0][:, 0:P]).then_inc(xT_done, 1)
                act.wait_ge(gu_done, i)
                act.copy(xqT[:, :], bank[0][:, P:2 * P]).then_inc(xT_done, 1)
                act.wait_ge(gu_done, i + 1)
                act.activation(silu_g[:, :], bank[1][:, 0:INNER], ACT.Silu).then_inc(silu_done, 1)
                act.wait_ge(hid_done, i + 1)
                act.activation(fa[:, 0:INNER], hid[:, :], ACT.Abs).then_inc(hsign_done, 1)
                act.activation(fsg[:, 0:INNER], hid[:, :], ACT.Sign).then_inc(hsign_done, 1)
                act.wait_ge(h_turned, i + 1)
                act.copy(hqT[:, 0:2, :], bank[3][:, 0:2 * P].rearrange("p (c d) -> p c d", c=2)).then_inc(hT_done, 1)
                act.copy(hqT[0:INNER - 2 * P, 2, :], bank[3][0:INNER - 2 * P, 2 * P:3 * P]).then_inc(hT_done, 1)
            if stop == 1:
                return
            end_phase(act, 1)
            with act.Fori(0, T) as i:
                act.wait_ge(p_stored, 16 * i)
                for n in range(8):
                    act.wait_ge(p_mm, 8 * i + n + 1)
                    act.activation(prj[:, 512 * n:512 * n + 512], bank[n], ACT.Silu).then_inc(p_silu, 1)
                act.wait_ge(p_var, i + 1)
                act.activation(prj_n[:, 1, :], prj_n[:, 0, :], ACT.Sqrt).then_inc(p_std, 1)
            act.wait_ge(g_bias, 1)
            for n in range(8):
                act.wait_ge(g_mm, n + 1)
                act.activation(gates[:, 512 * n:512 * n + 512], bank[n][0:5 * H0, :], ACT.Sigmoid, bias=bgate[:, 2:3]).then_inc(g_done, 1)
            end_phase(act, 2)
            with act.Fori(0, L // (2 * STEPS)) as i:
                for s in range(2 * STEPS):
                    at = 2 * STEPS * i + s + 1
                    act.wait_ge(mixed, at)
                    act.activation(junk[:, :], banks[:, :], ACT.Square, accum_out=cap[:, 0:1]).then_inc(squared, 1)
                    act.wait_ge(ratio_set, at)
                    act.activation(cap[:, 2:3], cap[:, 1:2], ACT.Sqrt).then_inc(ratio_root, 1)
                    act.wait_ge(lam_set, at)
                    act.activation(S[:, :, :].rearrange("p k v -> p (k v)"), banks[:, :], ACT.Copy, scale=cap[:, 5:6]).then_inc(state_set, 1)
            end_phase(act, 3)
            with act.Fori(0, T) as i:
                act.wait_ge(o_var, i + 1)
                act.activation(orn[:, :], orn[:, :], ACT.Sqrt).then_inc(o_std, 1)
                act.wait_ge(og_turned, i + 1)
                for n in range(2):
                    act.copy(ogT[:, 4 * n:4 * n + 4, :].rearrange("p c d -> p (c d)"), bank[n]).then_inc(ogT_set, 1)
            if stop == 2:
                return
            end_phase(act, 4)
            act.wait_ge(var_done, 2)
            act.activation(stats[:, 0, :], stats[:, 1, :], ACT.Sqrt).then_inc(std_done, 1)
            act.wait_ge(norm_done, 2)
            act.activation(route[:, 0:1, :], stats[:, 0:1, 0:E1], ACT.Exp)
            with act.Fori(0, T) as i:
                act.wait_ge(x1_turned, i + 1)
                act.copy(xnT[:, ds(i * P, P)], bank[0][:, 0:P]).then_inc(x1T_set, 1)
                act.wait_ge(v_mm, i)
                act.copy(xt_x[:, :], bank[0][:, 0:P]).then_inc(x1T_set, 1)
            act.wait_ge(r_ready1, 1)
            act.activation(rt[:, 1, :, :], rt[:, 0, :, :], ACT.Exp).then_inc(r_exp, 1)
            with act.Fori(0, B) as b:
                with act.Fori(0, 4) as r:
                    i = b * 4 + r
                    for u in range(32):
                        g, j = u // TB, u % TB
                        if j == 0:
                            act.wait_ge(c_mm, 4 * i + max(g - 1, 0))
                        act.wait_ge(b_mm, 32 * i + u + 1)
                        at, w = sum(TB - x for x in range(j)) * P, L - P * j
                        act.activation(probs[:, g % 2, at:at + w], banks[:, 1024 * (u % 2):1024 * (u % 2) + w], ACT.Exp,
                                       scale=D1 ** -0.5).then_inc(exp_done, 1)
            end_phase(act, 5)
            with act.Fori(0, T) as i:
                act.wait_ge(o1_turned, i + 1)
                act.wait_ge(pr_mm, i)
                act.copy(oT1[:, :], bank[0][:, 0:P]).then_inc(o1T_set, 1)
            act.wait_ge(ld6, 16 * 13)
            with act.Fori(0, T // 4) as i:
                act.wait_ge(r_turned, i + 1)
                act.copy(rT[:, :], bank[6][0:E1, :]).then_inc(rT_set, 1)
                for e in range(E1):
                    act.wait_ge(e_mm, i * E1 + max(e - 1, 0))
                    for c in range(4):
                        act.wait_ge(h_mm, 4 * E1 * i + 4 * e + c + 1)
                        act.activation(hT1[:, e % 2, c, :], bank[c], ACT.Silu, bias=b1[:, e, c:c + 1]).then_inc(h_silu, 1)

        @block.vector
        def _(dve):
            seq = Count(dve, v_seq)
            dve.wait_ge(ld, 64)
            layernorm(dve, seq, res, xn, 0)
            dve.tensor_copy(stats[:, 3, 0:1], stats[:, 2, 0:1]).then_inc(norm_done, 1)
            xf = xn[:, :, :].rearrange("p t d -> p (t d)")
            quantize(dve, seq, xf, T * D // BLOCK, fa[:, :], fc[:, :], fsg[:, :], fsc,
                     xq[:, :, :].rearrange("p t d -> p (t d)"),
                     lambda: dve.wait_ge(sign_done, 2)).then_inc(xq_done, 1)
            dve.wait_ge(ld1, 112)
            dve.wait_ge(xq_done, 1)
            wneg = fa[:, NW:2 * NW]
            seq.link(dve.tensor_scalar(wneg, wraw[:, :], 0.0, None, ALU.is_lt))
            seq.link(dve.scalar_tensor_tensor(out=fsg[:, 0:NW], in0=wraw[:, :], scalar=0.0, in1=wneg,
                                              op0=ALU.is_gt, op1=ALU.subtract))
            seq.link(dve.tensor_tensor(fa[:, 0:NW], wraw[:, :], fsg[:, 0:NW], ALU.mult))
            quantize(dve, seq, wraw[:, :], NW // BLOCK, fa[:, 0:NW], fc[:, 0:NW], fsg[:, 0:NW], fsc,
                     wqt[:, :], lambda: None).then_inc(wq_done, 1)
            dve.wait_ge(wq_done, 1)
            ffn = Count(dve, v_ffn, per=13)
            with dve.Fori(0, T) as i:
                ffn.start(i)
                dve.wait_ge(silu_done, i + 1)
                dve.tensor_tensor(hid[:, :], silu_g[:, :], bank[2][:, 0:INNER], ALU.mult).then_inc(hid_done, 1)
                dve.wait_ge(hid_done, i + 1)
                dve.wait_ge(h_turned, i)
                quantize(dve, ffn, hid[:, :], INNER // BLOCK, fa[:, 0:INNER], fc[:, 0:INNER], fsg[:, 0:INNER],
                         fsc, hq[:, :], lambda: dve.wait_ge(hsign_done, 2 * i + 2)).then_inc(hq_done, 1)
                ffn.end()
                dve.wait_ge(down_done, i + 1)
                dve.tensor_tensor(tile(res, i), tile(res, i), bank[4][:, 0:D], ALU.add).then_inc(ffn_added, 1)
            if stop == 1:
                return
            end_phase(dve, 1)
            dve.wait_ge(ld2, 112)
            dve.tensor_tensor(bgate[:, 2:3], bgate[:, 0:1], bgate[:, 1:2], ALU.add).then_inc(g_bias, 1)
            prc = Count(dve, v_prj, per=3)
            with dve.Fori(0, T) as i:
                prc.start(i)
                dve.wait_ge(p_silu, 8 * i + 4)
                qk = prj[:, 0:2 * HD].rearrange("p (h d) -> p h d", d=DK)
                qk_sq = prj_sq[:, :].rearrange("p (h d) -> p h d", d=DK)
                prc.link(dve.tensor_tensor(qk_sq, qk, qk, ALU.mult))
                prc.link(dve.tensor_reduce(prj_n[:, 0, :], qk_sq, AX, ALU.add))
                dve.tensor_scalar(prj_n[:, 0, :], prj_n[:, 0, :], 1e-6, None, ALU.add).then_inc(p_var, 1)
                dve.wait_ge(p_std, i + 1)
                prc.link(dve.reciprocal(prj_n[:, 0, :], prj_n[:, 1, :]))
                prc.end()
                dve.tensor_tensor(qk, qk, prj_n[:, 0, :].unsqueeze(2).to_broadcast([P, 2 * H0, DK]), ALU.mult).then_inc(p_normed, 1)
            end_phase(dve, 2)
            pre = Count(dve, v_pre)
            dve.wait_ge(ld3, 16 * 25)
            dve.wait_ge(swap_set, 3)
            pre.link(dve.scalar_tensor_tensor(out=mix[:, :], in0=mix[:, :], scalar=rf_col[:, 0:1], in1=ident[:, :], op0=ALU.mult, op1=ALU.add))
            pre.link(dve.memset(S[:, :, :], 0.0))
            dve.tensor_scalar(gndec[:, :], gdec[:, :], -1.0, None, ALU.mult).then_inc(r_ready, 1)
            dve.wait_ge(r_ready, 1)
            PER = 4 + 2 * STEPS * 10
            rec = Count(dve, v_rec, per=PER)
            with dve.Fori(0, L // (2 * STEPS)) as i:
                rec.start(i)
                for n, g in enumerate((gbeta, gdec, gndec, gout)):
                    rec.link(dve.tensor_copy(gcur[:, n, :], g[:, ds(i * (2 * STEPS), 2 * STEPS)]))
                for s in range(2 * STEPS):
                    n, k = s // STEPS, s % STEPS
                    at = 2 * STEPS * i + s + 1
                    q_, k_, v_ = (qkv[:, n, w, k, :] for w in range(3))
                    if k == 0:
                        dve.wait_ge(qkv_in[n], 16 * 24 * (i + 1))
                        dve.wait_ge(o_stored[n], 128 * i)
                    if s:
                        dve.wait_ge(state_set, at - 1)
                    rec.link(dve.tensor_tensor(prod[:, :, :], S[:, :, :], k_.unsqueeze(2).to_broadcast([P, DK, DK]), ALU.mult))
                    rec.link(dve.tensor_reduce(small[:, 0, :], prod[:, :, :].rearrange("p k v -> p v k"), AX, ALU.add))
                    rec.link(dve.scalar_tensor_tensor(out=small[:, 1, :], in0=small[:, 0, :], scalar=gcur[:, 2, s:s + 1], in1=v_, op0=ALU.mult, op1=ALU.add))
                    rec.link(dve.tensor_scalar(small[:, 2, :], small[:, 1, :], gcur[:, 0, s:s + 1], None, ALU.mult))
                    rec.link(dve.tensor_tensor(outer[:, :, :], k_.unsqueeze(2).to_broadcast([P, DK, DK]),
                                               small[:, 2, :].unsqueeze(1).to_broadcast([P, DK, DK]), ALU.mult))
                    dve.scalar_tensor_tensor(out=Snew[:, :], in0=S[:, :, :].rearrange("p k v -> p (k v)"), scalar=gcur[:, 1, s:s + 1],
                                             in1=outer[:, :, :].rearrange("p k v -> p (k v)"), op0=ALU.mult, op1=ALU.add).then_inc(updated, 1)
                    dve.wait_ge(squared, at)
                    dve.tensor_scalar(cap[:, 1:2], cap[:, 0:1], 1.0 / (DK * DK), 1.0, ALU.mult, ALU.max).then_inc(ratio_set, 1)
                    rec.link(dve.tensor_scalar(cap[:, 3:4], cap[:, 0:1], float(DK * DK), None, ALU.is_gt))
                    dve.wait_ge(ratio_root, at)
                    rec.link(dve.reciprocal(cap[:, 4:5], cap[:, 2:3]))
                    rec.link(dve.scalar_tensor_tensor(out=cap[:, 4:5], in0=cap[:, 4:5], scalar=-1.0, in1=cap[:, 3:4], op0=ALU.add, op1=ALU.mult))
                    dve.tensor_scalar(cap[:, 5:6], cap[:, 4:5], 1.0, None, ALU.add).then_inc(lam_set, 1)
                    dve.wait_ge(state_set, at)
                    rec.link(dve.tensor_tensor(prod[:, :, :], S[:, :, :], q_.unsqueeze(2).to_broadcast([P, DK, DK]), ALU.mult))
                    rec.link(dve.tensor_reduce(small[:, 0, :], prod[:, :, :].rearrange("p k v -> p v k"), AX, ALU.add))
                    last = dve.tensor_scalar(obuf[:, n, k, :], small[:, 0, :], gcur[:, 3, s:s + 1], None, ALU.mult)
                    if k == STEPS - 1:
                        last.then_inc(stepped[n], 1)
                rec.end()
            end_phase(dve, 3)
            oc = Count(dve, v_out, per=6)
            dve.wait_ge(ld4, 160)
            with dve.Fori(0, T) as i:
                oc.start(i)
                dve.wait_ge(om_in, 32 * (i + 1))
                oc.link(dve.tensor_tensor(om[:, 0, :], om[:, 0, :], om[:, 1, :], ALU.add))
                o_h = om[:, 0, :].rearrange("p (h d) -> p h d", d=DK)
                oc.link(dve.tensor_tensor(osq[:, :], om[:, 0, :], om[:, 0, :], ALU.mult))
                oc.link(dve.tensor_reduce(orn[:, :], osq[:, :].rearrange("p (h d) -> p h d", d=DK), AX, ALU.add))
                dve.tensor_scalar(orn[:, :], orn[:, :], 1.0 / DK, 1e-5, ALU.mult, ALU.add).then_inc(o_var, 1)
                dve.wait_ge(o_std, i + 1)
                oc.link(dve.reciprocal(orn[:, :], orn[:, :]))
                oc.link(dve.tensor_tensor(o_h, o_h, orn[:, :].unsqueeze(2).to_broadcast([P, H0, DK]), ALU.mult))
                oc.link(dve.tensor_tensor(o_h, o_h, onw[:, :].unsqueeze(1).to_broadcast([P, H0, DK]), ALU.mult))
                oc.end()
                dve.wait_ge(og_turned, i)
                dve.tensor_tensor(og[:, :], om[:, 0, :], om[:, 2, :], ALU.mult).then_inc(og_set, 1)
                dve.wait_ge(o_mm, i + 1)
                dve.tensor_tensor(tile(res, i), tile(res, i), bank[2][:, 0:D], ALU.add).then_inc(o_added, 1)
            if stop == 2:
                return
            end_phase(dve, 4)
            layernorm(dve, seq, res, xn, 1)
            dve.tensor_copy(stats[:, 3, 0:1], stats[:, 2, 0:1]).then_inc(norm_done, 1)
            dve.wait_ge(mask_set, 7)
            dve.tensor_copy(ident_b[:, :], ident[:, :]).then_inc(c_set, 1)
            dve.tensor_reduce(row_one[:, :], ident[:, 0:P:32], AX, ALU.add).then_inc(c_set, 1)
            seq.link(dve.tensor_copy(number[:, :], number_i[:, :]))
            dve.wait_ge(ld5, 80)
            with dve.Fori(0, T) as i:
                dve.wait_ge(v_mm, i + 1)
                dve.tensor_copy(vaug[:, ds(i, 1), :, 0:D1].rearrange("p a h d -> p (a h) d"),
                                bank[1][:, 0:D].rearrange("p (h d) -> p h d", d=D1)).then_inc(v_set, 1)
                dve.tensor_tensor(tile(logit, i), bank[2][:, 0:E1], bg1[:, :], ALU.add).then_inc(v_set, 1)
            dve.wait_ge(v_set, 2 * T)
            wide = [P, T, E1]
            top = rs[:, 0, :]
            seq.link(dve.tensor_reduce(top, logit[:, :, :], AX, ALU.max))
            dve.tensor_tensor(rt[:, 0, :, :], logit[:, :, :], top.unsqueeze(2).to_broadcast(wide), ALU.subtract).then_inc(r_ready1, 1)
            dve.wait_ge(r_exp, 1)
            share = rt[:, 1, :, :]
            seq.link(dve.tensor_reduce(rs[:, 1, :], share, AX, ALU.add))
            seq.link(dve.reciprocal(rs[:, 0, :], rs[:, 1, :]))
            seq.link(dve.tensor_tensor(share, share, rs[:, 0, :].unsqueeze(2).to_broadcast(wide), ALU.mult))
            seq.link(dve.tensor_reduce(top, share, AX, ALU.max))
            best, cand = rt[:, 0, :, :], rt[:, 2, :, :]
            numbers = number[:, :].unsqueeze(1).to_broadcast(wide)
            seq.link(dve.tensor_tensor(best, share, top.unsqueeze(2).to_broadcast(wide), ALU.is_ge))
            seq.link(dve.scalar_tensor_tensor(out=cand, in0=numbers, scalar=-float(E1), in1=best, op0=ALU.add, op1=ALU.mult))
            seq.link(dve.tensor_reduce(rs[:, 1, :], cand, AX, ALU.min))
            seq.link(dve.scalar_tensor_tensor(out=best, in0=numbers, scalar=-float(E1), in1=rs[:, 1, :].unsqueeze(2).to_broadcast(wide),
                                              op0=ALU.add, op1=ALU.is_equal))
            seq.link(dve.tensor_tensor(route[:, :, :], best, share, ALU.mult))
            onc = Count(dve, v_on, per=4)
            with dve.Fori(0, B) as b:
                with dve.Fori(0, 4) as r:
                    i = b * 4 + r
                    onc.start(i)
                    dve.wait_ge(pj_mm, i + 1)
                    dve.tensor_copy(qpad[:, :], banks[:, 2048:3072]).then_inc(qk_set, 1)
                    dve.tensor_scalar(kaug[:, :], banks[:, 3072:4096], row_one[:, 0:1], None, ALU.add).then_inc(qk_set, 1)
                    for u in range(32):
                        g, t = u // TB, u % TB
                        dve.wait_ge(a_mm, 32 * i + u + 1)
                        dve.tensor_reduce(mxz[:, t, 32 * g:32 * g + 1], banks[:, 1024 * (u % 2):1024 * (u % 2) + (t + 1) * P],
                                          AX, ALU.max).then_inc(mx_read, 1)
                    dve.wait_ge(mx_turned, i + 1)
                    dve.tensor_tensor(qaug[:, :], qpad[:, :], banks[:, 2048:3072], ALU.subtract).then_inc(qaug_set, 1)
                    for g in range(4):
                        dve.wait_ge(c_mm, 4 * i + g + 1)
                        o_ps = bank[6 + g % 2][:, 0:TB * SLOT].rearrange("p (t d) -> p t d", d=SLOT)
                        onc.link(dve.reciprocal(inv_o[:, g, :], o_ps[:, :, D1:SLOT].rearrange("p t a -> p (t a)")))
                        dve.tensor_tensor(o_all[:, ds(b * TB, TB), ds(r * (4 * D1) + g * D1, D1)], o_ps[:, :, 0:D1],
                                          inv_o[:, g, :].unsqueeze(2).to_broadcast([P, TB, D1]), ALU.mult).then_inc(o_norm, 1)
                    onc.end()
            end_phase(dve, 5)
            with dve.Fori(0, T) as i:
                dve.wait_ge(pr_mm, i + 1)
                dve.tensor_tensor(tile(res, i), tile(res, i), bank[1][:, 0:D], ALU.add).then_inc(pr_added, 1)
            dve.wait_ge(pr_added, T)
            with dve.Fori(0, T // 4) as i:
                group = res[:, ds(4 * i, 4), :]
                dve.wait_ge(rb_mm, i + 1)
                dve.tensor_tensor(group, group, bank[7].rearrange("p (t d) -> p t d", d=D), ALU.add).then_inc(rb_added, 1)
                dve.wait_ge(rb_added, i + 1)
                for e in range(E1):
                    dve.wait_ge(e_mm, i * E1 + e + 1)
                    if e:
                        dve.wait_ge(e_added, i * (4 * E1) + 4 * e)
                    for t in range(4):
                        row = res[:, ds(4 * i + t, 1), :].rearrange("p a d -> p (a d)")
                        dve.scalar_tensor_tensor(out=row, in0=bank[4 + e % 2][:, P * t:P * t + P], scalar=st_r[:, E1 * t + e:E1 * t + e + 1],
                                                 in1=row, op0=ALU.mult, op1=ALU.add).then_inc(e_added, 1)


def kernel(**inputs):
    import concourse.bacc as bacc
    from concourse.bass_utils import run_bass_kernel_spmd

    n = {k: np.ascontiguousarray(v) for k, v in inputs.items()}
    arrays = {
        "x": n["L0_attn_hidden_states"].reshape(B * L, D),
        "w_gate": n["L0_ffn_w_gate"], "w_up": n["L0_ffn_w_up"], "w_down": n["L0_ffn_w_down"],
    }
    m = {k[8:]: v for k, v in n.items() if k.startswith("L0_attn_")}
    for w in ("Wq", "Wk", "Wv", "Wg", "Wo"):
        arrays[w] = m[w]
    arrays["bproj"] = np.concatenate([m["bq"], m["bk"], m["bv"], m["bg"]])[None]
    arrays["wgate"] = np.concatenate([m["Wb"], m["Wfd"], m["Wsd"], m["Wfg"], m["Wsg"]], 1)
    none = np.zeros(H0, np.float32)
    arrays["bgate"] = np.stack([np.concatenate([m["bb"], m["bfd"], m["bsd"], m["bfg"], m["bsg"]]),
                                np.concatenate([none, m["fast_decay_bias"], m["slow_decay_bias"], none, none])], 1)
    arrays["rf"] = m["resonance_flux"].reshape(1)
    arrays["onorm_w"] = m["onorm_w"]
    arrays["bo"] = m["bo"][None]
    for w in ("Wq", "Wk"):
        padded = np.zeros((D, 4, 4, 32), np.float32)
        padded[:, :, :, 1:1 + D1] = n["L1_attn_" + w].T.reshape(D, 4, 4, D1)
        arrays["W1" + w[1]] = padded.reshape(D, 4, P)
    arrays["W1v"] = n["L1_attn_Wv"].T
    arrays["W1p"] = n["L1_attn_Wp"].T
    arrays["bp1"] = n["L1_attn_bp"][None]
    arrays["Wg1"] = n["L1_ffn_Wg"]
    arrays["bg1"] = n["L1_ffn_bg"]
    arrays["W1"] = n["L1_ffn_W1"]
    arrays["W2"] = n["L1_ffn_W2"]
    arrays["b1"] = n["L1_ffn_b1"].reshape(E1, HID // P, P).transpose(2, 0, 1)
    arrays["b2"] = n["L1_ffn_b2"]
    arrays = {k: np.ascontiguousarray(v) for k, v in arrays.items()}
    nc = bacc.Bacc("TRN2", target_bir_lowering=False, num_devices=1)
    a = {k: nc.dram_tensor("in_" + k, v.shape, F32, kind="ExternalInput").ap() for k, v in arrays.items()}
    out = nc.dram_tensor("out_0", (B * L, D), F32, kind="ExternalOutput").ap()
    layer_kernel(nc, a, out, STOP)
    r = run_bass_kernel_spmd(nc, [{"in_" + k: v for k, v in arrays.items()}], core_ids=[0])
    return r.results[0]["out_0"].reshape(B, L, D)


STOP = 9
```

```python
from contextlib import ExitStack

import concourse.bass as bass
import numpy as np
from concourse import mybir

F32 = mybir.dt.float32
BF16 = mybir.dt.bfloat16
ALU = mybir.AluOpType
ACT = mybir.ActivationFunctionType
AX = mybir.AxisListType.X
ds = bass.ds

P = 128
D = 128
B, L = 4, 1024
T = B * L // P
H0, DK = 16, 64
HD = H0 * DK
INNER = 352
BLOCK = 16
H1, D1 = 16, 8
E1, HID = 8, 512
LN_EPS = 1e-5
TB = L // P
STEPS = 4
MASKED = -1e30
BOUND = 0.99 * DK
SUB = 16
NB = P // SUB
LEVELS = 3


class Count:

    def __init__(self, eng, sem, per=0):
        self.eng, self.sem, self.per, self.base, self.n = eng, sem, per, 0, 0

    def start(self, i):
        self.base, self.n = i * self.per, 0

    def done(self, ins):
        self.n += 1
        ins.then_inc(self.sem, 1)

    def link(self, ins):
        self.done(ins)
        self.eng.wait_ge(self.sem, self.base + self.n)

    def end(self):
        assert self.n == self.per, (self.n, self.per)


def layer_kernel(nc, a, out, stop=9):
    ctx = ExitStack()
    with ctx:
        def sem(name):
            return ctx.enter_context(nc.semaphore(name))

        def sb(name, shape, dt=F32, scope=ctx):
            return scope.enter_context(nc.sbuf_tensor(name, shape, dt))

        def dram(name, shape):
            return nc.dram_tensor(name, shape, F32, kind="Internal").ap()

        proj_s = dram("proj_s", (B * L, 4 * HD))
        gates_s = dram("gates_s", (5 * H0, B * L))
        mem_s = dram("mem_s", (B * L, HD))
        vnorm_s = dram("vnorm_s", (H0, B * L))
        nblk_s = dram("nblk_s", (T, H0 * NB, SUB * SUB))
        blk_s = dram("blk_s", (T, 3, H0, NB, SUB, SUB))
        pb_s = dram("pb_s", (H0, NB, T * 4))
        r_s = dram("r_s", (H0, 2 * NB, T, P))
        l_s = dram("l_s", (H0, 2 * NB, T, P))
        cf_s = dram("cf_s", (4 * H0, B * L))
        pc_s = dram("pc_s", (2, T, H0 // 2, 4))
        nrm_s = dram("nrm_s", (H0, T, 2))

        banks = ctx.enter_context(nc.psum_tensor("banks", [P, 8 * 512], F32))
        bank = [banks[:, 512 * n:512 * n + 512] for n in range(8)]

        res = sb("res", [P, T, D])
        ident = sb("ident", [P, P])
        ones_row = sb("ones_row", [1, P])
        stats = sb("stats", [P, 4, T])

        rf_c = sb("rf_c", [P, 1])
        capped_flag = sb("capped_flag", [1, 1], mybir.dt.int32)
        sA = ExitStack()
        xn = sb("xn", [P, T, D], scope=sA)
        xnT = sb("xnT", [P, B * L], scope=sA)

        s1 = ExitStack()
        xq = sb("xq", [P, T, D], scope=s1)
        fa = sb("fa", [P, T * D], scope=s1)
        fc = sb("fc", [P, T * D], scope=s1)
        fsg = sb("fsg", [P, T * D], scope=s1)
        fsc = sb("fsc", [P, 2, T * D // BLOCK], scope=s1)
        NW = 6 * P + INNER
        wraw = sb("wraw", [P, NW], scope=s1)
        wqt = sb("wqt", [P, NW], scope=s1)
        wguT = sb("wguT", [P, 2, 3 * P], scope=s1)
        wdT = sb("wdT", [P, 3, P], scope=s1)
        st_n = sb("st_n", [P, P], scope=s1)
        st_q = sb("st_q", [P, P], scope=s1)
        xqT = sb("xqT", [P, P], scope=s1)
        silu_g = sb("silu_g", [P, INNER], scope=s1)
        hid = sb("hid", [P, INNER], scope=s1)
        hq = sb("hq", [P, INNER], scope=s1)
        hqT = sb("hqT", [P, 3, P], scope=s1)
        s1.close()

        s2 = ExitStack()
        wproj = sb("wproj", [P, 4 * HD], scope=s2)
        bproj = sb("bproj", [1, 4 * HD], scope=s2)
        wgate = sb("wgate", [P, 5 * H0], scope=s2)
        bgate = sb("bgate", [5 * H0, 3], scope=s2)
        gates = sb("gates", [5 * H0, B * L], scope=s2)
        st_p = sb("st_p", [P, P], scope=s2)
        prj = sb("prj", [P, 4 * HD], scope=s2)
        prj_sq = sb("prj_sq", [P, 2 * HD], scope=s2)
        prj_n = sb("prj_n", [P, 2, 2 * H0], scope=s2)
        st_b = sb("st_b", [H0, P], scope=s2)
        sbeta = sb("sbeta", [H0, B * L], scope=s2)
        sb_tok = sb("sb_tok", [P, H0], scope=s2)
        vv = sb("vv", [P, H0], scope=s2)
        vrow = sb("vrow", [H0, B * L], scope=s2)
        s2.close()
        sA.close()

        sG = ExitStack()
        gu = sb("gu", [P, 4, T, SUB], scope=sG)
        cc = sb("cc", [P, 2, 2, T, SUB + 2], scope=sG)
        ca = sb("ca", [P, 2, T, SUB + 2], scope=sG)
        gl = sb("gl", [P, T, SUB + 2, SUB], scope=sG)
        rb = sb("rb", [P, 2 * NB, T, SUB], scope=sG)
        lx = sb("lx", [P, 2, T, NB, SUB], scope=sG)
        pb = sb("pb", [P, T, 4], scope=sG)
        pball = sb("pball", [P, NB * T * 4], scope=sG)
        cend = sb("cend", [P, 2, T, SUB], scope=sG)
        gam = sb("gam", [P, 2, T, SUB], scope=sG)
        yp = sb("yp", [P, T, 4], scope=sG)
        pc = sb("pc", [P, T, 4], scope=sG)
        y4 = sb("y4", [P, 2, T, 2, 2], scope=sG)
        bmask = sb("bmask", [P, NB], scope=sG)
        before = sb("before", [P, NB], scope=sG)
        one_rf = sb("one_rf", [P, 1], scope=sG)
        ka = sb("ka", [P, HD], scope=sG)
        kta = sb("kta", [P, 8 * P], scope=sG)
        ssa = sb("ssa", [P, H0, P], scope=sG)
        sG.close()
        sI = ExitStack()
        nb = sb("nb", [P, T, SUB * SUB], scope=sI)
        tb = sb("tb", [P, T, SUB, SUB], scope=sI)
        iprod = sb("iprod", [P, T * (SUB - 1) * (SUB - 1)], scope=sI)
        sI.close()
        sT = ExitStack()
        qkv_t = sb("qkv_t", [P, 2, 3 * HD], scope=sT)
        blk = sb("blk", [P, 2, 3, H0, P], scope=sT)
        rt_ = sb("rt_src", [P, 2, 8, P], scope=sT)
        lt_ = sb("lt", [P, 2, 8, P], scope=sT)
        cft = sb("cft", [64, 2, P], scope=sT)
        cf = sb("cf", [P, 64], scope=sT)
        kqt = sb("kqt", [P, 8, 2, P], scope=sT)
        cv = sb("cv", [P, 2, H0, DK], scope=sT)
        S_t = sb("S_t", [P, 8, 2 * DK], scope=sT)
        ss_sb = sb("ss_sb", [P, 2, 4, P], scope=sT)
        st_sb = sb("st_sb", [P, 2, 4, P], scope=sT)
        gt_sb = sb("gt_sb", [P, 2, 4, P], scope=sT)
        xs = sb("xs", [P, 2, 4, P], scope=sT)
        tw = sb("tw", [P, 2, 4, P], scope=sT)
        ttw = sb("ttw", [P, 2, 4, P], scope=sT)
        a_sb = sb("a_sb", [P, 2, 4, P], scope=sT)
        ag = sb("ag", [P, 2, 4, P], scope=sT)
        h_sb = sb("h_sb", [P, 2, 4, DK], scope=sT)
        ny = sb("ny", [P, 2, 4, P], scope=sT)
        zs = sb("zs", [P, 2, 2, P], scope=sT)
        za = sb("za", [P, 2, 2, 2, 2, DK], scope=sT)
        oa = sb("oa", [P, 2, 4, 2, DK], scope=sT)
        o_sb = sb("o_sb", [P, HD], scope=sT)
        sqs = sb("sqs", [P, HD], scope=sT)
        sqr = sb("sqr", [P, H0], scope=sT)
        half = sb("half", [P, 2], scope=sT)
        nrm_sb = sb("nrm_sb", [H0, T, 2], scope=sT)
        pcb = sb("pcb", [P, T * 8 * 4], scope=sT)
        lmask = sb("lmask", [P, LEVELS, P], scope=sT)
        umask = sb("umask", [P, P], scope=sT)
        sT.close()
        sB = ExitStack()
        bd = sb("bd", [P, 3, B, P], scope=sB)
        bn0 = sb("bn0", [P, B, 2], scope=sB)
        bnx = sb("bnx", [P, B, 2], scope=sB)
        bh = sb("bh", [P, P, 2, B], scope=sB)
        bt = sb("bt", [P, 2, B], scope=sB)
        rf_abs = sb("rf_abs", [P, 1], scope=sB)
        bmin = sb("bmin", [P, 1], scope=sB)
        sB.close()

        s3 = ExitStack()
        S = sb("S", [P, DK, DK], scope=s3)
        prod = sb("prod", [P, DK, DK], scope=s3)
        outer = sb("outer", [P, DK, DK], scope=s3)
        Snew = sb("Snew", [P, DK * DK], scope=s3)
        junk = sb("junk", [P, 8 * 512], BF16, scope=s3)
        qkv = sb("qkv", [P, 2, 3, STEPS, DK], scope=s3)
        ohalf = sb("ohalf", [P, STEPS, DK], scope=s3)
        obuf = sb("obuf", [B * H0, 2, STEPS, DK], scope=s3)
        pair_sum = sb("pair_sum", [P, B * H0], scope=s3)
        gdec = sb("gdec", [P, L], scope=s3)
        gndec = sb("gndec", [P, L], scope=s3)
        gout = sb("gout", [P, L], scope=s3)
        mix = sb("mix", [P, P], scope=s3)
        rf_col = sb("rf_col", [P, 1], scope=s3)
        small = sb("small", [P, 4, DK], scope=s3)
        gcur = sb("gcur", [P, 4, 2 * STEPS], scope=s3)
        cap = sb("cap", [P, 6], scope=s3)
        s3.close()

        s4 = ExitStack()
        om = sb("om", [P, 3, HD], scope=s4)
        osq = sb("osq", [P, HD], scope=s4)
        orn = sb("orn", [P, H0], scope=s4)
        og = sb("og", [P, HD], scope=s4)
        ogT = sb("ogT", [P, 8, P], scope=s4)
        wout = sb("wout", [P, 8, D], scope=s4)
        bout = sb("bout", [1, D], scope=s4)
        onw = sb("onw", [P, DK], scope=s4)
        s4.close()

        s5 = ExitStack()
        xn1 = sb("xn1", [P, T, D], scope=s5)
        xnT1 = sb("xnT1", [P, B * L], scope=s5)
        SLOT = 9
        vaug = sb("vaug", [P, T, H1, SLOT], scope=s5)
        o_all = sb("o_all", [P, T, D], scope=s5)
        route = sb("route", [P, T, E1], scope=s5)
        s6 = ExitStack()
        wq1 = sb("wq1", [P, 4, P], scope=s6)
        wk1 = sb("wk1", [P, 4, P], scope=s6)
        wv1 = sb("wv1", [P, D], scope=s6)
        wg1 = sb("wg1", [P, E1], scope=s6)
        bg1 = sb("bg1", [P, E1], scope=s6)
        logit = sb("logit", [P, T, E1], scope=s6)
        rt = sb("rt", [P, 3, T, E1], scope=s6)
        rs = sb("rs", [P, 2, T], scope=s6)
        number_i = sb("number_i", [P, E1], mybir.dt.int32, scope=s6)
        number = sb("number", [P, E1], scope=s6)
        st_x = sb("st_x", [P, P], scope=s6)
        xt_x = sb("xt_x", [P, P], scope=s6)
        st_wq = sb("st_wq", [P, P], scope=s6)
        st_wk = sb("st_wk", [P, P], scope=s6)
        qpad = sb("qpad", [P, L], scope=s6)
        qaug = sb("qaug", [P, L], scope=s6)
        kaug = sb("kaug", [P, L], scope=s6)
        mxz = sb("mxz", [P, TB, P], scope=s6)
        row_one = sb("row_one", [P, 1], scope=s6)
        ident_b = sb("ident_b", [P, P], BF16, scope=s6)
        above = sb("above", [P, P], BF16, scope=s6)
        below = sb("below", [P, P], BF16, scope=s6)
        TRI = TB * (TB + 1) // 2 * P
        probs = sb("probs", [P, 2, TRI], scope=s6)
        inv_o = sb("inv_o", [P, 4, TB], scope=s6)
        s6.close()
        s7 = ExitStack()
        w1 = sb("w1", [P, E1, HID], scope=s7)
        w2 = sb("w2", [P, E1, HID // P, D], scope=s7)
        b1 = sb("b1", [P, E1, HID // P], scope=s7)
        b2 = sb("b2", [E1, D], scope=s7)
        wp1 = sb("wp1", [P, D], scope=s7)
        bp1 = sb("bp1", [1, D], scope=s7)
        st_o = sb("st_o", [P, P], scope=s7)
        oT1 = sb("oT1", [P, P], scope=s7)
        st_r = sb("st_r", [P, 4 * E1], scope=s7)
        rT = sb("rT", [E1, 4 * P], scope=s7)
        hT1 = sb("hT1", [P, 2, 4, 512], scope=s7)
        s7.close()
        s5.close()

        ld = sem("ld")
        ld1 = sem("ld1")
        const_set = sem("const_set")
        v_seq = sem("v_seq")
        norm_done = sem("norm_done")
        var_done = sem("var_done")
        std_done = sem("std_done")
        sign_done = sem("sign_done")
        wq_done = sem("wq_done")
        wt_done = sem("wt_done")
        wT_done = sem("wT_done")
        xq_done = sem("xq_done")
        staged = sem("staged")
        x_turned = sem("x_turned")
        xT_done = sem("xT_done")
        gu_done = sem("gu_done")
        silu_done = sem("silu_done")
        hid_done = sem("hid_done")
        hsign_done = sem("hsign_done")
        v_ffn = sem("v_ffn")
        hq_done = sem("hq_done")
        h_turned = sem("h_turned")
        hT_done = sem("hT_done")
        down_done = sem("down_done")
        ffn_added = sem("ffn_added")

        phase = sem("phase")
        ld2 = sem("ld2")
        p_staged = sem("p_staged")
        p_mm = sem("p_mm")
        p_silu = sem("p_silu")
        p_var = sem("p_var")
        p_std = sem("p_std")
        v_prj = sem("v_prj")
        p_normed = sem("p_normed")
        p_stored = sem("p_stored")
        g_bias = sem("g_bias")
        g_mm = sem("g_mm")
        g_done = sem("g_done")
        g_stored = sem("g_stored")
        ld3 = sem("ld3")
        swap_set = sem("swap_set")
        v_pre = sem("v_pre")
        r_ready = sem("r_ready")
        v_rec = sem("v_rec")
        qkv_in = [sem(f"qkv_in{n}") for n in range(2)]
        stepped = [sem(f"stepped{n}") for n in range(2)]
        updated = sem("updated")
        mixed = sem("mixed")
        squared = sem("squared")
        ratio_set = sem("ratio_set")
        ratio_root = sem("ratio_root")
        lam_set = sem("lam_set")
        state_set = sem("state_set")
        state_read = sem("state_read")
        o_stored = [sem(f"o_stored{n}") for n in range(2)]
        ld4 = sem("ld4")
        om_in = sem("om_in")
        v_out = sem("v_out")
        o_var = sem("o_var")
        o_std = sem("o_std")
        og_set = sem("og_set")
        og_turned = sem("og_turned")
        ogT_set = sem("ogT_set")
        o_mm = sem("o_mm")
        o_added = sem("o_added")


        sb_root = sem("sb_root")
        sbt_set = sem("sbt_set")
        vv_set = sem("vv_set")
        vv_turned = sem("vv_turned")
        vrow_set = sem("vrow_set")
        vrow_root = sem("vrow_root")
        pb_turned = sem("pb_turned")
        answered = sem("answered")
        summed = sem("summed")

        gu_in = sem("gu_in")
        ka_in = sem("ka_in")
        ka_turned = sem("ka_turned")
        kt_kept = sem("kt_kept")
        ss_mm = sem("ss_mm")
        ss_kept = sem("ss_kept")
        nblk_out = sem("nblk_out")
        pb_set = sem("pb_set")
        pb_out = sem("pb_out")
        pball_in = sem("pball_in")
        gate_set = sem("gate_set")
        gate_out = sem("gate_out")
        cc_set = sem("cc_set")
        nb_in = sem("nb_in")
        inv_set = sem("inv_set")
        inv_out = sem("inv_out")
        pc_in = sem("pc_in")
        zero_set = sem("zero_set")
        lm_set = sem("lm_set")
        kq_turned = sem("kq_turned")
        kq_kept = sem("kq_kept")
        sq_set = sem("sq_set")
        nrm_mm = sem("nrm_mm")
        nrm_set = sem("nrm_set")
        nrm_out = sem("nrm_out")
        cf_kept = sem("cf_kept")
        cv_set = sem("cv_set")
        kq_mm = sem("kq_mm")
        g_mm2 = sem("g_mm2")
        ss_set = sem("ss_set")
        st_set = sem("st_set")
        g_kept = sem("g_kept")
        y_mm = sem("y_mm")
        ny_set = sem("ny_set")
        am_mm = sem("am_mm")
        a_kept = sem("a_kept")
        hm_mm = sem("hm_mm")
        h_kept = sem("h_kept")
        z_mm = sem("z_mm")
        qs_mm = sem("qs_mm")
        av_mm = sem("av_mm")
        ag_set = sem("ag_set")
        s_new = sem("s_new")
        s_zero = sem("s_zero")
        o_set = sem("o_set")
        o_kept = sem("o_kept")
        v_tile = sem("v_tile")
        bd_in = sem("bd_in")
        bn_root = sem("bn_root")
        bmin_set = sem("bmin_set")
        bt_mm = sem("bt_mm")
        flag_set = sem("flag_set")
        x_mm = [sem(f"x_mm{n}") for n in range(LEVELS)]
        x_set = [sem(f"x_set{n}") for n in range(LEVELS)]
        u_mm = [sem(f"u_mm{n}") for n in range(LEVELS)]
        tw_set = [sem(f"tw_set{n}") for n in range(LEVELS)]
        ut_mm = [sem(f"ut_mm{n}") for n in range(LEVELS - 1)]
        ttw_set = [sem(f"ttw_set{n}") for n in range(LEVELS - 1)]
        tile_in = [sem(f"tile_in{n}") for n in range(2)]
        tile_free = [sem(f"tile_free{n}") for n in range(2)]
        cleared = sem("cleared")
        again = [gu_in, ka_in, ka_turned, kt_kept, ss_mm, ss_kept, pb_set, pb_out, pball_in, gate_set, gate_out, cc_set, nb_in, inv_set, inv_out, pc_in, zero_set, lm_set, kq_turned, kq_kept, sq_set, nrm_mm, nrm_set, nrm_out, cf_kept, cv_set, kq_mm, g_mm2, ss_set, st_set, g_kept, y_mm, ny_set, am_mm, a_kept, hm_mm, h_kept, z_mm]
        (ld5, mask_set, c_set, x1_staged, x1_turned, x1T_set, v_mm, v_set, w_staged, pj_mm, qk_set, a_mm, mx_read, mx_turned, qaug_set, b_mm, exp_done, c_mm, v_on, o_norm, ld6, o_staged, o1_turned, o1T_set, pr_mm, pr_added, r_exp, r_ready1, r_staged, r_turned, rT_set, rb_mm, rb_added, h_mm, h_silu, e_mm, e_added, out_stored) = again
        block = ctx.enter_context(nc.Block())

        phases = {}

        def end_phase(eng):
            phases[eng] = phases.get(eng, 0) + 5
            eng.drain().then_inc(phase, 1)
            eng.wait_ge(phase, phases[eng])

        def tile(buf, i):
            return buf[:, ds(i, 1), :].rearrange("p a d -> p (a d)")

        def layernorm(dve, c, src, dst, turned, layer):
            tot, mean, rstd = stats[:, 0, :], stats[:, 1, :], stats[:, 2, :]
            c.link(dve.tensor_reduce(tot, src[:, :, :], AX, ALU.add))
            c.link(dve.tensor_scalar(mean, tot, 1.0 / D, None, ALU.mult))
            c.link(dve.tensor_tensor(dst[:, :, :], src[:, :, :], mean.unsqueeze(2).to_broadcast([P, T, D]), ALU.subtract))
            sq = turned[:, :].rearrange("p (t d) -> p t d", d=D)
            c.link(dve.tensor_tensor(sq, dst[:, :, :], dst[:, :, :], ALU.mult))
            c.link(dve.tensor_reduce(tot, sq, AX, ALU.add))
            dve.tensor_scalar(mean, tot, 1.0 / D, LN_EPS, ALU.mult, ALU.add).then_inc(var_done, 1)
            dve.wait_ge(std_done, layer + 1)
            c.link(dve.reciprocal(rstd, tot))
            c.link(dve.tensor_tensor(dst[:, :, :], dst[:, :, :], rstd.unsqueeze(2).to_broadcast([P, T, D]), ALU.mult))

        def quantize(dve, c, src, n, a_, acc, sgn, sc, dst, sign_ready):
            def blocks(x):
                return x.rearrange("p (n k) -> p n k", k=BLOCK)
            scale, inv = sc[:, 0, 0:n], sc[:, 1, 0:n]
            c.link(dve.tensor_reduce(scale, blocks(src), AX, ALU.max, apply_absolute_value=True))
            c.link(dve.tensor_scalar(scale, scale, 1.0 / 6.0, 1e-12, ALU.mult, ALU.max))
            c.link(dve.reciprocal(inv, scale))
            sign_ready()
            c.link(dve.tensor_tensor(blocks(a_), blocks(a_), inv.unsqueeze(2).to_broadcast([P, n, BLOCK]), ALU.mult))
            c.link(dve.tensor_scalar(acc, a_, 5.0, 2.0, ALU.is_gt, ALU.mult))
            for mid in (3.5, 2.5):
                c.link(dve.scalar_tensor_tensor(out=acc, in0=a_, scalar=mid, in1=acc, op0=ALU.is_gt, op1=ALU.add))
            c.link(dve.tensor_scalar(acc, acc, 2.0, None, ALU.mult))
            for mid in (1.75, 1.25, 0.75, 0.25):
                c.link(dve.scalar_tensor_tensor(out=acc, in0=a_, scalar=mid, in1=acc, op0=ALU.is_gt, op1=ALU.add))
            c.link(dve.scalar_tensor_tensor(out=acc, in0=acc, scalar=0.5, in1=sgn, op0=ALU.mult, op1=ALU.mult))
            return dve.tensor_tensor(blocks(dst), blocks(acc), scale.unsqueeze(2).to_broadcast([P, n, BLOCK]), ALU.mult)

        def chunk_sync(sp):
            for k in range(4):
                for h in range(H0):
                    sp.dma_start(gu[NB * h:NB * h + NB, k, :, :],
                                 gates_s[(k + 1) * H0 + h, :].rearrange("(t j o) -> j t o", j=NB, o=SUB)).then_inc(gu_in, 16)
            sp.dma_start(rf_c[:, :], a["rf"].partition_broadcast(P)).then_inc(gu_in, 16)
            pj = proj_s.rearrange("(t p) n -> t p n", p=P)
            with sp.Fori(0, T) as i:
                sp.wait_ge(ka_turned, i)
                sp.dma_start(ka[:, :], pj[ds(i, 1), :, HD:2 * HD].rearrange("a p n -> (a p) n")).then_inc(ka_in, 16)
            sp.wait_ge(pb_set, 1)
            sp.dma_start(pb_s.rearrange("h j n -> (h j) n"), pb[:, :, :].rearrange("p t q -> p (t q)")).then_inc(pb_out, 16)
            sp.wait_ge(pb_out, 16)
            for h in range(H0):
                sp.dma_start(pball[NB * h:NB * h + NB, :], pb_s[h, :, :].rearrange("j n -> (j n)").partition_broadcast(NB))\
                    .then_inc(pball_in, 16)
            sp.wait_ge(gate_set, 1)
            sp.dma_start(blk_s[:, 2, :, :, :, :].rearrange("t h j s o -> (h j) t (s o)"),
                         gl[:, :, 0:SUB, :].rearrange("p t s o -> p t (s o)")).then_inc(gate_out, 16)
            for h in range(H0):
                u = slice(NB * h, NB * h + NB)
                sp.dma_start(r_s[h, :, :, :].rearrange("r t (j s) -> j (r t) s", s=SUB),
                             rb[u, :, :, :].rearrange("p r t s -> p (r t) s")).then_inc(gate_out, 16)
                sp.dma_start(l_s[h, :, :, :].rearrange("(i r) t n -> i (r t n)", r=2),
                             lx[u, :, :, :, :].rearrange("p r t j o -> p (r t j o)")).then_inc(gate_out, 16)
                for k, src in enumerate((gam[u, 0], gam[u, 1], cend[u, 0], cend[u, 1])):
                    sp.dma_start(cf_s[k * H0 + h, :].rearrange("(t j o) -> j t o", j=NB, o=SUB), src).then_inc(gate_out, 16)
                sp.dma_start(pc_s[h % 2, :, h // 2, :].rearrange("(a t) q -> a t q", a=1), pc[NB * h:NB * h + 1, :, :]).then_inc(gate_out, 16)
            sp.wait_ge(gate_out, 16 * (1 + 7 * H0))
            end_phase(sp)
            sp.dma_start(nb[:, :, :], nblk_s.rearrange("t u n -> u t n")).then_inc(nb_in, 16)
            sp.wait_ge(inv_set, 1)
            sp.dma_start(blk_s[:, 0, :, :, :, :].rearrange("t h j s o -> (h j) t (s o)"), tb[:, :, :, :].rearrange("p t s o -> p t (s o)")).then_inc(inv_out, 16)
            sp.wait_ge(inv_set, 2)
            sp.dma_start(blk_s[:, 1, :, :, :, :].rearrange("t h j s o -> (h j) t (s o)"), nb[:, :, :]).then_inc(inv_out, 16)
            sp.wait_ge(inv_out, 32)
            end_phase(sp)
            for e in range(2):
                sp.dma_start(pcb[64 * e:64 * e + 64, :], pc_s[e, :, :, :].rearrange("t h q -> (t h q)").partition_broadcast(64)).then_inc(pc_in, 16)
            cf_t = cf_s.rearrange("r (t p) -> t r p", p=P)
            ms = mem_s.rearrange("(t p) n -> t p n", p=P)
            sp.wait_ge(zero_set, 2)
            with sp.Fori(0, B) as b:
                with sp.Fori(0, TB // 2) as c:
                    for n in range(2):
                        i = b * TB + c * 2 + n
                        sp.wait_ge(tile_free[n], b * (TB // 2) + c)
                        sp.dma_start(qkv_t[:, n, :], pj[ds(i, 1), :, 0:3 * HD].rearrange("a p n -> (a p) n")).then_inc(tile_in[n], 16)
                        for j in range(NB):
                            sp.dma_start(blk[SUB * j:SUB * j + SUB, n, :, :, SUB * j:SUB * j + SUB].rearrange("p k h o -> p (k h) o"),
                                         blk_s[ds(i, 1), :, :, j, :, :].rearrange("a k h s o -> s (a k h) o")).then_inc(tile_in[n], 16)
                        for m in range(2):
                            for buf, src in ((rt_, r_s), (lt_, l_s)):
                                sp.dma_start(buf[32 * m:32 * m + 16, n, :, :],
                                             src[m:H0:2, :, ds(i, 1), :].rearrange("g r a s -> r g (a s)")).then_inc(tile_in[n], 16)
                        sp.dma_start(cft[:, n, :], cf_t[ds(i, 1), :, :].rearrange("a r p -> (a r) p")).then_inc(tile_in[n], 16)
            sp.wait_ge(nrm_set, T)
            sp.dma_start(nrm_s[:, :, :], nrm_sb[:, :, :]).then_inc(nrm_out, 16)
            sp.wait_ge(nrm_out, 16)
            sp.wait_ge(o_kept, 16 * T)
            end_phase(sp)
            for h in range(H0):
                u = slice(TB * h, TB * h + TB)
                for k, src in enumerate((gates_s[H0 + h], gates_s[2 * H0 + h], vnorm_s[h])):
                    sp.dma_start(bd[u, k, :, :], src.rearrange("(b c o) -> c b o", b=B, c=TB)).then_inc(bd_in, 16)
                for j in range(2):
                    sp.dma_start(bn0[u, :, j:j + 1], nrm_s[(h // 2) * 2 + j, :, h % 2:h % 2 + 1].rearrange("(b c) e -> c b e", b=B),
                                 allow_slow_non_contiguous=True).then_inc(bd_in, 16)
            end_phase(sp)

        def chunk_pool(pool):
            if True:
                pool.memset(cc[:, :, :, :, :], 0.0).then_inc(cc_set, 1)
            nv = nblk_s.rearrange("t (h j) (s o) -> t j s h o", j=NB, o=SUB)
            with pool.Fori(0, T) as i:
                pool.wait_ge(ss_kept, 4 * i + 4)
                for j in range(NB):
                    pool.dma_start(nv[ds(i, 1), j, :, :, :].rearrange("a s h o -> (a s) h o"),
                                   ssa[SUB * j:SUB * j + SUB, :, SUB * j:SUB * j + SUB]).then_inc(nblk_out, 16)
                pool.wait_ge(nblk_out, 16 * NB * (i + 1))
            end_phase(pool)
            end_phase(pool)
            pool.memset(blk[:, :, :, :, :], 0.0).then_inc(zero_set, 1)
            pool.memset(half[:, :], 0.0).then_inc(zero_set, 1)
            pool.memset(lmask[:, :, :], 0.0).then_inc(lm_set, 1)
            pool.memset(umask[:, :], 1.0).then_inc(lm_set, 1)
            pool.wait_ge(zero_set, 2)
            pool.wait_ge(lm_set, 2)
            pool.memset(half[0:64, 0:1], 1.0).then_inc(lm_set, 1)
            pool.wait_ge(lm_set, 3)
            pool.memset(half[64:128, 1:2], 1.0).then_inc(lm_set, 1)
            pool.wait_ge(lm_set, 4)
            for n in range(LEVELS):
                w = SUB << n
                v = lmask[:, n, :].rearrange("p (q a c) -> p q a c", a=2, c=w)[:, :, 0, :]
                pool.memset(v, 1.0).then_inc(lm_set, 1)
            pool.wait_ge(lm_set, 4 + LEVELS)
            for n in range(LEVELS):
                w = SUB << n
                v = lmask[:, n, :].rearrange("p (q a c) -> p q a c", a=2, c=w)[:, :, 0, :]
                pool.affine_select(out=v, in_=v, compare_op=ALU.is_ge, fill=0.0, base=-w,
                                   pattern=[[-2 * w, P // (2 * w)], [0, w]], channel_multiplier=1).then_inc(lm_set, 1)
                pool.wait_ge(lm_set, 5 + LEVELS + 2 * n)
                pool.affine_select(out=v, in_=v, compare_op=ALU.is_ge, fill=0.0, base=2 * w - 1,
                                   pattern=[[2 * w, P // (2 * w)], [0, w]], channel_multiplier=-1).then_inc(lm_set, 1)
            pool.affine_select(out=umask[:, :], in_=umask[:, :], compare_op=ALU.is_ge, fill=0.0, base=0,
                               pattern=[[1, P]], channel_multiplier=-1).then_inc(lm_set, 1)
            ms = mem_s.rearrange("(t p) n -> t p n", p=P)
            with pool.Fori(0, B) as b:
                with pool.Fori(0, TB) as c:
                    i = b * TB + c
                    for g in range(4):
                        at = 4 * i + g + 1
                        y = g % 2
                        pool.wait_ge(a_kept, at)
                        pool.wait_ge(g_kept, at)
                        pool.tensor_tensor(ag[:, y, :, :], a_sb[:, y, :, :], gt_sb[:, y, :, :], ALU.mult).then_inc(ag_set, 1)
                    pool.wait_ge(o_set, 4 * i + 4)
                    pool.dma_start(ms[ds(i, 1), :, :].rearrange("a p n -> (a p) n"), o_sb[:, :]).then_inc(o_kept, 16)
            end_phase(pool)
            end_phase(pool)

        def chunk_pe(pe):
            with pe.Fori(0, T) as i:
                pe.wait_ge(ka_in, 16 * (i + 1))
                pe.wait_ge(kt_kept, 2 * i)
                for p in range(8):
                    last = pe.transpose(bank[p // 4][:, P * (p % 4):P * (p % 4) + P], ka[:, P * p:P * p + P], ident[:, :])
                last.then_inc(ka_turned, 1)
                pe.wait_ge(kt_kept, 2 * i + 2)
                pe.wait_ge(ss_kept, 4 * i)
                for p in range(8):
                    for e in range(2):
                        kt = kta[64 * e:64 * e + 64, P * p:P * p + P]
                        last = pe.matmul(bank[2 + 2 * (p // 4) + e][:, P * (p % 4):P * (p % 4) + P], kt, kt, start=True, stop=True)
                    if p % 4 == 3:
                        last.then_inc(ss_mm, 2)
            end_phase(pe)
            end_phase(pe)
            pe.wait_ge(lm_set, 5 + 3 * LEVELS)

            def heads(g):
                return [(m, 4 * g + m, slice(64 * (m % 2), 64 * (m % 2) + 64), (4 * g + m) // 2) for m in range(4)]

            def cols(bk, m, w=P):
                return bk[:, w * m:w * m + w]

            with pe.Fori(0, B) as b:
                with pe.Fori(0, TB // 2) as c:
                    for n in range(2):
                        i = b * TB + c * 2 + n
                        k_ = qkv_t[:, n, HD:2 * HD]
                        v_ = qkv_t[:, n, 2 * HD:3 * HD]
                        pe.wait_ge(tile_in[n], 16 * 14 * (b * (TB // 2) + c + 1))
                        pe.wait_ge(o_set, 4 * i)
                        pe.wait_ge(s_new, 4 * i)
                        for w, at in ((1, 0), (0, 2)):
                            for p in range(8):
                                last = pe.transpose(cols(bank[at + p // 4], p % 4), qkv_t[:, n, w * HD + P * p:w * HD + P * p + P], ident[:, :])
                        pe.transpose(bank[4][:, 0:64], cft[:, n, :], ident[0:64, 0:64]).then_inc(kq_turned, 1)
                        pe.wait_ge(sq_set, i + 1)
                        pe.matmul(bank[5][0:H0, 0:2], sqr[:, :], half[:, :], start=True, stop=True).then_inc(nrm_mm, 1)
                        pe.wait_ge(kq_kept, 4 * i + 4)
                        pe.wait_ge(cf_kept, i + 1)
                        pe.wait_ge(nrm_set, i + 1)
                        for q in range(2):
                            pair = (2 * q, 2 * q + 1)

                            def at(g):
                                return 4 * i + g + 1
                            for g in pair:
                                bk = bank[4 * (g % 2):4 * (g % 2) + 4]
                                if g >= 2:
                                    pe.wait_ge(o_set, at(g) - 2)
                                    pe.wait_ge(s_new, at(g) - 2)
                                for m, h, r, p in heads(g):
                                    last = pe.matmul(bk[m % 2][:, 256 * (m // 2):256 * (m // 2) + 256], kqt[r, p, 0, :],
                                                     kqt[r, p, :, :].rearrange("p w t -> p (w t)"), start=True, stop=True)
                                last.then_inc(kq_mm, 1)
                                for m, h, r, p in heads(g):
                                    last = pe.matmul(cols(bk[2 + m % 2], m // 2), rt_[32 * (m % 2):32 * (m % 2) + 16, n, p, :], lt_[32 * (m % 2):32 * (m % 2) + 16, n, p, :],
                                                     start=True, stop=True)
                                last.then_inc(g_mm2, 1)
                            for lv in range(LEVELS):
                                def cur(buf, kind, g, h):
                                    return blk[:, n, kind, h, :] if lv == 0 else buf[:, g % 2, h % 4, :]
                                for g in pair:
                                    bk = bank[4 * (g % 2):4 * (g % 2) + 4]
                                    if lv == 0:
                                        pe.wait_ge(ss_set, at(g))
                                        pe.wait_ge(g_kept, at(g))
                                    else:
                                        pe.wait_ge(tw_set[lv - 1], at(g))
                                    for m, h, r, p in heads(g):
                                        last = pe.matmul(cols(bk[3], m), ss_sb[:, g % 2, m, :], cur(tw, 0, g, h), start=True, stop=True)
                                    last.then_inc(x_mm[lv], 1)
                                for g in pair:
                                    bk = bank[4 * (g % 2):4 * (g % 2) + 4]
                                    pe.wait_ge(x_set[lv], at(g))
                                    if lv == 0:
                                        pe.wait_ge(st_set, at(g))
                                    else:
                                        pe.wait_ge(ttw_set[lv - 1], at(g))
                                    for m, h, r, p in heads(g):
                                        last = pe.matmul(cols(bk[0], m), cur(ttw, 1, g, h), xs[:, g % 2, m, :], start=True, stop=True)
                                    last.then_inc(u_mm[lv], 1)
                                    if lv < LEVELS - 1:
                                        for m, h, r, p in heads(g):
                                            last = pe.matmul(cols(bk[1], m), xs[:, g % 2, m, :], cur(ttw, 1, g, h), start=True, stop=True)
                                        last.then_inc(ut_mm[lv], 1)
                            for g in pair:
                                bk = bank[4 * (g % 2):4 * (g % 2) + 4]
                                for m, h, r, p in heads(g):
                                    last = pe.matmul(cols(bk[3 - m % 2], m // 2), kqt[r, p, 0, :], S_t[r, p, :], start=True, stop=True)
                                last.then_inc(y_mm, 1)
                            for g in pair:
                                bk = bank[4 * (g % 2):4 * (g % 2) + 4]
                                pe.wait_ge(tw_set[LEVELS - 1], at(g))
                                for m, h, r, p in heads(g):
                                    last = pe.matmul(cols(bk[1], m), tw[:, g % 2, m, :], st_sb[:, g % 2, m, :], start=True, stop=True)
                                last.then_inc(am_mm, 1)
                                pe.wait_ge(ny_set, at(g))
                                for m, h, r, p in heads(g):
                                    last = pe.matmul(cols(bk[2], m, 64), tw[:, g % 2, m, :], k_[:, DK * h:DK * h + DK], start=True, stop=True)
                                last.then_inc(hm_mm, 1)
                            for g in pair:
                                bk = bank[4 * (g % 2):4 * (g % 2) + 4]
                                pe.wait_ge(ny_set, at(g))
                                pe.wait_ge(h_kept, at(g))
                                pe.wait_ge(cv_set, i + 1)
                                for m, h, r, p in heads(g):
                                    pe.matmul(bk[0][r, P * (m // 2):P * (m // 2) + P], h_sb[:, g % 2, m, :], ny[:, g % 2, m, :], start=True, stop=True)
                                    last = pe.matmul(bk[0][r, 256 + P * (m // 2):256 + P * (m // 2) + P], h_sb[:, g % 2, m, :],
                                                     cv[:, :, h, :], start=True, stop=True)
                                last.then_inc(z_mm, 1)
                                pe.wait_ge(a_kept, at(g))
                                for m, h, r, p in heads(g):
                                    pe.matmul(cols(bk[2 + m % 2], m // 2), kqt[r, p, 1, :], S_t[r, p, :], start=True, stop=False)
                                    last = pe.matmul(cols(bk[2 + m % 2], m // 2), a_sb[:, g % 2, m, :], ny[:, g % 2, m, :], start=False, stop=True)
                                last.then_inc(qs_mm, 1)
                                pe.wait_ge(ag_set, at(g))
                                for m, h, r, p in heads(g):
                                    last = pe.matmul(cols(bk[1], m, 64), ag[:, g % 2, m, :], v_[:, DK * h:DK * h + DK], start=True, stop=True)
                                last.then_inc(av_mm, 1)
            end_phase(pe)
            pe.wait_ge(bmin_set, 1)
            pe.transpose(bank[0][0:1, 0:P], bmin[:, :], ident[:, :]).then_inc(bt_mm, 1)
            end_phase(pe)

        def chunk_act(act):
            with act.Fori(0, T) as i:
                act.wait_ge(ka_turned, i + 1)
                act.wait_ge(ss_mm, 4 * i)
                for q in range(2):
                    act.copy(kta[:, 512 * q:512 * q + 512], bank[q]).then_inc(kt_kept, 1)
                act.wait_ge(nblk_out, 16 * NB * i)
                for g in range(4):
                    act.wait_ge(ss_mm, 4 * i + 2 * (g // 2) + 2)
                    h = 8 * (g // 2) + g % 2
                    act.copy(ssa[:, h:h + 7:2, :], bank[2 + g].rearrange("p (h t) -> p h t", t=P)).then_inc(ss_kept, 1)
            end_phase(act)
            end_phase(act)
            with act.Fori(0, B) as b:
                with act.Fori(0, TB) as c:
                    i = b * TB + c
                    act.wait_ge(kq_turned, i + 1)
                    for w, at in ((0, 0), (1, 2)):
                        for q in range(2):
                            act.copy(kqt[:, 4 * q:4 * q + 4, w, :], bank[at + q].rearrange("p (h t) -> p h t", t=P)).then_inc(kq_kept, 1)
                    act.wait_ge(nrm_mm, i + 1)
                    act.copy(nrm_sb[:, ds(i, 1), :].rearrange("p a j -> p (a j)"), bank[5][0:H0, 0:2]).then_inc(nrm_set, 1)
                    for q in range(2):
                        pair = (2 * q, 2 * q + 1)
                        for g in pair:
                            y = g % 2
                            act.wait_ge(kq_mm, 4 * i + g + 1)
                            act.copy(ss_sb[:, y, :, :].rearrange("p (k e) t -> p e k t", e=2),
                                     banks[:, 2048 * y:2048 * y + 1024].rearrange("p (e k w t) -> p e k w t", e=2, w=2, t=P)[:, :, :, 0, :])\
                                .then_inc(ss_set, 1)
                        for g in pair:
                            y = g % 2
                            act.wait_ge(y_mm, 4 * i + g + 1)
                            act.mul(ny[:, y, 0:4:2, :], bank[4 * y + 3][:, 0:256].rearrange("p (k t) -> p k t", t=P), -1.0)
                            act.mul(ny[:, y, 1:4:2, :], bank[4 * y + 2][:, 0:256].rearrange("p (k t) -> p k t", t=P), -1.0).then_inc(ny_set, 1)
                        for g in pair:
                            y = g % 2
                            act.wait_ge(am_mm, 4 * i + g + 1)
                            act.copy(a_sb[:, y, :, :].rearrange("p h t -> p (h t)"), bank[4 * y + 1]).then_inc(a_kept, 1)
                            act.wait_ge(hm_mm, 4 * i + g + 1)
                            act.copy(h_sb[:, y, :, :].rearrange("p h t -> p (h t)"), bank[4 * y + 2][:, 0:256]).then_inc(h_kept, 1)
            end_phase(act)
            act.wait_ge(bd_in, 16 * 5 * H0)
            act.activation(bnx[:, :, :], bn0[:, :, :], ACT.Sqrt).then_inc(bn_root, 1)
            act.activation(rf_abs[:, :], rf_c[:, :], ACT.Abs).then_inc(bn_root, 1)
            end_phase(act)

        def chunk_dve(dve, seq):
            dve.wait_ge(gu_in, 16 * (4 * H0 + 1))
            dve.wait_ge(cc_set, 1)
            seq.link(dve.tensor_scalar(one_rf[:, :], rf_c[:, :], 1.0, None, ALU.add))
            seq.link(dve.tensor_reduce(bmask[:, :], ident[:, :].rearrange("p (h j) -> p j h", j=NB), AX, ALU.add))
            seq.link(dve.memset(cc[:, 0, 0, :, SUB:SUB + 1], 1.0))
            seq.link(dve.memset(cc[:, 0, 1, :, SUB + 1:SUB + 2], 1.0))
            full = [P, T, SUB + 2]
            for t in range(SUB):
                src, dst = cc[:, t % 2], cc[:, (t + 1) % 2]
                fd_, sd_, fg_, sg_ = (gu[:, k, :, t].unsqueeze(2).to_broadcast(full) for k in range(4))
                seq.link(dve.tensor_tensor(ca[:, 0], src[:, 0], fd_, ALU.mult))
                seq.link(dve.tensor_tensor(ca[:, 1], src[:, 1], sd_, ALU.mult))
                seq.link(dve.scalar_tensor_tensor(out=dst[:, 0], in0=ca[:, 1], scalar=rf_c[:, 0:1], in1=ca[:, 0], op0=ALU.mult, op1=ALU.add))
                seq.link(dve.scalar_tensor_tensor(out=dst[:, 1], in0=ca[:, 0], scalar=rf_c[:, 0:1], in1=ca[:, 1], op0=ALU.mult, op1=ALU.add))
                seq.link(dve.tensor_copy(dst[:, :, :, t], one_rf[:, 0:1].unsqueeze(2).to_broadcast([P, 2, T])))
                seq.link(dve.tensor_tensor(ca[:, 0], dst[:, 0], fg_, ALU.mult))
                seq.link(dve.tensor_tensor(ca[:, 1], dst[:, 1], sg_, ALU.mult))
                seq.link(dve.tensor_tensor(gl[:, :, :, t], ca[:, 0], ca[:, 1], ALU.add))
            last = cc[:, SUB % 2]
            for m in range(2):
                seq.link(dve.tensor_copy(pb[:, :, 2 * m:2 * m + 2], last[:, m, :, SUB:SUB + 2]))
            dve.tensor_copy(bmask[:, 0:1], bmask[:, 0:1]).then_inc(pb_set, 1)
            dve.wait_ge(pb_set, 1)
            dve.wait_ge(pball_in, 16 * H0)
            pv = pball[:, :].rearrange("p (j t q) -> p j t q", j=NB, q=4)
            wide = [P, T, SUB]
            seq.link(dve.memset(rb[:, 0:2, :, :], 0.0))
            for j in range(NB):
                for m in range(2):
                    out_ = rb[:, 2 * (j + 1) + m, :, :] if j < NB - 1 else cend[:, m]
                    r_ = last[:, m, :, 0:SUB]
                    if j == 0:
                        seq.link(dve.tensor_scalar(out_, r_, bmask[:, 0:1], None, ALU.mult))
                        continue
                    prev = [rb[:, 2 * j + k, :, :] for k in range(2)]
                    seq.link(dve.tensor_tensor(ca[:, 0, :, 0:SUB], prev[0], pv[:, j, :, 2 * m].unsqueeze(2).to_broadcast(wide), ALU.mult))
                    seq.link(dve.tensor_tensor(ca[:, 1, :, 0:SUB], prev[1], pv[:, j, :, 2 * m + 1].unsqueeze(2).to_broadcast(wide), ALU.mult))
                    seq.link(dve.tensor_tensor(ca[:, 0, :, 0:SUB], ca[:, 0, :, 0:SUB], ca[:, 1, :, 0:SUB], ALU.add))
                    seq.link(dve.scalar_tensor_tensor(out=out_, in0=r_, scalar=bmask[:, j:j + 1], in1=ca[:, 0, :, 0:SUB], op0=ALU.mult, op1=ALU.add))
            seq.link(dve.memset(before[:, NB - 1:NB], 0.0))
            for j in range(NB - 2, -1, -1):
                seq.link(dve.tensor_tensor(before[:, j:j + 1], before[:, j + 1:j + 2], bmask[:, j + 1:j + 2], ALU.add))
            for buf in (yp, pc):
                seq.link(dve.memset(buf[:, :, :], 0.0))
                seq.link(dve.memset(buf[:, :, 0:4:3], 1.0))
            q4 = [P, T, 2, 2]

            def times(buf, j):
                v = buf[:, :, :].rearrange("p t (i k) -> p t i k", k=2)
                pj_ = pv[:, j, :, :].rearrange("p t (i k) -> p t i k", k=2)
                for k in range(2):
                    seq.link(dve.tensor_tensor(y4[:, k], pj_[:, :, :, k:k + 1].to_broadcast(q4), v[:, :, k:k + 1, :].to_broadcast(q4), ALU.mult))
                return y4[:, 0].rearrange("p t i k -> p t (i k)"), y4[:, 1].rearrange("p t i k -> p t (i k)")
            for j in range(NB):
                y0, y1 = times(pc, j)
                seq.link(dve.tensor_tensor(pc[:, :, :], y0, y1, ALU.add))
                y0, y1 = times(yp, j)
                seq.link(dve.tensor_tensor(y0, y0, y1, ALU.add))
                seq.link(dve.tensor_tensor(y0, y0, yp[:, :, :], ALU.subtract))
                seq.link(dve.scalar_tensor_tensor(out=yp[:, :, :], in0=y0, scalar=before[:, j:j + 1], in1=yp[:, :, :], op0=ALU.mult, op1=ALU.add))
            for m in range(2):
                seq.link(dve.tensor_tensor(ca[:, 0, :, 0:SUB], gl[:, :, SUB, :], yp[:, :, m].unsqueeze(2).to_broadcast(wide), ALU.mult))
                seq.link(dve.tensor_tensor(ca[:, 1, :, 0:SUB], gl[:, :, SUB + 1, :], yp[:, :, 2 + m].unsqueeze(2).to_broadcast(wide), ALU.mult))
                seq.link(dve.tensor_tensor(gam[:, m], ca[:, 0, :, 0:SUB], ca[:, 1, :, 0:SUB], ALU.add))
            for m in range(2):
                seq.link(dve.tensor_tensor(lx[:, m, :, :, :], gl[:, :, SUB + m, :].unsqueeze(2).to_broadcast([P, T, NB, SUB]),
                                           bmask[:, :].unsqueeze(1).unsqueeze(3).to_broadcast([P, T, NB, SUB]), ALU.mult))
            dve.tensor_copy(one_rf[:, :], one_rf[:, :]).then_inc(gate_set, 1)
            end_phase(dve)
            dve.wait_ge(nb_in, 16)
            seq.link(dve.memset(tb[:, :, :, :], 0.0))
            seq.link(dve.memset(tb[:, :, :, :].rearrange("p t s o -> p t (s o)")[:, :, 0:SUB * SUB:SUB + 1], 1.0))
            nv = nb[:, :, :].rearrange("p t (s o) -> p t s o", o=SUB)
            for s in range(1, SUB):
                sh = [P, T, s, s]
                pr = iprod[:, 0:T * s * s].rearrange("p (t k j) -> p t k j", k=s, j=s)
                seq.link(dve.tensor_tensor(pr, nv[:, :, s, 0:s].unsqueeze(2).to_broadcast(sh), tb[:, :, 0:s, 0:s].rearrange("p t j k -> p t k j"), ALU.mult))
                seq.link(dve.tensor_reduce(tb[:, :, s, 0:s], pr, AX, ALU.add, negate=True))
            dve.tensor_copy(iprod[:, 0:1], iprod[:, 0:1]).then_inc(inv_set, 1)
            dve.tensor_copy(nv, tb[:, :, :, :].rearrange("p t s o -> p t o s")).then_inc(inv_set, 1)
            end_phase(dve)
            dve.wait_ge(pc_in, 32)
            dve.wait_ge(lm_set, 5 + 3 * LEVELS)
            ch = Count(dve, v_tile, per=2 * (1 + 4 * 7))
            with dve.Fori(0, B) as b:
                dve.wait_ge(s_new, b * (4 * TB))
                dve.memset(S_t[:, :, :], 0.0).then_inc(s_zero, 1)
                with dve.Fori(0, TB // 2) as c:
                    ch.start(b * (TB // 2) + c)
                    for n in range(2):
                        i = b * TB + c * 2 + n
                        if n == 0:
                            dve.wait_ge(s_zero, b + 1)
                        dve.wait_ge(s_new, 4 * i)
                        ch.link(dve.tensor_tensor(sqs[:, :], S_t[:, :, :].rearrange("p h v -> p (h v)"), S_t[:, :, :].rearrange("p h v -> p (h v)"), ALU.mult))
                        dve.tensor_reduce(sqr[:, :], sqs[:, :].rearrange("p (q v) -> p q v", v=DK), AX, ALU.add).then_inc(sq_set, 1)
                        dve.wait_ge(kq_turned, i + 1)
                        dve.tensor_copy(cf[:, :], bank[4][:, 0:64]).then_inc(cf_kept, 1)
                        dve.wait_ge(cf_kept, i + 1)
                        dve.tensor_tensor(cv[:, :, :, :], cf[:, 32:64].rearrange("p (m h) -> p m h", m=2).unsqueeze(3).to_broadcast([P, 2, H0, DK]),
                                          qkv_t[:, n, 2 * HD:3 * HD].rearrange("p (h v) -> p h v", v=DK).unsqueeze(1).to_broadcast([P, 2, H0, DK]),
                                          ALU.mult).then_inc(cv_set, 1)
                        for q in range(2):
                            pair = (2 * q, 2 * q + 1)

                            def at(g):
                                return 4 * i + g + 1

                            def ps4(k):
                                return bank[k].rearrange("p (h t) -> p h t", t=P)
                            for g in pair:
                                y = g % 2
                                dve.wait_ge(kq_mm, at(g))
                                dve.wait_ge(ss_set, at(g))
                                for e in range(2):
                                    last = dve.tensor_tensor(st_sb[:, y, e:4:2, :], bank[4 * y + e].rearrange("p (k w t) -> p k w t", w=2, t=P)[:, :, 1, :],
                                                             umask[:, :].unsqueeze(1).to_broadcast([P, 2, P]), ALU.mult)
                                last.then_inc(st_set, 1)
                                dve.wait_ge(g_mm2, at(g))
                                dve.tensor_tensor(gt_sb[:, y, :, :].rearrange("p (k e) t -> p e k t", e=2),
                                                  banks[:, 2048 * y + 1024:2048 * y + 2048].rearrange("p (e c) -> p e c", e=2)[:, :, 0:256]
                                                  .rearrange("p e (k t) -> p e k t", t=P),
                                                  blk[:, n, 2, 4 * g:4 * g + 4, :].rearrange("p (k e) t -> p e k t", e=2), ALU.add).then_inc(g_kept, 1)
                            for lv in range(LEVELS):
                                for g in pair:
                                    y = g % 2
                                    dve.wait_ge(x_mm[lv], at(g))
                                    dve.tensor_tensor(xs[:, y, :, :], ps4(4 * y + 3), lmask[:, lv, :].unsqueeze(1).to_broadcast([P, 4, P]), ALU.mult)\
                                        .then_inc(x_set[lv], 1)
                                for g in pair:
                                    y = g % 2
                                    old = blk[:, n, 0, 4 * g:4 * g + 4, :] if lv == 0 else tw[:, y, :, :]
                                    oldT = blk[:, n, 1, 4 * g:4 * g + 4, :] if lv == 0 else ttw[:, y, :, :]
                                    dve.wait_ge(u_mm[lv], at(g))
                                    dve.tensor_tensor(tw[:, y, :, :], old, ps4(4 * y), ALU.subtract).then_inc(tw_set[lv], 1)
                                    if lv < LEVELS - 1:
                                        dve.wait_ge(ut_mm[lv], at(g))
                                        dve.tensor_tensor(ttw[:, y, :, :], oldT, ps4(4 * y + 1), ALU.subtract).then_inc(ttw_set[lv], 1)
                            for g in pair:
                                y = g % 2
                                dve.wait_ge(z_mm, at(g))
                                st = S_t[:, 2 * g:2 * g + 2, :]
                                zz = bank[4 * y][:, 0:256].rearrange("p (q v) -> p q v", q=2)
                                ww = bank[4 * y][:, 256:512].rearrange("p (q m v) -> p q m v", q=2, m=2)
                                ch.link(dve.tensor_tensor(zs[:, y, :, :], st, zz, ALU.add))
                                sh = [P, 2, 2, DK]
                                pcv = pcb[:, :].rearrange("p (t h m k) -> p t h m k", t=T, h=8, m=2)[:, ds(i, 1), 2 * g:2 * g + 2, :, :]\
                                    .rearrange("p a h m k -> p (a h) m k")
                                zv = zs[:, y, :, :].rearrange("p q (k v) -> p q k v", k=2)
                                for k in range(2):
                                    ch.link(dve.tensor_tensor(za[:, y, k], zv[:, :, k:k + 1, :].to_broadcast(sh), pcv[:, :, :, k:k + 1].to_broadcast(sh), ALU.mult))
                                ch.link(dve.tensor_tensor(za[:, y, 0], za[:, y, 0], za[:, y, 1], ALU.add))
                                dve.wait_ge(qs_mm, at(g))
                                dve.tensor_tensor(st.rearrange("p q (m v) -> p q m v", m=2), za[:, y, 0], ww, ALU.add).then_inc(s_new, 1)
                                ov = o_sb[:, 256 * g:256 * g + 256].rearrange("p (h v) -> p h v", v=DK)
                                if g == 0:
                                    dve.wait_ge(o_kept, 16 * i)
                                for e in range(2):
                                    oq = bank[4 * y + 2 + e][:, 0:256].rearrange("p (h m v) -> p h m v", m=2, v=DK)
                                    gm_ = cf[:, 0:32].rearrange("p (m h) -> p h m", m=2)[:, 4 * g + e:4 * g + 4:2, :].unsqueeze(3).to_broadcast([P, 2, 2, DK])
                                    ch.link(dve.tensor_tensor(oa[:, y, e:4:2, :, :], oq, gm_, ALU.mult))
                                dve.wait_ge(av_mm, at(g))
                                ch.link(dve.tensor_tensor(ov, oa[:, y, :, 0, :], oa[:, y, :, 1, :], ALU.add))
                                dve.tensor_tensor(ov, ov, bank[4 * y + 1][:, 0:256].rearrange("p (h v) -> p h v", v=DK), ALU.add).then_inc(o_set, 1)
                            if q == 1:
                                dve.wait_ge(o_set, at(3))
                                dve.wait_ge(s_new, at(3))
                                dve.sem_inc(tile_free[n], 1)
                    ch.end()
            end_phase(dve)
            dve.wait_ge(bd_in, 16 * 5 * H0)
            dve.wait_ge(bn_root, 2)
            bdv = bd[:, 0:2, :, :]
            for t in range(P):
                sh = [P, 2, B]
                cur_ = bnx[:, :, :].rearrange("p b j -> p j b") if t == 0 else bh[:, (t - 1), :, :]
                seq.link(dve.tensor_tensor(bt[:, :, :], cur_, bdv[:, :, :, t], ALU.mult))
                seq.link(dve.tensor_tensor(bt[:, :, :], bt[:, :, :], bd[:, 2, :, t].unsqueeze(1).to_broadcast(sh), ALU.add))
                for j in range(2):
                    last = dve.scalar_tensor_tensor(out=bh[:, t, j, :], in0=bt[:, 1 - j, :], scalar=rf_abs[:, 0:1], in1=bt[:, j, :], op0=ALU.mult, op1=ALU.add)
                    seq.done(last)
                dve.wait_ge(v_seq, seq.base + seq.n)
            seq.link(dve.tensor_scalar(bh[:, :, :, :], bh[:, :, :, :], BOUND, None, ALU.is_le))
            dve.tensor_reduce(bmin[:, :], bh[:, :, :, :].rearrange("p t j b -> p (t j b)"), AX, ALU.min).then_inc(bmin_set, 1)
            dve.wait_ge(bt_mm, 1)
            seq.link(dve.tensor_reduce(bmin[0:1, :], bank[0][0:1, 0:P], AX, ALU.min))
            seq.link(dve.tensor_scalar(bmin[0:1, :], bmin[0:1, :], -1.0, 1.0, ALU.mult, ALU.add))
            dve.tensor_copy(capped_flag[:, :], bmin[0:1, :]).then_inc(flag_set, 1)
            end_phase(dve)

        def capped(eng):
            eng.wait_ge(flag_set, 1)
            flag = eng.value_load(capped_flag[0:1, 0:1], min_val=0, max_val=1)
            return eng.If(flag > 0)

        @block.sync
        def _(sp):
            xv = a["x"].rearrange("(t p) d -> p t d", p=P)
            for c in range(4):
                sp.dma_start(res[:, 8 * c:8 * c + 8, :], xv[:, 8 * c:8 * c + 8, :]).then_inc(ld, 16)
            sp.wait_ge(const_set, 1)
            for m, w in enumerate(("w_gate", "w_up")):
                for c in range(3):
                    rows = min(P, INNER - P * c)
                    sp.dma_start(wraw[0:rows, (3 * m + c) * P:(3 * m + c + 1) * P],
                                 a[w][P * c:P * c + rows, :]).then_inc(ld1, 16)
            sp.dma_start(wraw[:, 6 * P:NW], a["w_down"]).then_inc(ld1, 16)
            if stop == 1:
                sp.wait_ge(ffn_added, T)
                sp.dma_start(out.rearrange("(t p) d -> p t d", p=P), res[:, :, :]).then_inc(ld, 16)
                sp.wait_ge(ld, 80)
                return
            end_phase(sp)
            for n, w in enumerate(("Wq", "Wk", "Wv", "Wg")):
                sp.dma_start(wproj[:, HD * n:HD * n + HD], a[w]).then_inc(ld2, 16)
            sp.dma_start(bproj[:, :], a["bproj"]).then_inc(ld2, 16)
            sp.dma_start(wgate[:, :], a["wgate"]).then_inc(ld2, 16)
            sp.dma_start(bgate[:, 0:2], a["bgate"]).then_inc(ld2, 16)
            sp.wait_ge(g_done, 8)
            sp.dma_start(gates_s, gates[:, :]).then_inc(g_stored, 16)
            ps_v = proj_s.rearrange("(t p) n -> t p n", p=P)
            with sp.Fori(0, T) as i:
                sp.wait_ge(p_normed, 2 * i + 2)
                sp.wait_ge(p_silu, 8 * i + 8)
                sp.dma_start(ps_v[ds(i, 1), :, :].rearrange("a p n -> (a p) n"), prj[:, :]).then_inc(p_stored, 16)
            sp.wait_ge(vrow_root, 1)
            sp.dma_start(vnorm_s, vrow[:, :]).then_inc(g_stored, 16)
            sp.wait_ge(g_stored, 32)
            sp.wait_ge(p_stored, 16 * T)
            end_phase(sp)
            chunk_sync(sp)
            with capped(sp):
                sp.dma_start(rf_col[:, :], a["rf"].partition_broadcast(P)).then_inc(ld3, 16)
                for j in range(2):
                    for b in range(B):
                        p0 = j * B * H0 + b * H0
                        for buf, kind in ((gdec, 1 + j), (gout, 3 + j)):
                            sp.dma_start(buf[p0:p0 + H0, :], gates_s[kind * H0:kind * H0 + H0, b * L:b * L + L]).then_inc(ld3, 16)
                pv = proj_s.rearrange("(b t) (w h d) -> w b h t d", b=B, w=4, h=H0)
                with sp.Fori(0, L // (2 * STEPS)) as i:
                    for n in range(2):
                        sp.wait_ge(stepped[n], i)
                        for w in range(3):
                            for j in range(2):
                                for b in range(B):
                                    p0 = j * B * H0 + b * H0
                                    sp.dma_start(qkv[p0:p0 + H0, n, w, :, :], pv[w, b, :, ds(i * (2 * STEPS) + n * STEPS, STEPS), :])\
                                        .then_inc(qkv_in[n], 16)
            end_phase(sp)
            for c in range(8):
                sp.dma_start(wout[:, c, :], a["Wo"][P * c:P * c + P, :]).then_inc(ld4, 16)
            sp.dma_start(bout[:, :], a["bo"]).then_inc(ld4, 16)
            sp.dma_start(onw[:, :], a["onorm_w"].partition_broadcast(P)).then_inc(ld4, 16)
            mt = mem_s.rearrange("(t p) n -> t p n", p=P)
            with sp.Fori(0, T) as i:
                sp.wait_ge(og_set, i)
                sp.dma_start(om[:, 0, :], mt[ds(i, 1), :, :].rearrange("a p n -> (a p) n")).then_inc(om_in, 16)
                sp.dma_start(om[:, 2, :], ps_v[ds(i, 1), :, 3 * HD:4 * HD].rearrange("a p n -> (a p) n")).then_inc(om_in, 16)
            if stop == 2:
                sp.wait_ge(o_added, T)
                sp.dma_start(out.rearrange("(t p) d -> p t d", p=P), res[:, :, :]).then_inc(ld, 16)
                sp.wait_ge(ld, 80)
                return
            end_phase(sp)
            sp.wait_ge(cleared, len(again))
            sp.drain()
            sp.dma_start(wq1[:, :, :], a["W1q"]).then_inc(ld5, 16)
            sp.dma_start(wk1[:, :, :], a["W1k"]).then_inc(ld5, 16)
            sp.dma_start(wv1[:, :], a["W1v"]).then_inc(ld5, 16)
            sp.dma_start(wg1[:, :], a["Wg1"]).then_inc(ld5, 16)
            sp.dma_start(bg1[:, :], a["bg1"].partition_broadcast(P)).then_inc(ld5, 16)
            end_phase(sp)
            sp.dma_start(wp1[:, :], a["W1p"]).then_inc(ld6, 16)
            sp.dma_start(bp1[:, :], a["bp1"]).then_inc(ld6, 16)
            sp.dma_start(w1[:, :, :], a["W1"].rearrange("e p n -> p e n")).then_inc(ld6, 16)
            for e in range(E1):
                sp.dma_start(w2[:, e, :, :], a["W2"][e].rearrange("(c p) d -> p c d", p=P)).then_inc(ld6, 16)
            sp.dma_start(b1[:, :, :], a["b1"]).then_inc(ld6, 16)
            sp.dma_start(b2[:, :], a["b2"]).then_inc(ld6, 16)
            ov = out.rearrange("(t p) d -> p t d", p=P)
            with sp.Fori(0, T // 4) as i:
                sp.wait_ge(e_added, (i + 1) * (4 * E1))
                sp.dma_start(ov[:, ds(4 * i, 4), :], res[:, ds(4 * i, 4), :]).then_inc(out_stored, 16)
            sp.wait_ge(out_stored, 16 * (T // 4))

        @block.gpsimd
        def _(pool):
            pool.memset(wraw[:, :], 0.0).then_inc(const_set, 1)
            pool.memset(ident[:, :], 0.0).then_inc(const_set, 1)
            pool.memset(ones_row[:, :], 1.0).then_inc(const_set, 1)
            pool.wait_ge(const_set, 3)
            pool.affine_select(out=ident[:, :], in_=ident[:, :], compare_op=ALU.not_equal, fill=1.0, base=0,
                               pattern=[[-1, P]], channel_multiplier=1).then_inc(const_set, 1)
            pool.wait_ge(xq_done, 1)
            with pool.Fori(0, T) as i:
                pool.wait_ge(x_turned, i)
                pool.tensor_copy(st_n[:, :], tile(xn, i)).then_inc(staged, 1)
                pool.tensor_copy(st_q[:, :], tile(xq, i)).then_inc(staged, 1)
            if stop == 1:
                return
            end_phase(pool)
            pool.wait_ge(sb_root, 1)
            with pool.Fori(0, T) as i:
                pool.wait_ge(p_mm, 8 * i)
                pool.wait_ge(pb_turned, i)
                pool.tensor_copy(st_p[:, :], xnT[:, ds(i * P, P)]).then_inc(p_staged, 1)
                pool.tensor_copy(st_b[:, :], sbeta[:, ds(i * P, P)]).then_inc(p_staged, 1)
            end_phase(pool)
            chunk_pool(pool)
            with capped(pool):
                pool.memset(mix[:, :], 0.0).then_inc(swap_set, 1)
                for n, off in enumerate((64, -64)):
                    pool.wait_ge(swap_set, n + 1)
                    pool.affine_select(out=mix[:, :], in_=mix[:, :], compare_op=ALU.not_equal, fill=1.0, base=off,
                                       pattern=[[-1, P]], channel_multiplier=1).then_inc(swap_set, 1)
                mv = mem_s.rearrange("(b t) (h d) -> b h t d", b=B, h=H0)
                with pool.Fori(0, L // (2 * STEPS)) as i:
                    for n in range(2):
                        pool.wait_ge(stepped[n], i + 1)
                        for b in range(B):
                            pool.dma_start(mv[b, :, ds(i * (2 * STEPS) + n * STEPS, STEPS), :], obuf[b * H0:b * H0 + H0, n, :, :])\
                                .then_inc(o_stored[n], 16)
                for n in range(2):
                    pool.wait_ge(o_stored[n], L // (2 * STEPS) * 64)
            end_phase(pool)
            if stop == 2:
                return
            end_phase(pool)
            for x in again:
                pool.sem_clear(x).then_inc(cleared, 1)
            pool.wait_ge(cleared, len(again))
            pool.drain()
            pool.iota(number_i[:, :], pattern=[[1, E1]], base=0, channel_multiplier=0).then_inc(mask_set, 1)
            for m in (above, below):
                pool.memset(m[:, :], 0.0).then_inc(mask_set, 1)
            pool.memset(vaug[:, :, :, :], 1.0).then_inc(mask_set, 1)
            pool.memset(mxz[:, :, :], 0.0).then_inc(mask_set, 1)
            pool.wait_ge(mask_set, 5)
            for m, (cm, step) in ((above, (1, -1)), (below, (-1, 1))):
                pool.affine_select(out=m[:, :], in_=m[:, :], compare_op=ALU.is_ge, fill=MASKED, base=0,
                                   pattern=[[step, P]], channel_multiplier=cm).then_inc(mask_set, 1)
            pool.wait_ge(norm_done, 2)
            with pool.Fori(0, T) as i:
                pool.wait_ge(x1_turned, i)
                pool.tensor_copy(st_x[:, :], tile(xn1, i)).then_inc(x1_staged, 1)
            with pool.Fori(0, B) as b:
                with pool.Fori(0, 4) as r:
                    pool.wait_ge(pj_mm, b * 4 + r)
                    pool.tensor_copy(st_wq[:, :], tile(wq1, r)).then_inc(w_staged, 1)
                    pool.tensor_copy(st_wk[:, :], tile(wk1, r)).then_inc(w_staged, 1)
            end_phase(pool)
            with pool.Fori(0, T) as i:
                pool.wait_ge(o1_turned, i)
                pool.tensor_copy(st_o[:, :], tile(o_all, i)).then_inc(o_staged, 1)
            with pool.Fori(0, T // 4) as i:
                pool.wait_ge(e_added, i * (4 * E1))
                pool.tensor_copy(st_r[:, :], route[:, ds(4 * i, 4), :].rearrange("p t e -> p (t e)")).then_inc(r_staged, 1)

        @block.tensor
        def _(pe):
            pe.wait_ge(const_set, 4)
            pe.wait_ge(wq_done, 1)
            for n in range(6):
                pe.transpose(bank[n // 3][:, P * (n % 3):P * (n % 3 + 1)], wqt[:, P * n:P * (n + 1)], ident[:, :])
            for c in range(3):
                w = min(P, INNER - P * c)
                last = pe.transpose(bank[2][0:w, P * c:P * (c + 1)], wqt[:, 6 * P + P * c:6 * P + P * c + w], ident[:, :])
            last.then_inc(wt_done, 1)
            pe.wait_ge(wT_done, 3)
            with pe.Fori(0, T) as i:
                pe.wait_ge(staged, 2 * i + 2)
                pe.transpose(bank[0][:, 0:P], st_n[:, :], ident[:, :])
                pe.transpose(bank[0][:, P:2 * P], st_q[:, :], ident[:, :]).then_inc(x_turned, 1)
                pe.wait_ge(xT_done, 2 * i + 2)
                pe.wait_ge(hid_done, i)
                pe.matmul(bank[1][:, 0:INNER], xqT[:, :], wguT[:, 0, 0:INNER], start=True, stop=True)
                pe.matmul(bank[2][:, 0:INNER], xqT[:, :], wguT[:, 1, 0:INNER], start=True, stop=True).then_inc(gu_done, 1)
                pe.wait_ge(hq_done, i + 1)
                for c in range(3):
                    w = min(P, INNER - P * c)
                    last = pe.transpose(bank[3][0:w, P * c:P * (c + 1)], hq[:, P * c:P * c + w], ident[:, :])
                last.then_inc(h_turned, 1)
                pe.wait_ge(hT_done, 2 * i + 2)
                pe.wait_ge(ffn_added, i)
                for c in range(3):
                    w = min(P, INNER - P * c)
                    last = pe.matmul(bank[4][:, 0:D], hqT[0:w, c, :], wdT[0:w, c, :], start=(c == 0), stop=(c == 2))
                last.then_inc(down_done, 1)
            if stop == 1:
                return
            end_phase(pe)
            pe.wait_ge(ld2, 112)
            for n in range(8):
                pe.matmul(bank[n][0:5 * H0, :], wgate[:, :], xnT[:, 512 * n:512 * n + 512], start=True, stop=True).then_inc(g_mm, 1)
            pe.wait_ge(g_done, 8)
            with pe.Fori(0, T) as i:
                pe.wait_ge(p_staged, 2 * i + 2)
                pe.wait_ge(p_silu, 8 * i)
                pe.wait_ge(sbt_set, i)
                pe.wait_ge(vrow_set, i)
                for n in range(8):
                    pe.matmul(bank[n], st_p[:, :], wproj[:, 512 * n:512 * n + 512], start=True, stop=False)
                    pe.matmul(bank[n], ones_row[:, :], bproj[:, 512 * n:512 * n + 512], start=False, stop=True).then_inc(p_mm, 1)
                pe.wait_ge(p_silu, 8 * i + 2)
                pe.matmul(bank[0][:, 0:H0], st_b[:, :], ident[0:H0, 0:H0], start=True, stop=True).then_inc(pb_turned, 1)
                pe.wait_ge(vv_set, i + 1)
                pe.transpose(bank[1][0:H0, 0:P], vv[:, :], ident[:, :]).then_inc(vv_turned, 1)
            end_phase(pe)
            chunk_pe(pe)
            with capped(pe):
                pe.wait_ge(r_ready, 1)
                with pe.Fori(0, L // (2 * STEPS)) as i:
                    for s in range(2 * STEPS):
                        pe.wait_ge(updated, 2 * STEPS * i + s + 1)
                        for n in range(8):
                            last = pe.matmul(bank[n], mix[:, :], Snew[:, 512 * n:512 * n + 512], start=True, stop=True)
                        last.then_inc(mixed, 1)
                        if s % STEPS == STEPS - 1:
                            n = s // STEPS
                            pe.wait_ge(answered, 2 * i + n + 1)
                            pe.matmul(bank[0][0:B * H0, 0:STEPS * DK], pair_sum[:, :], ohalf[:, :, :].rearrange("p k d -> p (k d)"),
                                      start=True, stop=True).then_inc(summed, 1)
            end_phase(pe)
            pe.wait_ge(ld4, 160)
            with pe.Fori(0, T) as i:
                pe.wait_ge(og_set, i + 1)
                for c in range(8):
                    last = pe.transpose(bank[c // 4][:, P * (c % 4):P * (c % 4) + P], og[:, P * c:P * c + P], ident[:, :])
                last.then_inc(og_turned, 1)
                pe.wait_ge(ogT_set, 2 * i + 2)
                pe.wait_ge(o_added, i)
                for c in range(8):
                    pe.matmul(bank[2][:, 0:D], ogT[:, c, :], wout[:, c, :], start=(c == 0), stop=False)
                pe.matmul(bank[2][:, 0:D], ones_row[:, :], bout[:, :], start=False, stop=True).then_inc(o_mm, 1)
            if stop == 2:
                return
            end_phase(pe)
            pe.wait_ge(cleared, len(again))
            pe.drain()
            pe.wait_ge(ld5, 80)
            with pe.Fori(0, T) as i:
                pe.wait_ge(x1_staged, i + 1)
                pe.wait_ge(x1T_set, 2 * i)
                pe.transpose(bank[0][:, 0:P], st_x[:, :], ident[:, :]).then_inc(x1_turned, 1)
                pe.wait_ge(x1T_set, 2 * i + 2)
                pe.wait_ge(v_set, 2 * i)
                pe.matmul(bank[1][:, 0:D], xt_x[:, :], wv1[:, :], start=True, stop=True)
                pe.matmul(bank[2][:, 0:E1], xt_x[:, :], wg1[:, :], start=True, stop=True).then_inc(v_mm, 1)
            pe.wait_ge(c_set, 2)
            pe.wait_ge(v_set, 2 * T)
            with pe.Fori(0, B) as b:
                with pe.Fori(0, 4) as r:
                    i = b * 4 + r
                    pe.wait_ge(w_staged, 2 * i + 2)
                    pe.wait_ge(o_norm, 4 * i)
                    for n in range(2):
                        pe.matmul(bank[4 + n], st_wq[:, :], xnT1[:, ds(b * L + 512 * n, 512)], start=True, stop=True)
                    for n in range(2):
                        last = pe.matmul(bank[6 + n], st_wk[:, :], xnT1[:, ds(b * L + 512 * n, 512)], start=True, stop=True)
                    last.then_inc(pj_mm, 1)
                    pe.wait_ge(qk_set, 2 * i + 2)
                    pe.wait_ge(exp_done, 32 * i)
                    for u in range(32):
                        g, t = u // TB, u % TB
                        rows = slice(32 * g, 32 * g + 32)
                        if u >= 2:
                            pe.wait_ge(mx_read, 32 * i + u - 1)
                        for n in range((t + 4) // 4):
                            w = min(512, (t + 1) * P - 512 * n)
                            pe.matmul(bank[2 * (u % 2) + n][:, 0:w], qpad[rows, t * P:t * P + P], kaug[rows, 512 * n:512 * n + w],
                                      start=True, stop=(n != t // 4))
                        pe.matmul(bank[2 * (u % 2) + t // 4][:, P * (t % 4):P * (t % 4) + P], ident_b[:, :], above[:, :],
                                  start=False, stop=True).then_inc(a_mm, 1)
                    pe.wait_ge(mx_read, 32 * i + 32)
                    for t in range(TB):
                        last = pe.matmul(bank[4 + t // 4][:, P * (t % 4):P * (t % 4) + P], mxz[:, t, :], ident[:, :], start=True, stop=True)
                    last.then_inc(mx_turned, 1)
                    pe.wait_ge(qaug_set, i + 1)

                    def values(g):
                        pe.wait_ge(exp_done, 32 * i + 8 * g + 8)
                        if g >= 2:
                            pe.wait_ge(o_norm, 4 * i + g - 1)
                        for t in range(TB):
                            for j in range(t + 1):
                                at = sum(TB - x for x in range(j)) * P + (t - j) * P
                                last = pe.matmul(bank[6 + g % 2][:, SLOT * t:SLOT * t + SLOT], probs[:, g % 2, at:at + P],
                                                 vaug[:, ds(b * TB + j, 1), ds(r * 4 + g, 1), :].rearrange("p a h d -> p (a h d)"),
                                                 start=(j == 0), stop=(j == t))
                        last.then_inc(c_mm, 1)

                    for g in range(4):
                        rows = slice(32 * g, 32 * g + 32)
                        for j in range(TB):
                            u = 8 * g + j
                            if u >= 2:
                                pe.wait_ge(exp_done, 32 * i + u - 1)
                            wide = L - P * j
                            for n in range((wide + 511) // 512):
                                w = min(512, wide - 512 * n)
                                last = pe.matmul(bank[2 * (u % 2) + n][:, 0:w], kaug[rows, P * j:P * j + P],
                                                 qaug[rows, P * j + 512 * n:P * j + 512 * n + w], start=True, stop=(n > 0))
                                if n == 0:
                                    last = pe.matmul(bank[2 * (u % 2)][:, 0:P], ident_b[:, :], below[:, :], start=False, stop=True)
                            last.then_inc(b_mm, 1)
                        if g:
                            values(g - 1)
                    values(3)
            end_phase(pe)
            pe.wait_ge(ld6, 16 * 13)
            with pe.Fori(0, T) as i:
                pe.wait_ge(o_staged, i + 1)
                pe.wait_ge(o1T_set, i)
                pe.transpose(bank[0][:, 0:P], st_o[:, :], ident[:, :]).then_inc(o1_turned, 1)
                pe.wait_ge(o1T_set, i + 1)
                pe.wait_ge(pr_added, i)
                pe.matmul(bank[1][:, 0:D], oT1[:, :], wp1[:, :], start=True, stop=False)
                pe.matmul(bank[1][:, 0:D], ones_row[:, :], bp1[:, :], start=False, stop=True).then_inc(pr_mm, 1)
            pe.wait_ge(pr_added, T)
            with pe.Fori(0, T // 4) as i:
                pe.wait_ge(r_staged, i + 1)
                for t in range(4):
                    last = pe.transpose(bank[6][0:E1, P * t:P * t + P], st_r[:, E1 * t:E1 * t + E1], ident[:, :])
                last.then_inc(r_turned, 1)
                pe.wait_ge(rT_set, i + 1)
                for t in range(4):
                    last = pe.matmul(bank[7][:, P * t:P * t + P], rT[:, P * t:P * t + P], b2[:, :], start=True, stop=True)
                last.then_inc(rb_mm, 1)

                def second(e):
                    pe.wait_ge(h_silu, 4 * E1 * i + 4 * e + 4)
                    if e >= 2:
                        pe.wait_ge(e_added, 4 * E1 * i + 4 * (e - 1))
                    for t in range(4):
                        for c in range(4):
                            last = pe.matmul(bank[4 + e % 2][:, P * t:P * t + P], hT1[:, e % 2, c, P * t:P * t + P], w2[:, e, c, :],
                                             start=(c == 0), stop=(c == 3))
                    last.then_inc(e_mm, 1)

                for e in range(E1):
                    for c in range(4):
                        if e or c:
                            pe.wait_ge(h_silu, 4 * E1 * i + max(4 * e + c - 3, 0))
                        pe.matmul(bank[c], w1[:, e, P * c:P * c + P], xnT1[:, ds(i * 512, 512)], start=True, stop=True).then_inc(h_mm, 1)
                    if e:
                        second(e - 1)
                second(E1 - 1)

        @block.scalar
        def _(act):
            act.wait_ge(var_done, 1)
            act.activation(stats[:, 0, :], stats[:, 1, :], ACT.Sqrt).then_inc(std_done, 1)
            act.wait_ge(norm_done, 1)
            act.activation(fa[:, :], xn[:, :, :].rearrange("p t d -> p (t d)"), ACT.Abs).then_inc(sign_done, 1)
            act.activation(fsg[:, :], xn[:, :, :].rearrange("p t d -> p (t d)"), ACT.Sign).then_inc(sign_done, 1)
            act.wait_ge(wt_done, 1)
            act.wait_ge(ld1, 112)
            for m in range(2):
                act.copy(wguT[:, m, :], bank[m][:, 0:3 * P]).then_inc(wT_done, 1)
            act.copy(wdT[:, 0:2, :], bank[2][:, 0:2 * P].rearrange("p (c d) -> p c d", c=2))
            act.copy(wdT[0:INNER - 2 * P, 2, :], bank[2][0:INNER - 2 * P, 2 * P:3 * P]).then_inc(wT_done, 1)
            with act.Fori(0, T) as i:
                act.wait_ge(x_turned, i + 1)
                act.copy(xnT[:, ds(i * P, P)], bank[0][:, 0:P]).then_inc(xT_done, 1)
                act.wait_ge(gu_done, i)
                act.copy(xqT[:, :], bank[0][:, P:2 * P]).then_inc(xT_done, 1)
                act.wait_ge(gu_done, i + 1)
                act.activation(silu_g[:, :], bank[1][:, 0:INNER], ACT.Silu).then_inc(silu_done, 1)
                act.wait_ge(hid_done, i + 1)
                act.activation(fa[:, 0:INNER], hid[:, :], ACT.Abs).then_inc(hsign_done, 1)
                act.activation(fsg[:, 0:INNER], hid[:, :], ACT.Sign).then_inc(hsign_done, 1)
                act.wait_ge(h_turned, i + 1)
                act.copy(hqT[:, 0:2, :], bank[3][:, 0:2 * P].rearrange("p (c d) -> p c d", c=2)).then_inc(hT_done, 1)
                act.copy(hqT[0:INNER - 2 * P, 2, :], bank[3][0:INNER - 2 * P, 2 * P:3 * P]).then_inc(hT_done, 1)
            if stop == 1:
                return
            end_phase(act)
            act.wait_ge(g_bias, 1)
            for n in range(8):
                act.wait_ge(g_mm, n + 1)
                act.activation(gates[:, 512 * n:512 * n + 512], bank[n][0:5 * H0, :], ACT.Sigmoid, bias=bgate[:, 2:3]).then_inc(g_done, 1)
            act.wait_ge(g_done, 8)
            act.activation(sbeta[:, :], gates[0:H0, :], ACT.Sqrt).then_inc(sb_root, 1)
            with act.Fori(0, T) as i:
                act.wait_ge(p_stored, 16 * i)
                for n in range(8):
                    act.wait_ge(p_mm, 8 * i + n + 1)
                    act.activation(prj[:, 512 * n:512 * n + 512], bank[n], ACT.Silu).then_inc(p_silu, 1)
                act.wait_ge(p_var, i + 1)
                act.activation(prj_n[:, 1, :], prj_n[:, 0, :], ACT.Sqrt).then_inc(p_std, 1)
                act.wait_ge(vv_turned, i + 1)
                act.copy(vrow[:, ds(i * P, P)], bank[1][0:H0, 0:P]).then_inc(vrow_set, 1)
            act.wait_ge(vrow_set, T)
            act.activation(vrow[:, :], vrow[:, :], ACT.Sqrt).then_inc(vrow_root, 1)
            end_phase(act)
            chunk_act(act)
            with capped(act):
                with act.Fori(0, L // (2 * STEPS)) as i:
                    for s in range(2 * STEPS):
                        at = 2 * STEPS * i + s + 1
                        act.wait_ge(mixed, at)
                        act.activation(junk[:, :], banks[:, :], ACT.Square, accum_out=cap[:, 0:1]).then_inc(squared, 1)
                        act.wait_ge(ratio_set, at)
                        act.activation(cap[:, 2:3], cap[:, 1:2], ACT.Sqrt).then_inc(ratio_root, 1)
                        act.wait_ge(lam_set, at)
                        act.activation(S[:, :, :].rearrange("p k v -> p (k v)"), banks[:, :], ACT.Copy, scale=cap[:, 5:6]).then_inc(state_set, 1)
            end_phase(act)
            with act.Fori(0, T) as i:
                act.wait_ge(o_var, i + 1)
                act.activation(orn[:, :], orn[:, :], ACT.Sqrt).then_inc(o_std, 1)
                act.wait_ge(og_turned, i + 1)
                for n in range(2):
                    act.copy(ogT[:, 4 * n:4 * n + 4, :].rearrange("p c d -> p (c d)"), bank[n]).then_inc(ogT_set, 1)
            if stop == 2:
                return
            end_phase(act)
            act.wait_ge(cleared, len(again))
            act.drain()
            act.wait_ge(var_done, 2)
            act.activation(stats[:, 0, :], stats[:, 1, :], ACT.Sqrt).then_inc(std_done, 1)
            act.wait_ge(norm_done, 2)
            act.activation(route[:, 0:1, :], stats[:, 0:1, 0:E1], ACT.Exp)
            with act.Fori(0, T) as i:
                act.wait_ge(x1_turned, i + 1)
                act.copy(xnT1[:, ds(i * P, P)], bank[0][:, 0:P]).then_inc(x1T_set, 1)
                act.wait_ge(v_mm, i)
                act.copy(xt_x[:, :], bank[0][:, 0:P]).then_inc(x1T_set, 1)
            act.wait_ge(r_ready1, 1)
            act.activation(rt[:, 1, :, :], rt[:, 0, :, :], ACT.Exp).then_inc(r_exp, 1)
            with act.Fori(0, B) as b:
                with act.Fori(0, 4) as r:
                    i = b * 4 + r
                    for u in range(32):
                        g, j = u // TB, u % TB
                        if j == 0:
                            act.wait_ge(c_mm, 4 * i + max(g - 1, 0))
                        act.wait_ge(b_mm, 32 * i + u + 1)
                        at, w = sum(TB - x for x in range(j)) * P, L - P * j
                        act.activation(probs[:, g % 2, at:at + w], banks[:, 1024 * (u % 2):1024 * (u % 2) + w], ACT.Exp,
                                       scale=D1 ** -0.5).then_inc(exp_done, 1)
            end_phase(act)
            with act.Fori(0, T) as i:
                act.wait_ge(o1_turned, i + 1)
                act.wait_ge(pr_mm, i)
                act.copy(oT1[:, :], bank[0][:, 0:P]).then_inc(o1T_set, 1)
            act.wait_ge(ld6, 16 * 13)
            with act.Fori(0, T // 4) as i:
                act.wait_ge(r_turned, i + 1)
                act.copy(rT[:, :], bank[6][0:E1, :]).then_inc(rT_set, 1)
                for e in range(E1):
                    act.wait_ge(e_mm, i * E1 + max(e - 1, 0))
                    for c in range(4):
                        act.wait_ge(h_mm, 4 * E1 * i + 4 * e + c + 1)
                        act.activation(hT1[:, e % 2, c, :], bank[c], ACT.Silu, bias=b1[:, e, c:c + 1]).then_inc(h_silu, 1)

        @block.vector
        def _(dve):
            seq = Count(dve, v_seq)
            dve.wait_ge(ld, 64)
            layernorm(dve, seq, res, xn, xnT, 0)
            dve.tensor_copy(stats[:, 3, 0:1], stats[:, 2, 0:1]).then_inc(norm_done, 1)
            xf = xn[:, :, :].rearrange("p t d -> p (t d)")
            quantize(dve, seq, xf, T * D // BLOCK, fa[:, :], fc[:, :], fsg[:, :], fsc,
                     xq[:, :, :].rearrange("p t d -> p (t d)"),
                     lambda: dve.wait_ge(sign_done, 2)).then_inc(xq_done, 1)
            dve.wait_ge(ld1, 112)
            dve.wait_ge(xq_done, 1)
            wneg = fa[:, NW:2 * NW]
            seq.link(dve.tensor_scalar(wneg, wraw[:, :], 0.0, None, ALU.is_lt))
            seq.link(dve.scalar_tensor_tensor(out=fsg[:, 0:NW], in0=wraw[:, :], scalar=0.0, in1=wneg,
                                              op0=ALU.is_gt, op1=ALU.subtract))
            seq.link(dve.tensor_tensor(fa[:, 0:NW], wraw[:, :], fsg[:, 0:NW], ALU.mult))
            quantize(dve, seq, wraw[:, :], NW // BLOCK, fa[:, 0:NW], fc[:, 0:NW], fsg[:, 0:NW], fsc,
                     wqt[:, :], lambda: None).then_inc(wq_done, 1)
            dve.wait_ge(wq_done, 1)
            ffn = Count(dve, v_ffn, per=13)
            with dve.Fori(0, T) as i:
                ffn.start(i)
                dve.wait_ge(silu_done, i + 1)
                dve.tensor_tensor(hid[:, :], silu_g[:, :], bank[2][:, 0:INNER], ALU.mult).then_inc(hid_done, 1)
                dve.wait_ge(hid_done, i + 1)
                dve.wait_ge(h_turned, i)
                quantize(dve, ffn, hid[:, :], INNER // BLOCK, fa[:, 0:INNER], fc[:, 0:INNER], fsg[:, 0:INNER],
                         fsc, hq[:, :], lambda: dve.wait_ge(hsign_done, 2 * i + 2)).then_inc(hq_done, 1)
                ffn.end()
                dve.wait_ge(down_done, i + 1)
                dve.tensor_tensor(tile(res, i), tile(res, i), bank[4][:, 0:D], ALU.add).then_inc(ffn_added, 1)
            if stop == 1:
                return
            end_phase(dve)
            dve.wait_ge(ld2, 112)
            dve.tensor_tensor(bgate[:, 2:3], bgate[:, 0:1], bgate[:, 1:2], ALU.add).then_inc(g_bias, 1)
            prc = Count(dve, v_prj, per=6)
            with dve.Fori(0, T) as i:
                prc.start(i)
                dve.wait_ge(p_silu, 8 * i + 4)
                qk = prj[:, 0:2 * HD].rearrange("p (h d) -> p h d", d=DK)
                qk_sq = prj_sq[:, :].rearrange("p (h d) -> p h d", d=DK)
                prc.link(dve.tensor_tensor(qk_sq, qk, qk, ALU.mult))
                prc.link(dve.tensor_reduce(prj_n[:, 0, :], qk_sq, AX, ALU.add))
                dve.tensor_scalar(prj_n[:, 0, :], prj_n[:, 0, :], 1e-6, None, ALU.add).then_inc(p_var, 1)
                dve.wait_ge(p_std, i + 1)
                prc.link(dve.reciprocal(prj_n[:, 0, :], prj_n[:, 1, :]))
                dve.wait_ge(pb_turned, i + 1)
                dve.tensor_copy(sb_tok[:, :], bank[0][:, 0:H0]).then_inc(sbt_set, 1)
                dve.wait_ge(sbt_set, i + 1)
                prc.link(dve.tensor_tensor(prj_n[:, 0, H0:2 * H0], prj_n[:, 0, H0:2 * H0], sb_tok[:, :], ALU.mult))
                dve.wait_ge(p_silu, 8 * i + 6)
                val = prj[:, 2 * HD:3 * HD].rearrange("p (h d) -> p h d", d=DK)
                dve.tensor_tensor(val, val, sb_tok[:, :].unsqueeze(2).to_broadcast([P, H0, DK]), ALU.mult).then_inc(p_normed, 1)
                dve.wait_ge(p_normed, 2 * i + 1)
                prc.link(dve.tensor_tensor(qk_sq[:, 0:H0, :], val, val, ALU.mult))
                prc.link(dve.tensor_reduce(vv[:, :], qk_sq[:, 0:H0, :], AX, ALU.add))
                dve.wait_ge(vv_turned, i) if False else None
                dve.tensor_copy(prj_n[:, 1, 0:1], prj_n[:, 0, 0:1]).then_inc(vv_set, 1)
                prc.end()
                dve.tensor_tensor(qk, qk, prj_n[:, 0, :].unsqueeze(2).to_broadcast([P, 2 * H0, DK]), ALU.mult).then_inc(p_normed, 1)
            end_phase(dve)
            chunk_dve(dve, seq)
            with capped(dve):
                pre = Count(dve, v_pre)
                dve.wait_ge(ld3, 16 * 17)
                dve.wait_ge(swap_set, 3)
                pre.link(dve.tensor_tensor(pair_sum[:, :], ident[:, 0:B * H0], ident[:, B * H0:P], ALU.add))
                pre.link(dve.scalar_tensor_tensor(out=mix[:, :], in0=mix[:, :], scalar=rf_col[:, 0:1], in1=ident[:, :], op0=ALU.mult, op1=ALU.add))
                pre.link(dve.memset(S[:, :, :], 0.0))
                dve.tensor_scalar(gndec[:, :], gdec[:, :], -1.0, None, ALU.mult).then_inc(r_ready, 1)
                dve.wait_ge(r_ready, 1)
                PER = 3 + 2 * STEPS * 9
                rec = Count(dve, v_rec, per=PER)
                with dve.Fori(0, L // (2 * STEPS)) as i:
                    rec.start(i)
                    for n, g in enumerate((gdec, gndec, gout)):
                        rec.link(dve.tensor_copy(gcur[:, n, :], g[:, ds(i * (2 * STEPS), 2 * STEPS)]))
                    for s in range(2 * STEPS):
                        n, k = s // STEPS, s % STEPS
                        at = 2 * STEPS * i + s + 1
                        q_, k_, v_ = (qkv[:, n, w, k, :] for w in range(3))
                        if k == 0:
                            dve.wait_ge(qkv_in[n], 16 * 24 * (i + 1))
                            dve.wait_ge(o_stored[n], 64 * i)
                        if s:
                            dve.wait_ge(state_set, at - 1)
                        rec.link(dve.tensor_tensor(prod[:, :, :], S[:, :, :], k_.unsqueeze(2).to_broadcast([P, DK, DK]), ALU.mult))
                        rec.link(dve.tensor_reduce(small[:, 0, :], prod[:, :, :].rearrange("p k v -> p v k"), AX, ALU.add))
                        rec.link(dve.scalar_tensor_tensor(out=small[:, 1, :], in0=small[:, 0, :], scalar=gcur[:, 1, s:s + 1], in1=v_, op0=ALU.mult, op1=ALU.add))
                        rec.link(dve.tensor_tensor(outer[:, :, :], k_.unsqueeze(2).to_broadcast([P, DK, DK]),
                                                   small[:, 1, :].unsqueeze(1).to_broadcast([P, DK, DK]), ALU.mult))
                        dve.scalar_tensor_tensor(out=Snew[:, :], in0=S[:, :, :].rearrange("p k v -> p (k v)"), scalar=gcur[:, 0, s:s + 1],
                                                 in1=outer[:, :, :].rearrange("p k v -> p (k v)"), op0=ALU.mult, op1=ALU.add).then_inc(updated, 1)
                        dve.wait_ge(squared, at)
                        dve.tensor_scalar(cap[:, 1:2], cap[:, 0:1], 1.0 / (DK * DK), 1.0, ALU.mult, ALU.max).then_inc(ratio_set, 1)
                        rec.link(dve.tensor_scalar(cap[:, 3:4], cap[:, 0:1], float(DK * DK), None, ALU.is_gt))
                        dve.wait_ge(ratio_root, at)
                        rec.link(dve.reciprocal(cap[:, 4:5], cap[:, 2:3]))
                        rec.link(dve.scalar_tensor_tensor(out=cap[:, 4:5], in0=cap[:, 4:5], scalar=-1.0, in1=cap[:, 3:4], op0=ALU.add, op1=ALU.mult))
                        dve.tensor_scalar(cap[:, 5:6], cap[:, 4:5], 1.0, None, ALU.add).then_inc(lam_set, 1)
                        dve.wait_ge(state_set, at)
                        rec.link(dve.tensor_tensor(prod[:, :, :], S[:, :, :], q_.unsqueeze(2).to_broadcast([P, DK, DK]), ALU.mult))
                        rec.link(dve.tensor_reduce(small[:, 0, :], prod[:, :, :].rearrange("p k v -> p v k"), AX, ALU.add))
                        last = dve.tensor_scalar(ohalf[:, k, :], small[:, 0, :], gcur[:, 2, s:s + 1], None, ALU.mult)
                        if k == STEPS - 1:
                            last.then_inc(answered, 1)
                            dve.wait_ge(summed, 2 * i + n + 1)
                            dve.tensor_copy(obuf[:, n, :, :].rearrange("p k d -> p (k d)"), bank[0][0:B * H0, 0:STEPS * DK]).then_inc(stepped[n], 1)
                    rec.end()
            end_phase(dve)
            oc = Count(dve, v_out, per=5)
            dve.wait_ge(ld4, 160)
            with dve.Fori(0, T) as i:
                oc.start(i)
                dve.wait_ge(om_in, 32 * (i + 1))
                o_h = om[:, 0, :].rearrange("p (h d) -> p h d", d=DK)
                oc.link(dve.tensor_tensor(osq[:, :], om[:, 0, :], om[:, 0, :], ALU.mult))
                oc.link(dve.tensor_reduce(orn[:, :], osq[:, :].rearrange("p (h d) -> p h d", d=DK), AX, ALU.add))
                dve.tensor_scalar(orn[:, :], orn[:, :], 1.0 / DK, 1e-5, ALU.mult, ALU.add).then_inc(o_var, 1)
                dve.wait_ge(o_std, i + 1)
                oc.link(dve.reciprocal(orn[:, :], orn[:, :]))
                oc.link(dve.tensor_tensor(o_h, o_h, orn[:, :].unsqueeze(2).to_broadcast([P, H0, DK]), ALU.mult))
                oc.link(dve.tensor_tensor(o_h, o_h, onw[:, :].unsqueeze(1).to_broadcast([P, H0, DK]), ALU.mult))
                oc.end()
                dve.wait_ge(og_turned, i)
                dve.tensor_tensor(og[:, :], om[:, 0, :], om[:, 2, :], ALU.mult).then_inc(og_set, 1)
                dve.wait_ge(o_mm, i + 1)
                dve.tensor_tensor(tile(res, i), tile(res, i), bank[2][:, 0:D], ALU.add).then_inc(o_added, 1)
            if stop == 2:
                return
            end_phase(dve)
            dve.wait_ge(cleared, len(again))
            dve.drain()
            layernorm(dve, seq, res, xn1, xnT1, 1)
            dve.tensor_copy(stats[:, 3, 0:1], stats[:, 2, 0:1]).then_inc(norm_done, 1)
            dve.wait_ge(mask_set, 7)
            dve.tensor_copy(ident_b[:, :], ident[:, :]).then_inc(c_set, 1)
            dve.tensor_reduce(row_one[:, :], ident[:, 0:P:32], AX, ALU.add).then_inc(c_set, 1)
            seq.link(dve.tensor_copy(number[:, :], number_i[:, :]))
            dve.wait_ge(ld5, 80)
            with dve.Fori(0, T) as i:
                dve.wait_ge(v_mm, i + 1)
                dve.tensor_copy(vaug[:, ds(i, 1), :, 0:D1].rearrange("p a h d -> p (a h) d"),
                                bank[1][:, 0:D].rearrange("p (h d) -> p h d", d=D1)).then_inc(v_set, 1)
                dve.tensor_tensor(tile(logit, i), bank[2][:, 0:E1], bg1[:, :], ALU.add).then_inc(v_set, 1)
            dve.wait_ge(v_set, 2 * T)
            wide = [P, T, E1]
            top = rs[:, 0, :]
            seq.link(dve.tensor_reduce(top, logit[:, :, :], AX, ALU.max))
            dve.tensor_tensor(rt[:, 0, :, :], logit[:, :, :], top.unsqueeze(2).to_broadcast(wide), ALU.subtract).then_inc(r_ready1, 1)
            dve.wait_ge(r_exp, 1)
            share = rt[:, 1, :, :]
            seq.link(dve.tensor_reduce(rs[:, 1, :], share, AX, ALU.add))
            seq.link(dve.reciprocal(rs[:, 0, :], rs[:, 1, :]))
            seq.link(dve.tensor_tensor(share, share, rs[:, 0, :].unsqueeze(2).to_broadcast(wide), ALU.mult))
            seq.link(dve.tensor_reduce(top, share, AX, ALU.max))
            best, cand = rt[:, 0, :, :], rt[:, 2, :, :]
            numbers = number[:, :].unsqueeze(1).to_broadcast(wide)
            seq.link(dve.tensor_tensor(best, share, top.unsqueeze(2).to_broadcast(wide), ALU.is_ge))
            seq.link(dve.scalar_tensor_tensor(out=cand, in0=numbers, scalar=-float(E1), in1=best, op0=ALU.add, op1=ALU.mult))
            seq.link(dve.tensor_reduce(rs[:, 1, :], cand, AX, ALU.min))
            seq.link(dve.scalar_tensor_tensor(out=best, in0=numbers, scalar=-float(E1), in1=rs[:, 1, :].unsqueeze(2).to_broadcast(wide),
                                              op0=ALU.add, op1=ALU.is_equal))
            seq.link(dve.tensor_tensor(route[:, :, :], best, share, ALU.mult))
            onc = Count(dve, v_on, per=4)
            with dve.Fori(0, B) as b:
                with dve.Fori(0, 4) as r:
                    i = b * 4 + r
                    onc.start(i)
                    dve.wait_ge(pj_mm, i + 1)
                    dve.tensor_copy(qpad[:, :], banks[:, 2048:3072]).then_inc(qk_set, 1)
                    dve.tensor_scalar(kaug[:, :], banks[:, 3072:4096], row_one[:, 0:1], None, ALU.add).then_inc(qk_set, 1)
                    for u in range(32):
                        g, t = u // TB, u % TB
                        dve.wait_ge(a_mm, 32 * i + u + 1)
                        dve.tensor_reduce(mxz[:, t, 32 * g:32 * g + 1], banks[:, 1024 * (u % 2):1024 * (u % 2) + (t + 1) * P],
                                          AX, ALU.max).then_inc(mx_read, 1)
                    dve.wait_ge(mx_turned, i + 1)
                    dve.tensor_tensor(qaug[:, :], qpad[:, :], banks[:, 2048:3072], ALU.subtract).then_inc(qaug_set, 1)
                    for g in range(4):
                        dve.wait_ge(c_mm, 4 * i + g + 1)
                        o_ps = bank[6 + g % 2][:, 0:TB * SLOT].rearrange("p (t d) -> p t d", d=SLOT)
                        onc.link(dve.reciprocal(inv_o[:, g, :], o_ps[:, :, D1:SLOT].rearrange("p t a -> p (t a)")))
                        dve.tensor_tensor(o_all[:, ds(b * TB, TB), ds(r * (4 * D1) + g * D1, D1)], o_ps[:, :, 0:D1],
                                          inv_o[:, g, :].unsqueeze(2).to_broadcast([P, TB, D1]), ALU.mult).then_inc(o_norm, 1)
                    onc.end()
            end_phase(dve)
            with dve.Fori(0, T) as i:
                dve.wait_ge(pr_mm, i + 1)
                dve.tensor_tensor(tile(res, i), tile(res, i), bank[1][:, 0:D], ALU.add).then_inc(pr_added, 1)
            dve.wait_ge(pr_added, T)
            with dve.Fori(0, T // 4) as i:
                group = res[:, ds(4 * i, 4), :]
                dve.wait_ge(rb_mm, i + 1)
                dve.tensor_tensor(group, group, bank[7].rearrange("p (t d) -> p t d", d=D), ALU.add).then_inc(rb_added, 1)
                dve.wait_ge(rb_added, i + 1)
                for e in range(E1):
                    dve.wait_ge(e_mm, i * E1 + e + 1)
                    if e:
                        dve.wait_ge(e_added, i * (4 * E1) + 4 * e)
                    for t in range(4):
                        row = res[:, ds(4 * i + t, 1), :].rearrange("p a d -> p (a d)")
                        dve.scalar_tensor_tensor(out=row, in0=bank[4 + e % 2][:, P * t:P * t + P], scalar=st_r[:, E1 * t + e:E1 * t + e + 1],
                                                 in1=row, op0=ALU.mult, op1=ALU.add).then_inc(e_added, 1)


def kernel(**inputs):
    import concourse.bacc as bacc
    from concourse.bass_utils import run_bass_kernel_spmd

    n = {k: np.ascontiguousarray(v) for k, v in inputs.items()}
    arrays = {
        "x": n["L0_attn_hidden_states"].reshape(B * L, D),
        "w_gate": n["L0_ffn_w_gate"], "w_up": n["L0_ffn_w_up"], "w_down": n["L0_ffn_w_down"],
    }
    m = {k[8:]: v for k, v in n.items() if k.startswith("L0_attn_")}
    for w in ("Wq", "Wk", "Wv", "Wg", "Wo"):
        arrays[w] = m[w]
    arrays["bproj"] = np.concatenate([m["bq"], m["bk"], m["bv"], m["bg"]])[None]
    arrays["wgate"] = np.concatenate([m["Wb"], m["Wfd"], m["Wsd"], m["Wfg"], m["Wsg"]], 1)
    none = np.zeros(H0, np.float32)
    arrays["bgate"] = np.stack([np.concatenate([m["bb"], m["bfd"], m["bsd"], m["bfg"], m["bsg"]]),
                                np.concatenate([none, m["fast_decay_bias"], m["slow_decay_bias"], none, none])], 1)
    arrays["rf"] = m["resonance_flux"].reshape(1)
    arrays["onorm_w"] = m["onorm_w"]
    arrays["bo"] = m["bo"][None]
    for w in ("Wq", "Wk"):
        padded = np.zeros((D, 4, 4, 32), np.float32)
        padded[:, :, :, 1:1 + D1] = n["L1_attn_" + w].T.reshape(D, 4, 4, D1)
        arrays["W1" + w[1]] = padded.reshape(D, 4, P)
    arrays["W1v"] = n["L1_attn_Wv"].T
    arrays["W1p"] = n["L1_attn_Wp"].T
    arrays["bp1"] = n["L1_attn_bp"][None]
    arrays["Wg1"] = n["L1_ffn_Wg"]
    arrays["bg1"] = n["L1_ffn_bg"]
    arrays["W1"] = n["L1_ffn_W1"]
    arrays["W2"] = n["L1_ffn_W2"]
    arrays["b1"] = n["L1_ffn_b1"].reshape(E1, HID // P, P).transpose(2, 0, 1)
    arrays["b2"] = n["L1_ffn_b2"]
    arrays = {k: np.ascontiguousarray(v) for k, v in arrays.items()}
    nc = bacc.Bacc("TRN2", target_bir_lowering=False, num_devices=1)
    a = {k: nc.dram_tensor("in_" + k, v.shape, F32, kind="ExternalInput").ap() for k, v in arrays.items()}
    out = nc.dram_tensor("out_0", (B * L, D), F32, kind="ExternalOutput").ap()
    layer_kernel(nc, a, out, STOP)
    r = run_bass_kernel_spmd(nc, [{"in_" + k: v for k, v in arrays.items()}], core_ids=[0])
    return r.results[0]["out_0"].reshape(B, L, D)


STOP = 9
```

```python
from contextlib import ExitStack

import concourse.bass as bass
import numpy as np
from concourse import mybir

F32 = mybir.dt.float32
BF16 = mybir.dt.bfloat16
ALU = mybir.AluOpType
ACT = mybir.ActivationFunctionType
AX = mybir.AxisListType.X
ds = bass.ds

P = 128
D = 128
B, L = 4, 1024
T = B * L // P
H0, DK = 16, 64
HD = H0 * DK
INNER = 352
BLOCK = 16
H1, D1 = 16, 8
E1, HID = 8, 512
LN_EPS = 1e-5
TB = L // P
STEPS = 4
MASKED = -1e30
BOUND = 0.99 * DK
SUB = 16
NB = P // SUB
LEVELS = 3


class Count:

    def __init__(self, eng, sem, per=0):
        self.eng, self.sem, self.per, self.base, self.n = eng, sem, per, 0, 0

    def start(self, i):
        self.base, self.n = i * self.per, 0

    def done(self, ins):
        self.n += 1
        ins.then_inc(self.sem, 1)

    def link(self, ins):
        self.done(ins)
        self.eng.wait_ge(self.sem, self.base + self.n)

    def end(self):
        assert self.n == self.per, (self.n, self.per)


def layer_kernel(nc, a, out):
    ctx = ExitStack()
    with ctx:
        def sem(name):
            return ctx.enter_context(nc.semaphore(name))

        def sb(name, shape, dt=F32, scope=ctx):
            return scope.enter_context(nc.sbuf_tensor(name, shape, dt))

        def dram(name, shape):
            return nc.dram_tensor(name, shape, F32, kind="Internal").ap()

        proj_s = dram("proj_s", (B * L, 4 * HD))
        gates_s = dram("gates_s", (5 * H0, B * L))
        mem_s = dram("mem_s", (B * L, HD))
        vnorm_s = dram("vnorm_s", (H0, B * L))
        nblk_s = dram("nblk_s", (T, H0 * NB, SUB * SUB))
        blk_s = dram("blk_s", (T, 3, H0, NB, SUB, SUB))
        pb_s = dram("pb_s", (H0, NB, T * 4))
        r_s = dram("r_s", (H0, 2 * NB, T, P))
        l_s = dram("l_s", (H0, 2 * NB, T, P))
        cf_s = dram("cf_s", (4 * H0, B * L))
        pc_s = dram("pc_s", (2, T, H0 // 2, 4))
        nrm_s = dram("nrm_s", (H0, T, 2))

        banks = ctx.enter_context(nc.psum_tensor("banks", [P, 8 * 512], F32))
        bank = [banks[:, 512 * n:512 * n + 512] for n in range(8)]

        res = sb("res", [P, T, D])
        ident = sb("ident", [P, P])
        ones_row = sb("ones_row", [1, P])
        stats = sb("stats", [P, 4, T])

        rf_c = sb("rf_c", [P, 1])
        capped_flag = sb("capped_flag", [1, 1], mybir.dt.int32)
        sA = ExitStack()
        xn = sb("xn", [P, T, D], scope=sA)
        xnT = sb("xnT", [P, B * L], scope=sA)

        s1 = ExitStack()
        xq = sb("xq", [P, T, D], scope=s1)
        fa = sb("fa", [P, T * D], scope=s1)
        fc = sb("fc", [P, T * D], scope=s1)
        fsg = sb("fsg", [P, T * D], scope=s1)
        fsc = sb("fsc", [P, 2, T * D // BLOCK], scope=s1)
        NW = 6 * P + INNER
        wraw = sb("wraw", [P, NW], scope=s1)
        wqt = sb("wqt", [P, NW], scope=s1)
        wguT = sb("wguT", [P, 2, 3 * P], scope=s1)
        wdT = sb("wdT", [P, 3, P], scope=s1)
        st_n = sb("st_n", [P, P], scope=s1)
        st_q = sb("st_q", [P, P], scope=s1)
        xqT = sb("xqT", [P, P], scope=s1)
        silu_g = sb("silu_g", [P, 2, INNER], scope=s1)
        hid = sb("hid", [P, 2, INNER], scope=s1)
        hq = sb("hq", [P, INNER], scope=s1)
        hqT = sb("hqT", [P, 3, P], scope=s1)
        s1.close()

        s2 = ExitStack()
        wproj = sb("wproj", [P, 4 * HD], scope=s2)
        bias_hi = sb("bias_hi", [3, 4 * HD], BF16, scope=s2)
        bias3 = sb("bias3", [3, 4 * HD], BF16, scope=s2)
        bias_part = sb("bias_part", [3, 2], scope=s2)
        ones3 = sb("ones3", [3, P], BF16, scope=s2)
        wgate = sb("wgate", [P, 5 * H0], scope=s2)
        bgate = sb("bgate", [5 * H0, 3], scope=s2)
        gates = sb("gates", [5 * H0, B * L], scope=s2)
        st_p = sb("st_p", [P, 2, P], scope=s2)
        prj = sb("prj", [P, 2, 4 * HD], scope=s2)
        prj_sq = sb("prj_sq", [P, 2 * HD], scope=s2)
        prj_n = sb("prj_n", [P, 2, 2 * H0], scope=s2)
        sbeta = sb("sbeta", [H0, B * L], scope=s2)
        sb_tok = sb("sb_tok", [P, T, H0], scope=s2)
        vv = sb("vv", [P, T, H0], scope=s2)
        vrow = sb("vrow", [H0, B * L], scope=s2)
        s2.close()
        sA.close()

        sG = ExitStack()
        gu = sb("gu", [P, 4, T, SUB], scope=sG)
        cc = sb("cc", [P, 2, 2, T, SUB + 2], scope=sG)
        ca = sb("ca", [P, 2, T, SUB + 2], scope=sG)
        gl = sb("gl", [P, T, SUB + 2, SUB], scope=sG)
        rb = sb("rb", [P, 2 * NB, T, SUB], scope=sG)
        lx = sb("lx", [P, 2, T, NB, SUB], scope=sG)
        pb = sb("pb", [P, T, 4], scope=sG)
        pball = sb("pball", [P, NB * T * 4], scope=sG)
        cend = sb("cend", [P, 2, T, SUB], scope=sG)
        gam = sb("gam", [P, 2, T, SUB], scope=sG)
        yp = sb("yp", [P, T, 4], scope=sG)
        pc = sb("pc", [P, T, 4], scope=sG)
        y4 = sb("y4", [P, 2, T, 2, 2], scope=sG)
        bmask = sb("bmask", [P, NB], scope=sG)
        before = sb("before", [P, NB], scope=sG)
        one_rf = sb("one_rf", [P, 1], scope=sG)
        ka = sb("ka", [P, 2, HD], scope=sG)
        kta = sb("kta", [P, 8 * P], scope=sG)
        ssa = sb("ssa", [P, 2, H0, P], scope=sG)
        sG.close()
        sI = ExitStack()
        nb = sb("nb", [P, T, SUB * SUB], scope=sI)
        tb = sb("tb", [P, T, SUB, SUB], scope=sI)
        iprod = sb("iprod", [P, T * (SUB - 1) * (SUB - 1)], scope=sI)
        sI.close()
        sT = ExitStack()
        qkv_t = sb("qkv_t", [P, 2, 3 * HD], scope=sT)
        blk = sb("blk", [P, 2, 3, H0, P], scope=sT)
        rt_ = sb("rt_src", [P, 2, 8, P], scope=sT)
        lt_ = sb("lt", [P, 2, 8, P], scope=sT)
        cft = sb("cft", [64, 2, P], scope=sT)
        cf = sb("cf", [P, 64], scope=sT)
        kqt = sb("kqt", [P, 8, 2, P], scope=sT)
        cv = sb("cv", [P, 2, H0, DK], scope=sT)
        S_t = sb("S_t", [P, 8, 2 * DK], scope=sT)
        ss_sb = sb("ss_sb", [P, 2, 4, P], scope=sT)
        st_sb = sb("st_sb", [P, 2, 4, P], scope=sT)
        gt_sb = sb("gt_sb", [P, 2, 4, P], scope=sT)
        xs = sb("xs", [P, 2, 4, P], scope=sT)
        tw = sb("tw", [P, 2, 4, P], scope=sT)
        ttw = sb("ttw", [P, 2, 4, P], scope=sT)
        a_sb = sb("a_sb", [P, 2, 4, P], scope=sT)
        ag = sb("ag", [P, 2, 4, P], scope=sT)
        h_sb = sb("h_sb", [P, 2, 4, DK], scope=sT)
        ny = sb("ny", [P, 2, 4, P], scope=sT)
        zs = sb("zs", [P, 2, 2, P], scope=sT)
        za = sb("za", [P, 2, 2, 2, 2, DK], scope=sT)
        oa = sb("oa", [P, 2, 4, 2, DK], scope=sT)
        o_sb = sb("o_sb", [P, HD], scope=sT)
        sqs = sb("sqs", [P, HD], scope=sT)
        sqr = sb("sqr", [P, H0], scope=sT)
        half = sb("half", [P, 2], scope=sT)
        nrm_sb = sb("nrm_sb", [H0, T, 2], scope=sT)
        pcb = sb("pcb", [P, T * 8 * 4], scope=sT)
        lmask = sb("lmask", [P, LEVELS, P], scope=sT)
        umask = sb("umask", [P, P], scope=sT)
        sT.close()
        sB = ExitStack()
        bd = sb("bd", [P, 3, B, P], scope=sB)
        bn0 = sb("bn0", [P, B, 2], scope=sB)
        bnx = sb("bnx", [P, B, 2], scope=sB)
        bh = sb("bh", [P, P, 2, B], scope=sB)
        bt = sb("bt", [P, 2, B], scope=sB)
        rf_abs = sb("rf_abs", [P, 1], scope=sB)
        bmin = sb("bmin", [P, 1], scope=sB)
        sB.close()

        s3 = ExitStack()
        S = sb("S", [P, DK, DK], scope=s3)
        prod = sb("prod", [P, DK, DK], scope=s3)
        outer = sb("outer", [P, DK, DK], scope=s3)
        Snew = sb("Snew", [P, DK * DK], scope=s3)
        junk = sb("junk", [P, 8 * 512], BF16, scope=s3)
        qkv = sb("qkv", [P, 2, 3, STEPS, DK], scope=s3)
        ohalf = sb("ohalf", [P, STEPS, DK], scope=s3)
        obuf = sb("obuf", [B * H0, 2, STEPS, DK], scope=s3)
        pair_sum = sb("pair_sum", [P, B * H0], scope=s3)
        gdec = sb("gdec", [P, L], scope=s3)
        gndec = sb("gndec", [P, L], scope=s3)
        gout = sb("gout", [P, L], scope=s3)
        mix = sb("mix", [P, P], scope=s3)
        rf_col = sb("rf_col", [P, 1], scope=s3)
        small = sb("small", [P, 4, DK], scope=s3)
        gcur = sb("gcur", [P, 4, 2 * STEPS], scope=s3)
        cap = sb("cap", [P, 6], scope=s3)
        s3.close()

        s4 = ExitStack()
        om = sb("om", [P, 3, HD], scope=s4)
        osq = sb("osq", [P, HD], scope=s4)
        orn = sb("orn", [P, H0], scope=s4)
        og = sb("og", [P, HD], scope=s4)
        ogT = sb("ogT", [P, 8, P], scope=s4)
        wout = sb("wout", [P, 8, D], scope=s4)
        bout = sb("bout", [1, D], scope=s4)
        onw = sb("onw", [P, DK], scope=s4)
        s4.close()

        s5 = ExitStack()
        xn1 = sb("xn1", [P, T, D], scope=s5)
        xnT1 = sb("xnT1", [P, B * L], scope=s5)
        SLOT = 9
        vaug = sb("vaug", [P, T, H1, SLOT], scope=s5)
        o_all = sb("o_all", [P, T, D], scope=s5)
        route = sb("route", [P, T, E1], scope=s5)
        s6 = ExitStack()
        wq1 = sb("wq1", [P, 8, P], scope=s6)
        wk1 = sb("wk1", [P, 8, P], scope=s6)
        wv1 = sb("wv1", [P, D], scope=s6)
        wg1 = sb("wg1", [P, E1], scope=s6)
        bg1 = sb("bg1", [P, E1], scope=s6)
        logit = sb("logit", [P, T, E1], scope=s6)
        rt = sb("rt", [P, 3, T, E1], scope=s6)
        rs = sb("rs", [P, 2, T], scope=s6)
        number_i = sb("number_i", [P, E1], mybir.dt.int32, scope=s6)
        number = sb("number", [P, E1], scope=s6)
        st_x = sb("st_x", [P, P], scope=s6)
        xt_x = sb("xt_x", [P, P], scope=s6)
        st_wq = sb("st_wq", [P, 2, P], scope=s6)
        st_wk = sb("st_wk", [P, 2, P], scope=s6)
        q_parts = sb("q_parts", [P, 2, L], BF16, scope=s6)
        k_parts = sb("k_parts", [P, 2, L], BF16, scope=s6)
        q_less = sb("q_less", [P, 2, L], BF16, scope=s6)
        hi = sb("hi", [P, 2, L], BF16, scope=s6)
        rest = sb("rest", [P, 2, L], scope=s6)
        mid = sb("mid", [P, 2, L], BF16, scope=s6)
        mx = sb("mx", [P, 4, TB], scope=s6)
        mx_rest = sb("mx_rest", [P, 2, TB], scope=s6)
        mxz = sb("mxz", [P, 2, TB, P], BF16, scope=s6)
        part = sb("part", [P, 5], scope=s6)
        ident_b = sb("ident_b", [P, P], BF16, scope=s6)
        above = sb("above", [P, P], BF16, scope=s6)
        below = sb("below", [P, P], BF16, scope=s6)
        TRI = TB * (TB + 1) // 2 * P
        probs = sb("probs", [P, 2, TRI], scope=s6)
        inv_o = sb("inv_o", [P, 4, TB], scope=s6)
        s6.close()
        s7 = ExitStack()
        w1 = sb("w1", [P, E1, HID], scope=s7)
        w2 = sb("w2", [P, E1, HID // P, D], scope=s7)
        b1 = sb("b1", [P, E1, HID // P], scope=s7)
        b2 = sb("b2", [E1, D], scope=s7)
        wp1 = sb("wp1", [P, D], scope=s7)
        bp1 = sb("bp1", [1, D], scope=s7)
        st_o = sb("st_o", [P, P], scope=s7)
        oT1 = sb("oT1", [P, P], scope=s7)
        st_r = sb("st_r", [P, 4 * E1], scope=s7)
        rT = sb("rT", [E1, 4 * P], scope=s7)
        hT1 = sb("hT1", [P, 2, 4, 512], scope=s7)
        s7.close()
        s5.close()

        ld = sem("ld")
        ld1 = sem("ld1")
        const_set = sem("const_set")
        v_seq = sem("v_seq")
        norm_done = sem("norm_done")
        var_done = sem("var_done")
        std_done = sem("std_done")
        sign_done = sem("sign_done")
        wq_done = sem("wq_done")
        wt_done = sem("wt_done")
        wT_done = sem("wT_done")
        xq_done = sem("xq_done")
        staged = sem("staged")
        x_turned = sem("x_turned")
        xT_done = sem("xT_done")
        gu_done = sem("gu_done")
        silu_done = sem("silu_done")
        hid_done = sem("hid_done")
        hsign_done = sem("hsign_done")
        v_ffn = sem("v_ffn")
        hq_done = sem("hq_done")
        h_turned = sem("h_turned")
        hT_done = sem("hT_done")
        down_done = sem("down_done")
        ffn_added = sem("ffn_added")

        phase = sem("phase")
        ld2 = sem("ld2")
        p_staged = sem("p_staged")
        p_mm = sem("p_mm")
        p_silu = sem("p_silu")
        p_var = sem("p_var")
        p_std = sem("p_std")
        v_prj = sem("v_prj")
        p_normed = sem("p_normed")
        p_stored = [sem(f"p_stored{n}") for n in range(2)]
        bias_set = sem("bias_set")
        g_bias = sem("g_bias")
        g_mm = sem("g_mm")
        g_done = sem("g_done")
        g_stored = sem("g_stored")
        ld3 = sem("ld3")
        swap_set = sem("swap_set")
        v_pre = sem("v_pre")
        r_ready = sem("r_ready")
        v_rec = sem("v_rec")
        qkv_in = [sem(f"qkv_in{n}") for n in range(2)]
        stepped = [sem(f"stepped{n}") for n in range(2)]
        updated = sem("updated")
        mixed = sem("mixed")
        squared = sem("squared")
        ratio_set = sem("ratio_set")
        ratio_root = sem("ratio_root")
        lam_set = sem("lam_set")
        state_set = sem("state_set")
        o_stored = [sem(f"o_stored{n}") for n in range(2)]
        ld4 = sem("ld4")
        om_in = sem("om_in")
        v_out = sem("v_out")
        o_var = sem("o_var")
        o_std = sem("o_std")
        og_set = sem("og_set")
        og_turned = sem("og_turned")
        ogT_set = sem("ogT_set")
        o_mm = sem("o_mm")
        o_added = sem("o_added")
        sb_root = sem("sb_root")
        sbt_set = sem("sbt_set")
        vv_set = sem("vv_set")
        vv_turned = sem("vv_turned")
        vrow_root = sem("vrow_root")
        pb_turned = sem("pb_turned")
        answered = sem("answered")
        summed = sem("summed")

        gu_in = sem("gu_in")
        ka_in = [sem(f"ka_in{n}") for n in range(2)]
        ka_turned = sem("ka_turned")
        kt_kept = sem("kt_kept")
        ss_mm = sem("ss_mm")
        ss_kept = sem("ss_kept")
        nblk_out = [sem(f"nblk_out{n}") for n in range(2)]
        pb_set = sem("pb_set")
        pb_out = sem("pb_out")
        pball_in = sem("pball_in")
        gate_set = sem("gate_set")
        gate_out = sem("gate_out")
        cc_set = sem("cc_set")
        nb_in = sem("nb_in")
        inv_set = sem("inv_set")
        inv_out = sem("inv_out")
        pc_in = sem("pc_in")
        zero_set = sem("zero_set")
        lm_set = sem("lm_set")
        kq_turned = sem("kq_turned")
        kq_kept = sem("kq_kept")
        sq_set = sem("sq_set")
        nrm_mm = sem("nrm_mm")
        nrm_set = sem("nrm_set")
        nrm_out = sem("nrm_out")
        cf_kept = sem("cf_kept")
        cv_set = sem("cv_set")
        kq_mm = sem("kq_mm")
        g_mm2 = sem("g_mm2")
        ss_set = sem("ss_set")
        st_set = sem("st_set")
        g_kept = sem("g_kept")
        y_mm = sem("y_mm")
        ny_set = sem("ny_set")
        am_mm = sem("am_mm")
        a_kept = sem("a_kept")
        hm_mm = sem("hm_mm")
        h_kept = sem("h_kept")
        z_mm = sem("z_mm")
        qs_mm = sem("qs_mm")
        av_mm = sem("av_mm")
        ag_set = sem("ag_set")
        s_new = sem("s_new")
        s_zero = sem("s_zero")
        o_set = sem("o_set")
        o_kept = sem("o_kept")
        v_tile = sem("v_tile")
        bd_in = sem("bd_in")
        bn_root = sem("bn_root")
        bmin_set = sem("bmin_set")
        bt_mm = sem("bt_mm")
        flag_set = sem("flag_set")
        x_mm = [sem(f"x_mm{n}") for n in range(LEVELS)]
        x_set = [sem(f"x_set{n}") for n in range(LEVELS)]
        u_mm = [sem(f"u_mm{n}") for n in range(LEVELS)]
        tw_set = [sem(f"tw_set{n}") for n in range(LEVELS)]
        ut_mm = [sem(f"ut_mm{n}") for n in range(LEVELS - 1)]
        ttw_set = [sem(f"ttw_set{n}") for n in range(LEVELS - 1)]
        tile_in = [sem(f"tile_in{n}") for n in range(2)]
        tile_free = [sem(f"tile_free{n}") for n in range(2)]
        cleared = sem("cleared")
        hi_set = sem("hi_set")
        rest_set = sem("rest_set")
        mid_set = sem("mid_set")
        max_split = sem("max_split")
        again = [gu_in, p_std, ka_turned, kt_kept, ss_mm, ss_kept, pb_set, pb_out, pball_in, gate_set, gate_out, cc_set, nb_in, inv_set, inv_out, pc_in, zero_set, lm_set, kq_turned, kq_kept, sq_set, nrm_mm, nrm_set, nrm_out, cf_kept, cv_set, kq_mm, g_mm2, ss_set, st_set, g_kept, y_mm, ny_set, am_mm, a_kept, hm_mm, h_kept, z_mm]
        (ld5, mask_set, c_set, x1_staged, x1_turned, x1T_set, v_mm, v_set, w_staged, pj_mm, qk_set, a_mm, mx_read, mx_turned, qaug_set, b_mm, exp_done, c_mm, v_on, o_norm, ld6, o_staged, o1_turned, o1T_set, pr_mm, pr_added, r_exp, r_ready1, r_staged, r_turned, rT_set, rb_mm, rb_added, h_mm, h_silu, e_mm, e_added, out_stored) = again
        block = ctx.enter_context(nc.Block())

        phases = {}

        def end_phase(eng):
            phases[eng] = phases.get(eng, 0) + 5
            eng.drain().then_inc(phase, 1)
            eng.wait_ge(phase, phases[eng])

        def tile(buf, i):
            return buf[:, ds(i, 1), :].rearrange("p a d -> p (a d)")

        def layernorm(dve, c, src, dst, turned, layer):
            tot, mean, rstd = stats[:, 0, :], stats[:, 1, :], stats[:, 2, :]
            c.link(dve.tensor_reduce(tot, src[:, :, :], AX, ALU.add))
            c.link(dve.tensor_scalar(mean, tot, 1.0 / D, None, ALU.mult))
            c.link(dve.tensor_tensor(dst[:, :, :], src[:, :, :], mean.unsqueeze(2).to_broadcast([P, T, D]), ALU.subtract))
            sq = turned[:, :].rearrange("p (t d) -> p t d", d=D)
            c.link(dve.tensor_tensor(sq, dst[:, :, :], dst[:, :, :], ALU.mult))
            c.link(dve.tensor_reduce(tot, sq, AX, ALU.add))
            dve.tensor_scalar(mean, tot, 1.0 / D, LN_EPS, ALU.mult, ALU.add).then_inc(var_done, 1)
            dve.wait_ge(std_done, layer + 1)
            c.link(dve.reciprocal(rstd, tot))
            c.link(dve.tensor_tensor(dst[:, :, :], dst[:, :, :], rstd.unsqueeze(2).to_broadcast([P, T, D]), ALU.mult))

        def ffn_steps(eng, step):
            step(0, True)
            step(1, True)
            with eng.Fori(1, T // 2 - 1) as j:
                for y in range(2):
                    step(2 * j + y, True, y)
            step(T - 2, False)
            step(T - 1, False)

        def buffer_a(u):
            return u % 2 if u < 16 else 1

        def buffer_b(u):
            return 0 if u < 16 else u % 2

        def quantize(dve, c, src, n, a_, acc, sgn, sc, dst, sign_ready):
            def blocks(x):
                return x.rearrange("p (n k) -> p n k", k=BLOCK)
            scale, inv = sc[:, 0, 0:n], sc[:, 1, 0:n]
            c.link(dve.tensor_reduce(scale, blocks(src), AX, ALU.max, apply_absolute_value=True))
            c.link(dve.tensor_scalar(scale, scale, 1.0 / 6.0, 1e-12, ALU.mult, ALU.max))
            c.link(dve.reciprocal(inv, scale))
            sign_ready()
            c.link(dve.tensor_tensor(blocks(a_), blocks(a_), inv.unsqueeze(2).to_broadcast([P, n, BLOCK]), ALU.mult))
            c.link(dve.tensor_scalar(acc, a_, 5.0, 2.0, ALU.is_gt, ALU.mult))
            for mid in (3.5, 2.5):
                c.link(dve.scalar_tensor_tensor(out=acc, in0=a_, scalar=mid, in1=acc, op0=ALU.is_gt, op1=ALU.add))
            c.link(dve.tensor_scalar(acc, acc, 2.0, None, ALU.mult))
            for mid in (1.75, 1.25, 0.75, 0.25):
                c.link(dve.scalar_tensor_tensor(out=acc, in0=a_, scalar=mid, in1=acc, op0=ALU.is_gt, op1=ALU.add))
            c.link(dve.scalar_tensor_tensor(out=acc, in0=acc, scalar=0.5, in1=sgn, op0=ALU.mult, op1=ALU.mult))
            return dve.tensor_tensor(blocks(dst), blocks(acc), scale.unsqueeze(2).to_broadcast([P, n, BLOCK]), ALU.mult)

        def chunk_sync(sp):
            for k in range(4):
                for h in range(H0):
                    sp.dma_start(gu[NB * h:NB * h + NB, k, :, :],
                                 gates_s[(k + 1) * H0 + h, :].rearrange("(t j o) -> j t o", j=NB, o=SUB)).then_inc(gu_in, 16)
            sp.dma_start(rf_c[:, :], a["rf"].partition_broadcast(P)).then_inc(gu_in, 16)
            pj = proj_s.rearrange("(t p) n -> t p n", p=P)
            def load_keys(i, n):
                sp.dma_start(ka[:, n, :], pj[i if isinstance(i, slice) else ds(i, 1), :, HD:2 * HD].rearrange("a p n -> (a p) n")).then_inc(ka_in[n], 16)

            for n in range(2):
                load_keys(slice(n, n + 1), n)
            with sp.Fori(0, T // 2 - 1) as j:
                for n in range(2):
                    sp.wait_ge(ka_turned, 2 * j + n + 1)
                    load_keys(2 * j + 2 + n, n)
            sp.wait_ge(pb_set, 1)
            sp.dma_start(pb_s.rearrange("h j n -> (h j) n"), pb[:, :, :].rearrange("p t q -> p (t q)")).then_inc(pb_out, 16)
            sp.wait_ge(pb_out, 16)
            for h in range(H0):
                sp.dma_start(pball[NB * h:NB * h + NB, :], pb_s[h, :, :].rearrange("j n -> (j n)").partition_broadcast(NB))\
                    .then_inc(pball_in, 16)
            sp.wait_ge(gate_set, 1)
            sp.dma_start(blk_s[:, 2, :, :, :, :].rearrange("t h j s o -> (h j) t (s o)"),
                         gl[:, :, 0:SUB, :].rearrange("p t s o -> p t (s o)")).then_inc(gate_out, 16)
            for h in range(H0):
                u = slice(NB * h, NB * h + NB)
                sp.dma_start(r_s[h, :, :, :].rearrange("r t (j s) -> j (r t) s", s=SUB),
                             rb[u, :, :, :].rearrange("p r t s -> p (r t) s")).then_inc(gate_out, 16)
                sp.dma_start(l_s[h, :, :, :].rearrange("(i r) t n -> i (r t n)", r=2),
                             lx[u, :, :, :, :].rearrange("p r t j o -> p (r t j o)")).then_inc(gate_out, 16)
                for k, src in enumerate((gam[u, 0], gam[u, 1], cend[u, 0], cend[u, 1])):
                    sp.dma_start(cf_s[k * H0 + h, :].rearrange("(t j o) -> j t o", j=NB, o=SUB), src).then_inc(gate_out, 16)
                sp.dma_start(pc_s[h % 2, :, h // 2, :].rearrange("(a t) q -> a t q", a=1), pc[NB * h:NB * h + 1, :, :]).then_inc(gate_out, 16)
            sp.wait_ge(gate_out, 16 * (1 + 7 * H0))
            end_phase(sp)
            sp.dma_start(nb[:, :, :], nblk_s.rearrange("t u n -> u t n")).then_inc(nb_in, 16)
            sp.wait_ge(inv_set, 1)
            sp.dma_start(blk_s[:, 0, :, :, :, :].rearrange("t h j s o -> (h j) t (s o)"), tb[:, :, :, :].rearrange("p t s o -> p t (s o)")).then_inc(inv_out, 16)
            sp.wait_ge(inv_set, 2)
            sp.dma_start(blk_s[:, 1, :, :, :, :].rearrange("t h j s o -> (h j) t (s o)"), nb[:, :, :]).then_inc(inv_out, 16)
            sp.wait_ge(inv_out, 32)
            end_phase(sp)
            for e in range(2):
                sp.dma_start(pcb[64 * e:64 * e + 64, :], pc_s[e, :, :, :].rearrange("t h q -> (t h q)").partition_broadcast(64)).then_inc(pc_in, 16)
            cf_t = cf_s.rearrange("r (t p) -> t r p", p=P)
            ms = mem_s.rearrange("(t p) n -> t p n", p=P)
            sp.wait_ge(zero_set, 2)
            with sp.Fori(0, B) as b:
                with sp.Fori(0, TB // 2) as c:
                    for n in range(2):
                        i = b * TB + c * 2 + n
                        sp.wait_ge(tile_free[n], b * (TB // 2) + c)
                        sp.dma_start(qkv_t[:, n, :], pj[ds(i, 1), :, 0:3 * HD].rearrange("a p n -> (a p) n")).then_inc(tile_in[n], 16)
                        for j in range(NB):
                            sp.dma_start(blk[SUB * j:SUB * j + SUB, n, :, :, SUB * j:SUB * j + SUB].rearrange("p k h o -> p (k h) o"),
                                         blk_s[ds(i, 1), :, :, j, :, :].rearrange("a k h s o -> s (a k h) o")).then_inc(tile_in[n], 16)
                        for m in range(2):
                            for buf, src in ((rt_, r_s), (lt_, l_s)):
                                sp.dma_start(buf[32 * m:32 * m + 16, n, :, :],
                                             src[m:H0:2, :, ds(i, 1), :].rearrange("g r a s -> r g (a s)")).then_inc(tile_in[n], 16)
                        sp.dma_start(cft[:, n, :], cf_t[ds(i, 1), :, :].rearrange("a r p -> (a r) p")).then_inc(tile_in[n], 16)
            sp.wait_ge(nrm_set, T)
            sp.dma_start(nrm_s[:, :, :], nrm_sb[:, :, :]).then_inc(nrm_out, 16)
            sp.wait_ge(nrm_out, 16)
            sp.wait_ge(o_kept, 16 * T)
            end_phase(sp)
            for h in range(H0):
                u = slice(TB * h, TB * h + TB)
                for k, src in enumerate((gates_s[H0 + h], gates_s[2 * H0 + h], vnorm_s[h])):
                    sp.dma_start(bd[u, k, :, :], src.rearrange("(b c o) -> c b o", b=B, c=TB)).then_inc(bd_in, 16)
                for j in range(2):
                    sp.dma_start(bn0[u, :, j:j + 1], nrm_s[(h // 2) * 2 + j, :, h % 2:h % 2 + 1].rearrange("(b c) e -> c b e", b=B),
                                 allow_slow_non_contiguous=True).then_inc(bd_in, 16)
            end_phase(sp)

        def chunk_pool(pool):
            pool.memset(cc[:, :, :, :, :], 0.0).then_inc(cc_set, 1)
            nv = nblk_s.rearrange("t (h j) (s o) -> t j s h o", j=NB, o=SUB)
            with pool.Fori(0, T // 2) as c:
                for n in range(2):
                    i = 2 * c + n
                    pool.wait_ge(ss_kept, 4 * i + 4)
                    for j in range(NB):
                        pool.dma_start(nv[ds(i, 1), j, :, :, :].rearrange("a s h o -> (a s) h o"),
                                       ssa[SUB * j:SUB * j + SUB, n, :, SUB * j:SUB * j + SUB]).then_inc(nblk_out[n], 16)
            for n in range(2):
                pool.wait_ge(nblk_out[n], 16 * NB * (T // 2))
            end_phase(pool)
            end_phase(pool)
            pool.memset(blk[:, :, :, :, :], 0.0).then_inc(zero_set, 1)
            pool.memset(half[:, :], 0.0).then_inc(zero_set, 1)
            pool.memset(lmask[:, :, :], 0.0).then_inc(lm_set, 1)
            pool.memset(umask[:, :], 1.0).then_inc(lm_set, 1)
            pool.wait_ge(zero_set, 2)
            pool.wait_ge(lm_set, 2)
            pool.memset(half[0:64, 0:1], 1.0).then_inc(lm_set, 1)
            pool.wait_ge(lm_set, 3)
            pool.memset(half[64:128, 1:2], 1.0).then_inc(lm_set, 1)
            pool.wait_ge(lm_set, 4)
            for n in range(LEVELS):
                w = SUB << n
                v = lmask[:, n, :].rearrange("p (q a c) -> p q a c", a=2, c=w)[:, :, 0, :]
                pool.memset(v, 1.0).then_inc(lm_set, 1)
            pool.wait_ge(lm_set, 4 + LEVELS)
            for n in range(LEVELS):
                w = SUB << n
                v = lmask[:, n, :].rearrange("p (q a c) -> p q a c", a=2, c=w)[:, :, 0, :]
                pool.affine_select(out=v, in_=v, compare_op=ALU.is_ge, fill=0.0, base=-w,
                                   pattern=[[-2 * w, P // (2 * w)], [0, w]], channel_multiplier=1).then_inc(lm_set, 1)
                pool.wait_ge(lm_set, 5 + LEVELS + 2 * n)
                pool.affine_select(out=v, in_=v, compare_op=ALU.is_ge, fill=0.0, base=2 * w - 1,
                                   pattern=[[2 * w, P // (2 * w)], [0, w]], channel_multiplier=-1).then_inc(lm_set, 1)
            pool.affine_select(out=umask[:, :], in_=umask[:, :], compare_op=ALU.is_ge, fill=0.0, base=0,
                               pattern=[[1, P]], channel_multiplier=-1).then_inc(lm_set, 1)
            ms = mem_s.rearrange("(t p) n -> t p n", p=P)
            with pool.Fori(0, B) as b:
                with pool.Fori(0, TB) as c:
                    i = b * TB + c
                    for g in range(4):
                        at = 4 * i + g + 1
                        y = g % 2
                        pool.wait_ge(a_kept, at)
                        pool.wait_ge(g_kept, at)
                        pool.tensor_tensor(ag[:, y, :, :], a_sb[:, y, :, :], gt_sb[:, y, :, :], ALU.mult).then_inc(ag_set, 1)
                    pool.wait_ge(o_set, 4 * i + 4)
                    pool.dma_start(ms[ds(i, 1), :, :].rearrange("a p n -> (a p) n"), o_sb[:, :]).then_inc(o_kept, 16)
            end_phase(pool)
            end_phase(pool)

        def chunk_pe(pe):
            with pe.Fori(0, T // 2) as c:
                for n in range(2):
                    i = 2 * c + n
                    pe.wait_ge(ka_in[n], 16 * (c + 1))
                    pe.wait_ge(kt_kept, 2 * i)
                    for p in range(8):
                        last = pe.transpose(bank[p // 4][:, P * (p % 4):P * (p % 4) + P], ka[:, n, P * p:P * p + P], ident[:, :])
                    last.then_inc(ka_turned, 1)
                    pe.wait_ge(kt_kept, 2 * i + 2)
                    pe.wait_ge(ss_kept, 4 * i)
                    for p in range(8):
                        for e in range(2):
                            kt = kta[64 * e:64 * e + 64, P * p:P * p + P]
                            last = pe.matmul(bank[2 + 2 * (p // 4) + e][:, P * (p % 4):P * (p % 4) + P], kt, kt, start=True, stop=True)
                        if p % 4 == 3:
                            last.then_inc(ss_mm, 2)
            end_phase(pe)
            end_phase(pe)
            pe.wait_ge(lm_set, 5 + 3 * LEVELS)

            def heads(g):
                return [(m, 4 * g + m, slice(64 * (m % 2), 64 * (m % 2) + 64), (4 * g + m) // 2) for m in range(4)]

            def cols(bk, m, w=P):
                return bk[:, w * m:w * m + w]

            with pe.Fori(0, B) as b:
                with pe.Fori(0, TB // 2) as c:
                    for n in range(2):
                        i = b * TB + c * 2 + n
                        k_ = qkv_t[:, n, HD:2 * HD]
                        v_ = qkv_t[:, n, 2 * HD:3 * HD]
                        pe.wait_ge(tile_in[n], 16 * 14 * (b * (TB // 2) + c + 1))
                        pe.wait_ge(o_set, 4 * i)
                        pe.wait_ge(s_new, 4 * i)
                        for w, at in ((1, 0), (0, 2)):
                            for p in range(8):
                                last = pe.transpose(cols(bank[at + p // 4], p % 4), qkv_t[:, n, w * HD + P * p:w * HD + P * p + P], ident[:, :])
                        pe.transpose(bank[4][:, 0:64], cft[:, n, :], ident[0:64, 0:64]).then_inc(kq_turned, 1)
                        pe.wait_ge(sq_set, i + 1)
                        pe.matmul(bank[5][0:H0, 0:2], sqr[:, :], half[:, :], start=True, stop=True).then_inc(nrm_mm, 1)
                        pe.wait_ge(kq_kept, 4 * i + 4)
                        pe.wait_ge(cf_kept, i + 1)
                        pe.wait_ge(nrm_set, i + 1)
                        for q in range(2):
                            pair = (2 * q, 2 * q + 1)

                            def at(g):
                                return 4 * i + g + 1
                            for g in pair:
                                bk = bank[4 * (g % 2):4 * (g % 2) + 4]
                                if g >= 2:
                                    pe.wait_ge(o_set, at(g) - 2)
                                    pe.wait_ge(s_new, at(g) - 2)
                                for m, h, r, p in heads(g):
                                    last = pe.matmul(bk[m % 2][:, 256 * (m // 2):256 * (m // 2) + 256], kqt[r, p, 0, :],
                                                     kqt[r, p, :, :].rearrange("p w t -> p (w t)"), start=True, stop=True)
                                last.then_inc(kq_mm, 1)
                                for m, h, r, p in heads(g):
                                    last = pe.matmul(cols(bk[2 + m % 2], m // 2), rt_[32 * (m % 2):32 * (m % 2) + 16, n, p, :], lt_[32 * (m % 2):32 * (m % 2) + 16, n, p, :],
                                                     start=True, stop=True)
                                last.then_inc(g_mm2, 1)
                            for lv in range(LEVELS):
                                def cur(buf, kind, g, h):
                                    return blk[:, n, kind, h, :] if lv == 0 else buf[:, g % 2, h % 4, :]
                                for g in pair:
                                    bk = bank[4 * (g % 2):4 * (g % 2) + 4]
                                    if lv == 0:
                                        pe.wait_ge(ss_set, at(g))
                                        pe.wait_ge(g_kept, at(g))
                                    else:
                                        pe.wait_ge(tw_set[lv - 1], at(g))
                                    for m, h, r, p in heads(g):
                                        last = pe.matmul(cols(bk[3], m), ss_sb[:, g % 2, m, :], cur(tw, 0, g, h), start=True, stop=True)
                                    last.then_inc(x_mm[lv], 1)
                                for g in pair:
                                    bk = bank[4 * (g % 2):4 * (g % 2) + 4]
                                    pe.wait_ge(x_set[lv], at(g))
                                    if lv == 0:
                                        pe.wait_ge(st_set, at(g))
                                    else:
                                        pe.wait_ge(ttw_set[lv - 1], at(g))
                                    for m, h, r, p in heads(g):
                                        last = pe.matmul(cols(bk[0], m), cur(ttw, 1, g, h), xs[:, g % 2, m, :], start=True, stop=True)
                                    last.then_inc(u_mm[lv], 1)
                                    if lv < LEVELS - 1:
                                        for m, h, r, p in heads(g):
                                            last = pe.matmul(cols(bk[1], m), xs[:, g % 2, m, :], cur(ttw, 1, g, h), start=True, stop=True)
                                        last.then_inc(ut_mm[lv], 1)
                            for g in pair:
                                bk = bank[4 * (g % 2):4 * (g % 2) + 4]
                                for m, h, r, p in heads(g):
                                    last = pe.matmul(cols(bk[3 - m % 2], m // 2), kqt[r, p, 0, :], S_t[r, p, :], start=True, stop=True)
                                last.then_inc(y_mm, 1)
                            for g in pair:
                                bk = bank[4 * (g % 2):4 * (g % 2) + 4]
                                pe.wait_ge(tw_set[LEVELS - 1], at(g))
                                for m, h, r, p in heads(g):
                                    last = pe.matmul(cols(bk[1], m), tw[:, g % 2, m, :], st_sb[:, g % 2, m, :], start=True, stop=True)
                                last.then_inc(am_mm, 1)
                                pe.wait_ge(ny_set, at(g))
                                for m, h, r, p in heads(g):
                                    last = pe.matmul(cols(bk[2], m, 64), tw[:, g % 2, m, :], k_[:, DK * h:DK * h + DK], start=True, stop=True)
                                last.then_inc(hm_mm, 1)
                            for g in pair:
                                bk = bank[4 * (g % 2):4 * (g % 2) + 4]
                                pe.wait_ge(ny_set, at(g))
                                pe.wait_ge(h_kept, at(g))
                                pe.wait_ge(cv_set, i + 1)
                                for m, h, r, p in heads(g):
                                    pe.matmul(bk[0][r, P * (m // 2):P * (m // 2) + P], h_sb[:, g % 2, m, :], ny[:, g % 2, m, :], start=True, stop=True)
                                    last = pe.matmul(bk[0][r, 256 + P * (m // 2):256 + P * (m // 2) + P], h_sb[:, g % 2, m, :],
                                                     cv[:, :, h, :], start=True, stop=True)
                                last.then_inc(z_mm, 1)
                                pe.wait_ge(a_kept, at(g))
                                for m, h, r, p in heads(g):
                                    pe.matmul(cols(bk[2 + m % 2], m // 2), kqt[r, p, 1, :], S_t[r, p, :], start=True, stop=False)
                                    last = pe.matmul(cols(bk[2 + m % 2], m // 2), a_sb[:, g % 2, m, :], ny[:, g % 2, m, :], start=False, stop=True)
                                last.then_inc(qs_mm, 1)
                                pe.wait_ge(ag_set, at(g))
                                for m, h, r, p in heads(g):
                                    last = pe.matmul(cols(bk[1], m, 64), ag[:, g % 2, m, :], v_[:, DK * h:DK * h + DK], start=True, stop=True)
                                last.then_inc(av_mm, 1)
            end_phase(pe)
            pe.wait_ge(bmin_set, 1)
            pe.transpose(bank[0][0:1, 0:P], bmin[:, :], ident[:, :]).then_inc(bt_mm, 1)
            end_phase(pe)

        def chunk_act(act):
            with act.Fori(0, T // 2) as c:
                for n in range(2):
                    i = 2 * c + n
                    act.wait_ge(ka_turned, i + 1)
                    act.wait_ge(ss_mm, 4 * i)
                    for q in range(2):
                        act.copy(kta[:, 512 * q:512 * q + 512], bank[q]).then_inc(kt_kept, 1)
                    act.wait_ge(nblk_out[n], 16 * NB * c)
                    for g in range(4):
                        act.wait_ge(ss_mm, 4 * i + 2 * (g // 2) + 2)
                        h = 8 * (g // 2) + g % 2
                        act.copy(ssa[:, n, h:h + 7:2, :], bank[2 + g].rearrange("p (h t) -> p h t", t=P)).then_inc(ss_kept, 1)
            end_phase(act)
            end_phase(act)
            with act.Fori(0, B) as b:
                with act.Fori(0, TB) as c:
                    i = b * TB + c
                    act.wait_ge(kq_turned, i + 1)
                    for w, at in ((0, 0), (1, 2)):
                        for q in range(2):
                            act.copy(kqt[:, 4 * q:4 * q + 4, w, :], bank[at + q].rearrange("p (h t) -> p h t", t=P)).then_inc(kq_kept, 1)
                    act.wait_ge(nrm_mm, i + 1)
                    act.copy(nrm_sb[:, ds(i, 1), :].rearrange("p a j -> p (a j)"), bank[5][0:H0, 0:2]).then_inc(nrm_set, 1)
                    for q in range(2):
                        pair = (2 * q, 2 * q + 1)
                        for g in pair:
                            y = g % 2
                            act.wait_ge(kq_mm, 4 * i + g + 1)
                            act.copy(ss_sb[:, y, :, :].rearrange("p (k e) t -> p e k t", e=2),
                                     banks[:, 2048 * y:2048 * y + 1024].rearrange("p (e k w t) -> p e k w t", e=2, w=2, t=P)[:, :, :, 0, :])\
                                .then_inc(ss_set, 1)
                        for g in pair:
                            y = g % 2
                            act.wait_ge(y_mm, 4 * i + g + 1)
                            act.mul(ny[:, y, 0:4:2, :], bank[4 * y + 3][:, 0:256].rearrange("p (k t) -> p k t", t=P), -1.0)
                            act.mul(ny[:, y, 1:4:2, :], bank[4 * y + 2][:, 0:256].rearrange("p (k t) -> p k t", t=P), -1.0).then_inc(ny_set, 1)
                        for g in pair:
                            y = g % 2
                            act.wait_ge(am_mm, 4 * i + g + 1)
                            act.copy(a_sb[:, y, :, :].rearrange("p h t -> p (h t)"), bank[4 * y + 1]).then_inc(a_kept, 1)
                            act.wait_ge(hm_mm, 4 * i + g + 1)
                            act.copy(h_sb[:, y, :, :].rearrange("p h t -> p (h t)"), bank[4 * y + 2][:, 0:256]).then_inc(h_kept, 1)
            end_phase(act)
            act.wait_ge(bd_in, 16 * 5 * H0)
            act.activation(bnx[:, :, :], bn0[:, :, :], ACT.Sqrt).then_inc(bn_root, 1)
            act.activation(rf_abs[:, :], rf_c[:, :], ACT.Abs).then_inc(bn_root, 1)
            end_phase(act)

        def chunk_dve(dve, seq):
            dve.wait_ge(gu_in, 16 * (4 * H0 + 1))
            dve.wait_ge(cc_set, 1)
            seq.link(dve.tensor_scalar(one_rf[:, :], rf_c[:, :], 1.0, None, ALU.add))
            seq.link(dve.tensor_reduce(bmask[:, :], ident[:, :].rearrange("p (h j) -> p j h", j=NB), AX, ALU.add))
            seq.link(dve.memset(cc[:, 0, 0, :, SUB:SUB + 1], 1.0))
            seq.link(dve.memset(cc[:, 0, 1, :, SUB + 1:SUB + 2], 1.0))
            full = [P, T, SUB + 2]
            for t in range(SUB):
                src, dst = cc[:, t % 2], cc[:, (t + 1) % 2]
                fd_, sd_, fg_, sg_ = (gu[:, k, :, t].unsqueeze(2).to_broadcast(full) for k in range(4))
                seq.link(dve.tensor_tensor(ca[:, 0], src[:, 0], fd_, ALU.mult))
                seq.link(dve.tensor_tensor(ca[:, 1], src[:, 1], sd_, ALU.mult))
                seq.link(dve.scalar_tensor_tensor(out=dst[:, 0], in0=ca[:, 1], scalar=rf_c[:, 0:1], in1=ca[:, 0], op0=ALU.mult, op1=ALU.add))
                seq.link(dve.scalar_tensor_tensor(out=dst[:, 1], in0=ca[:, 0], scalar=rf_c[:, 0:1], in1=ca[:, 1], op0=ALU.mult, op1=ALU.add))
                seq.link(dve.tensor_copy(dst[:, :, :, t], one_rf[:, 0:1].unsqueeze(2).to_broadcast([P, 2, T])))
                seq.link(dve.tensor_tensor(ca[:, 0], dst[:, 0], fg_, ALU.mult))
                seq.link(dve.tensor_tensor(ca[:, 1], dst[:, 1], sg_, ALU.mult))
                seq.link(dve.tensor_tensor(gl[:, :, :, t], ca[:, 0], ca[:, 1], ALU.add))
            last = cc[:, SUB % 2]
            for m in range(2):
                seq.link(dve.tensor_copy(pb[:, :, 2 * m:2 * m + 2], last[:, m, :, SUB:SUB + 2]))
            dve.tensor_copy(bmask[:, 0:1], bmask[:, 0:1]).then_inc(pb_set, 1)
            dve.wait_ge(pb_set, 1)
            dve.wait_ge(pball_in, 16 * H0)
            pv = pball[:, :].rearrange("p (j t q) -> p j t q", j=NB, q=4)
            wide = [P, T, SUB]
            seq.link(dve.memset(rb[:, 0:2, :, :], 0.0))
            for j in range(NB):
                for m in range(2):
                    out_ = rb[:, 2 * (j + 1) + m, :, :] if j < NB - 1 else cend[:, m]
                    r_ = last[:, m, :, 0:SUB]
                    if j == 0:
                        seq.link(dve.tensor_scalar(out_, r_, bmask[:, 0:1], None, ALU.mult))
                        continue
                    prev = [rb[:, 2 * j + k, :, :] for k in range(2)]
                    seq.link(dve.tensor_tensor(ca[:, 0, :, 0:SUB], prev[0], pv[:, j, :, 2 * m].unsqueeze(2).to_broadcast(wide), ALU.mult))
                    seq.link(dve.tensor_tensor(ca[:, 1, :, 0:SUB], prev[1], pv[:, j, :, 2 * m + 1].unsqueeze(2).to_broadcast(wide), ALU.mult))
                    seq.link(dve.tensor_tensor(ca[:, 0, :, 0:SUB], ca[:, 0, :, 0:SUB], ca[:, 1, :, 0:SUB], ALU.add))
                    seq.link(dve.scalar_tensor_tensor(out=out_, in0=r_, scalar=bmask[:, j:j + 1], in1=ca[:, 0, :, 0:SUB], op0=ALU.mult, op1=ALU.add))
            seq.link(dve.memset(before[:, NB - 1:NB], 0.0))
            for j in range(NB - 2, -1, -1):
                seq.link(dve.tensor_tensor(before[:, j:j + 1], before[:, j + 1:j + 2], bmask[:, j + 1:j + 2], ALU.add))
            for buf in (yp, pc):
                seq.link(dve.memset(buf[:, :, :], 0.0))
                seq.link(dve.memset(buf[:, :, 0:4:3], 1.0))
            q4 = [P, T, 2, 2]

            def times(buf, j):
                v = buf[:, :, :].rearrange("p t (i k) -> p t i k", k=2)
                pj_ = pv[:, j, :, :].rearrange("p t (i k) -> p t i k", k=2)
                for k in range(2):
                    seq.link(dve.tensor_tensor(y4[:, k], pj_[:, :, :, k:k + 1].to_broadcast(q4), v[:, :, k:k + 1, :].to_broadcast(q4), ALU.mult))
                return y4[:, 0].rearrange("p t i k -> p t (i k)"), y4[:, 1].rearrange("p t i k -> p t (i k)")
            for j in range(NB):
                y0, y1 = times(pc, j)
                seq.link(dve.tensor_tensor(pc[:, :, :], y0, y1, ALU.add))
                y0, y1 = times(yp, j)
                seq.link(dve.tensor_tensor(y0, y0, y1, ALU.add))
                seq.link(dve.tensor_tensor(y0, y0, yp[:, :, :], ALU.subtract))
                seq.link(dve.scalar_tensor_tensor(out=yp[:, :, :], in0=y0, scalar=before[:, j:j + 1], in1=yp[:, :, :], op0=ALU.mult, op1=ALU.add))
            for m in range(2):
                seq.link(dve.tensor_tensor(ca[:, 0, :, 0:SUB], gl[:, :, SUB, :], yp[:, :, m].unsqueeze(2).to_broadcast(wide), ALU.mult))
                seq.link(dve.tensor_tensor(ca[:, 1, :, 0:SUB], gl[:, :, SUB + 1, :], yp[:, :, 2 + m].unsqueeze(2).to_broadcast(wide), ALU.mult))
                seq.link(dve.tensor_tensor(gam[:, m], ca[:, 0, :, 0:SUB], ca[:, 1, :, 0:SUB], ALU.add))
            for m in range(2):
                seq.link(dve.tensor_tensor(lx[:, m, :, :, :], gl[:, :, SUB + m, :].unsqueeze(2).to_broadcast([P, T, NB, SUB]),
                                           bmask[:, :].unsqueeze(1).unsqueeze(3).to_broadcast([P, T, NB, SUB]), ALU.mult))
            dve.tensor_copy(one_rf[:, :], one_rf[:, :]).then_inc(gate_set, 1)
            end_phase(dve)
            dve.wait_ge(nb_in, 16)
            seq.link(dve.memset(tb[:, :, :, :], 0.0))
            seq.link(dve.memset(tb[:, :, :, :].rearrange("p t s o -> p t (s o)")[:, :, 0:SUB * SUB:SUB + 1], 1.0))
            nv = nb[:, :, :].rearrange("p t (s o) -> p t s o", o=SUB)
            for s in range(1, SUB):
                sh = [P, T, s, s]
                pr = iprod[:, 0:T * s * s].rearrange("p (t k j) -> p t k j", k=s, j=s)
                seq.link(dve.tensor_tensor(pr, nv[:, :, s, 0:s].unsqueeze(2).to_broadcast(sh), tb[:, :, 0:s, 0:s].rearrange("p t j k -> p t k j"), ALU.mult))
                seq.link(dve.tensor_reduce(tb[:, :, s, 0:s], pr, AX, ALU.add, negate=True))
            dve.tensor_copy(iprod[:, 0:1], iprod[:, 0:1]).then_inc(inv_set, 1)
            dve.tensor_copy(nv, tb[:, :, :, :].rearrange("p t s o -> p t o s")).then_inc(inv_set, 1)
            end_phase(dve)
            dve.wait_ge(pc_in, 32)
            dve.wait_ge(lm_set, 5 + 3 * LEVELS)
            ch = Count(dve, v_tile, per=2 * (1 + 4 * 7))
            with dve.Fori(0, B) as b:
                dve.wait_ge(s_new, b * (4 * TB))
                dve.memset(S_t[:, :, :], 0.0).then_inc(s_zero, 1)
                with dve.Fori(0, TB // 2) as c:
                    ch.start(b * (TB // 2) + c)
                    for n in range(2):
                        i = b * TB + c * 2 + n
                        if n == 0:
                            dve.wait_ge(s_zero, b + 1)
                        dve.wait_ge(s_new, 4 * i)
                        ch.link(dve.tensor_tensor(sqs[:, :], S_t[:, :, :].rearrange("p h v -> p (h v)"), S_t[:, :, :].rearrange("p h v -> p (h v)"), ALU.mult))
                        dve.tensor_reduce(sqr[:, :], sqs[:, :].rearrange("p (q v) -> p q v", v=DK), AX, ALU.add).then_inc(sq_set, 1)
                        dve.wait_ge(kq_turned, i + 1)
                        dve.tensor_copy(cf[:, :], bank[4][:, 0:64]).then_inc(cf_kept, 1)
                        dve.wait_ge(cf_kept, i + 1)
                        dve.tensor_tensor(cv[:, :, :, :], cf[:, 32:64].rearrange("p (m h) -> p m h", m=2).unsqueeze(3).to_broadcast([P, 2, H0, DK]),
                                          qkv_t[:, n, 2 * HD:3 * HD].rearrange("p (h v) -> p h v", v=DK).unsqueeze(1).to_broadcast([P, 2, H0, DK]),
                                          ALU.mult).then_inc(cv_set, 1)
                        for q in range(2):
                            pair = (2 * q, 2 * q + 1)

                            def at(g):
                                return 4 * i + g + 1

                            def ps4(k):
                                return bank[k].rearrange("p (h t) -> p h t", t=P)
                            for g in pair:
                                y = g % 2
                                dve.wait_ge(kq_mm, at(g))
                                dve.wait_ge(ss_set, at(g))
                                for e in range(2):
                                    last = dve.tensor_tensor(st_sb[:, y, e:4:2, :], bank[4 * y + e].rearrange("p (k w t) -> p k w t", w=2, t=P)[:, :, 1, :],
                                                             umask[:, :].unsqueeze(1).to_broadcast([P, 2, P]), ALU.mult)
                                last.then_inc(st_set, 1)
                                dve.wait_ge(g_mm2, at(g))
                                dve.tensor_tensor(gt_sb[:, y, :, :].rearrange("p (k e) t -> p e k t", e=2),
                                                  banks[:, 2048 * y + 1024:2048 * y + 2048].rearrange("p (e c) -> p e c", e=2)[:, :, 0:256]
                                                  .rearrange("p e (k t) -> p e k t", t=P),
                                                  blk[:, n, 2, 4 * g:4 * g + 4, :].rearrange("p (k e) t -> p e k t", e=2), ALU.add).then_inc(g_kept, 1)
                            for lv in range(LEVELS):
                                for g in pair:
                                    y = g % 2
                                    dve.wait_ge(x_mm[lv], at(g))
                                    dve.tensor_tensor(xs[:, y, :, :], ps4(4 * y + 3), lmask[:, lv, :].unsqueeze(1).to_broadcast([P, 4, P]), ALU.mult)\
                                        .then_inc(x_set[lv], 1)
                                for g in pair:
                                    y = g % 2
                                    old = blk[:, n, 0, 4 * g:4 * g + 4, :] if lv == 0 else tw[:, y, :, :]
                                    oldT = blk[:, n, 1, 4 * g:4 * g + 4, :] if lv == 0 else ttw[:, y, :, :]
                                    dve.wait_ge(u_mm[lv], at(g))
                                    dve.tensor_tensor(tw[:, y, :, :], old, ps4(4 * y), ALU.subtract).then_inc(tw_set[lv], 1)
                                    if lv < LEVELS - 1:
                                        dve.wait_ge(ut_mm[lv], at(g))
                                        dve.tensor_tensor(ttw[:, y, :, :], oldT, ps4(4 * y + 1), ALU.subtract).then_inc(ttw_set[lv], 1)
                            for g in pair:
                                y = g % 2
                                dve.wait_ge(z_mm, at(g))
                                st = S_t[:, 2 * g:2 * g + 2, :]
                                zz = bank[4 * y][:, 0:256].rearrange("p (q v) -> p q v", q=2)
                                ww = bank[4 * y][:, 256:512].rearrange("p (q m v) -> p q m v", q=2, m=2)
                                ch.link(dve.tensor_tensor(zs[:, y, :, :], st, zz, ALU.add))
                                sh = [P, 2, 2, DK]
                                pcv = pcb[:, :].rearrange("p (t h m k) -> p t h m k", t=T, h=8, m=2)[:, ds(i, 1), 2 * g:2 * g + 2, :, :]\
                                    .rearrange("p a h m k -> p (a h) m k")
                                zv = zs[:, y, :, :].rearrange("p q (k v) -> p q k v", k=2)
                                for k in range(2):
                                    ch.link(dve.tensor_tensor(za[:, y, k], zv[:, :, k:k + 1, :].to_broadcast(sh), pcv[:, :, :, k:k + 1].to_broadcast(sh), ALU.mult))
                                ch.link(dve.tensor_tensor(za[:, y, 0], za[:, y, 0], za[:, y, 1], ALU.add))
                                dve.wait_ge(qs_mm, at(g))
                                dve.tensor_tensor(st.rearrange("p q (m v) -> p q m v", m=2), za[:, y, 0], ww, ALU.add).then_inc(s_new, 1)
                                ov = o_sb[:, 256 * g:256 * g + 256].rearrange("p (h v) -> p h v", v=DK)
                                if g == 0:
                                    dve.wait_ge(o_kept, 16 * i)
                                for e in range(2):
                                    oq = bank[4 * y + 2 + e][:, 0:256].rearrange("p (h m v) -> p h m v", m=2, v=DK)
                                    gm_ = cf[:, 0:32].rearrange("p (m h) -> p h m", m=2)[:, 4 * g + e:4 * g + 4:2, :].unsqueeze(3).to_broadcast([P, 2, 2, DK])
                                    ch.link(dve.tensor_tensor(oa[:, y, e:4:2, :, :], oq, gm_, ALU.mult))
                                dve.wait_ge(av_mm, at(g))
                                ch.link(dve.tensor_tensor(ov, oa[:, y, :, 0, :], oa[:, y, :, 1, :], ALU.add))
                                dve.tensor_tensor(ov, ov, bank[4 * y + 1][:, 0:256].rearrange("p (h v) -> p h v", v=DK), ALU.add).then_inc(o_set, 1)
                            if q == 1:
                                dve.wait_ge(o_set, at(3))
                                dve.wait_ge(s_new, at(3))
                                dve.sem_inc(tile_free[n], 1)
                    ch.end()
            end_phase(dve)
            dve.wait_ge(bd_in, 16 * 5 * H0)
            dve.wait_ge(bn_root, 2)
            bdv = bd[:, 0:2, :, :]
            for t in range(P):
                sh = [P, 2, B]
                cur_ = bnx[:, :, :].rearrange("p b j -> p j b") if t == 0 else bh[:, (t - 1), :, :]
                seq.link(dve.tensor_tensor(bt[:, :, :], cur_, bdv[:, :, :, t], ALU.mult))
                seq.link(dve.tensor_tensor(bt[:, :, :], bt[:, :, :], bd[:, 2, :, t].unsqueeze(1).to_broadcast(sh), ALU.add))
                for j in range(2):
                    last = dve.scalar_tensor_tensor(out=bh[:, t, j, :], in0=bt[:, 1 - j, :], scalar=rf_abs[:, 0:1], in1=bt[:, j, :], op0=ALU.mult, op1=ALU.add)
                    seq.done(last)
                dve.wait_ge(v_seq, seq.base + seq.n)
            seq.link(dve.tensor_scalar(bh[:, :, :, :], bh[:, :, :, :], BOUND, None, ALU.is_le))
            dve.tensor_reduce(bmin[:, :], bh[:, :, :, :].rearrange("p t j b -> p (t j b)"), AX, ALU.min).then_inc(bmin_set, 1)
            dve.wait_ge(bt_mm, 1)
            seq.link(dve.tensor_reduce(bmin[0:1, :], bank[0][0:1, 0:P], AX, ALU.min))
            seq.link(dve.tensor_scalar(bmin[0:1, :], bmin[0:1, :], -1.0, 1.0, ALU.mult, ALU.add))
            dve.tensor_copy(capped_flag[:, :], bmin[0:1, :]).then_inc(flag_set, 1)
            end_phase(dve)

        def capped(eng):
            eng.wait_ge(flag_set, 1)
            flag = eng.value_load(capped_flag[0:1, 0:1], min_val=0, max_val=1)
            return eng.If(flag > 0)

        @block.sync
        def _(sp):
            xv = a["x"].rearrange("(t p) d -> p t d", p=P)
            for c in range(4):
                sp.dma_start(res[:, 8 * c:8 * c + 8, :], xv[:, 8 * c:8 * c + 8, :]).then_inc(ld, 16)
            sp.wait_ge(const_set, 1)
            for m, w in enumerate(("w_gate", "w_up")):
                for c in range(3):
                    rows = min(P, INNER - P * c)
                    sp.dma_start(wraw[0:rows, (3 * m + c) * P:(3 * m + c + 1) * P],
                                 a[w][P * c:P * c + rows, :]).then_inc(ld1, 16)
            sp.dma_start(wraw[:, 6 * P:NW], a["w_down"]).then_inc(ld1, 16)
            end_phase(sp)
            for n, w in enumerate(("Wq", "Wk", "Wv", "Wg")):
                sp.dma_start(wproj[:, HD * n:HD * n + HD], a[w]).then_inc(ld2, 16)
            sp.dma_start(prj[0:3, 0, :], a["bproj"].partition_broadcast(3)).then_inc(ld2, 16)
            sp.dma_start(bias_part[:, :], a["bias_part"]).then_inc(ld2, 16)
            sp.dma_start(wgate[:, :], a["wgate"]).then_inc(ld2, 16)
            sp.dma_start(bgate[:, 0:2], a["bgate"]).then_inc(ld2, 16)
            sp.wait_ge(g_done, 8)
            sp.dma_start(gates_s, gates[:, :]).then_inc(g_stored, 16)
            ps_v = proj_s.rearrange("(t p) n -> t p n", p=P)
            with sp.Fori(0, T // 2) as j:
                for n in range(2):
                    i = 2 * j + n
                    sp.wait_ge(p_normed, 2 * i + 2)
                    sp.wait_ge(p_silu, 8 * i + 16)
                    sp.dma_start(ps_v[ds(i, 1), :, :].rearrange("a p n -> (a p) n"), prj[:, n, :]).then_inc(p_stored[n], 16)
            sp.wait_ge(vrow_root, 8)
            sp.dma_start(vnorm_s, vrow[:, :]).then_inc(g_stored, 16)
            sp.wait_ge(g_stored, 32)
            for n in range(2):
                sp.wait_ge(p_stored[n], 16 * (T // 2))
            end_phase(sp)
            chunk_sync(sp)
            with capped(sp):
                sp.dma_start(rf_col[:, :], a["rf"].partition_broadcast(P)).then_inc(ld3, 16)
                for j in range(2):
                    for b in range(B):
                        p0 = j * B * H0 + b * H0
                        for buf, kind in ((gdec, 1 + j), (gout, 3 + j)):
                            sp.dma_start(buf[p0:p0 + H0, :], gates_s[kind * H0:kind * H0 + H0, b * L:b * L + L]).then_inc(ld3, 16)
                pv = proj_s.rearrange("(b t) (w h d) -> w b h t d", b=B, w=4, h=H0)
                with sp.Fori(0, L // (2 * STEPS)) as i:
                    for n in range(2):
                        sp.wait_ge(stepped[n], i)
                        for w in range(3):
                            for j in range(2):
                                for b in range(B):
                                    p0 = j * B * H0 + b * H0
                                    sp.dma_start(qkv[p0:p0 + H0, n, w, :, :], pv[w, b, :, ds(i * (2 * STEPS) + n * STEPS, STEPS), :])\
                                        .then_inc(qkv_in[n], 16)
            end_phase(sp)
            for c in range(8):
                sp.dma_start(wout[:, c, :], a["Wo"][P * c:P * c + P, :]).then_inc(ld4, 16)
            sp.dma_start(bout[:, :], a["bo"]).then_inc(ld4, 16)
            sp.dma_start(onw[:, :], a["onorm_w"].partition_broadcast(P)).then_inc(ld4, 16)
            mt = mem_s.rearrange("(t p) n -> t p n", p=P)
            with sp.Fori(0, T) as i:
                sp.wait_ge(og_set, i)
                sp.dma_start(om[:, 0, :], mt[ds(i, 1), :, :].rearrange("a p n -> (a p) n")).then_inc(om_in, 16)
                sp.dma_start(om[:, 2, :], ps_v[ds(i, 1), :, 3 * HD:4 * HD].rearrange("a p n -> (a p) n")).then_inc(om_in, 16)
            end_phase(sp)
            sp.wait_ge(cleared, len(again))
            sp.drain()
            sp.dma_start(wq1[:, :, :], a["W1q"]).then_inc(ld5, 16)
            sp.dma_start(wk1[:, :, :], a["W1k"]).then_inc(ld5, 16)
            sp.dma_start(part[:, :], a["part"]).then_inc(ld5, 16)
            sp.dma_start(wv1[:, :], a["W1v"]).then_inc(ld5, 16)
            sp.dma_start(wg1[:, :], a["Wg1"]).then_inc(ld5, 16)
            sp.dma_start(bg1[:, :], a["bg1"].partition_broadcast(P)).then_inc(ld5, 16)
            end_phase(sp)
            sp.dma_start(wp1[:, :], a["W1p"]).then_inc(ld6, 16)
            sp.dma_start(bp1[:, :], a["bp1"]).then_inc(ld6, 16)
            sp.dma_start(w1[:, :, :], a["W1"].rearrange("e p n -> p e n")).then_inc(ld6, 16)
            for e in range(E1):
                sp.dma_start(w2[:, e, :, :], a["W2"][e].rearrange("(c p) d -> p c d", p=P)).then_inc(ld6, 16)
            sp.dma_start(b1[:, :, :], a["b1"]).then_inc(ld6, 16)
            sp.dma_start(b2[:, :], a["b2"]).then_inc(ld6, 16)
            ov = out.rearrange("(t p) d -> p t d", p=P)
            with sp.Fori(0, T // 4) as i:
                sp.wait_ge(e_added, (i + 1) * (4 * E1))
                sp.dma_start(ov[:, ds(4 * i, 4), :], res[:, ds(4 * i, 4), :]).then_inc(out_stored, 16)
            sp.wait_ge(out_stored, 16 * (T // 4))

        @block.gpsimd
        def _(pool):
            pool.memset(wraw[:, :], 0.0).then_inc(const_set, 1)
            pool.memset(ident[:, :], 0.0).then_inc(const_set, 1)
            pool.memset(ones_row[:, :], 1.0).then_inc(const_set, 1)
            pool.wait_ge(const_set, 3)
            pool.affine_select(out=ident[:, :], in_=ident[:, :], compare_op=ALU.not_equal, fill=1.0, base=0,
                               pattern=[[-1, P]], channel_multiplier=1).then_inc(const_set, 1)
            pool.wait_ge(xq_done, 1)
            with pool.Fori(0, T) as i:
                pool.wait_ge(x_turned, i)
                pool.tensor_copy(st_n[:, :], tile(xn, i)).then_inc(staged, 1)
                pool.tensor_copy(st_q[:, :], tile(xq, i)).then_inc(staged, 1)
            end_phase(pool)
            pool.sem_inc(p_silu, 8)
            pool.sem_inc(p_mm, 8)
            with pool.Fori(0, T // 2) as j:
                for n in range(2):
                    i = 2 * j + n
                    pool.wait_ge(p_mm, 8 * i)
                    pool.tensor_copy(st_p[:, n, :], xnT[:, ds(i * P, P)]).then_inc(p_staged, 1)
            end_phase(pool)
            chunk_pool(pool)
            with capped(pool):
                pool.memset(mix[:, :], 0.0).then_inc(swap_set, 1)
                for n, off in enumerate((64, -64)):
                    pool.wait_ge(swap_set, n + 1)
                    pool.affine_select(out=mix[:, :], in_=mix[:, :], compare_op=ALU.not_equal, fill=1.0, base=off,
                                       pattern=[[-1, P]], channel_multiplier=1).then_inc(swap_set, 1)
                mv = mem_s.rearrange("(b t) (h d) -> b h t d", b=B, h=H0)
                with pool.Fori(0, L // (2 * STEPS)) as i:
                    for n in range(2):
                        pool.wait_ge(stepped[n], i + 1)
                        for b in range(B):
                            pool.dma_start(mv[b, :, ds(i * (2 * STEPS) + n * STEPS, STEPS), :], obuf[b * H0:b * H0 + H0, n, :, :])\
                                .then_inc(o_stored[n], 16)
                for n in range(2):
                    pool.wait_ge(o_stored[n], L // (2 * STEPS) * 64)
            end_phase(pool)
            end_phase(pool)
            for x in again:
                pool.sem_clear(x).then_inc(cleared, 1)
            pool.wait_ge(cleared, len(again))
            pool.drain()
            pool.iota(number_i[:, :], pattern=[[1, E1]], base=0, channel_multiplier=0).then_inc(mask_set, 1)
            for m in (above, below):
                pool.memset(m[:, :], 0.0).then_inc(mask_set, 1)
            pool.memset(vaug[:, :, :, :], 1.0).then_inc(mask_set, 1)
            pool.memset(mxz[:, :, :, :], 0.0).then_inc(mask_set, 1)
            pool.wait_ge(mask_set, 5)
            for m, (cm, step) in ((above, (1, -1)), (below, (-1, 1))):
                pool.affine_select(out=m[:, :], in_=m[:, :], compare_op=ALU.is_ge, fill=MASKED, base=0,
                                   pattern=[[step, P]], channel_multiplier=cm).then_inc(mask_set, 1)
            pool.wait_ge(norm_done, 2)
            with pool.Fori(0, T) as i:
                pool.wait_ge(x1_turned, i)
                pool.tensor_copy(st_x[:, :], tile(xn1, i)).then_inc(x1_staged, 1)
            with pool.Fori(0, B) as b:
                with pool.Fori(0, 4) as r:
                    pool.wait_ge(pj_mm, 16 * b + 4 * r)
                    pool.tensor_copy(st_wq[:, :, :], wq1[:, ds(2 * r, 2), :]).then_inc(w_staged, 1)
                    pool.tensor_copy(st_wk[:, :, :], wk1[:, ds(2 * r, 2), :]).then_inc(w_staged, 1)
            end_phase(pool)
            with pool.Fori(0, T) as i:
                pool.wait_ge(o1_turned, i)
                pool.tensor_copy(st_o[:, :], tile(o_all, i)).then_inc(o_staged, 1)
            with pool.Fori(0, T // 4) as i:
                pool.wait_ge(e_added, i * (4 * E1))
                pool.tensor_copy(st_r[:, :], route[:, ds(4 * i, 4), :].rearrange("p t e -> p (t e)")).then_inc(r_staged, 1)

        @block.tensor
        def _(pe):
            pe.wait_ge(const_set, 4)
            pe.wait_ge(wq_done, 1)
            for n in range(6):
                pe.transpose(bank[n // 3][:, P * (n % 3):P * (n % 3 + 1)], wqt[:, P * n:P * (n + 1)], ident[:, :])
            for c in range(3):
                w = min(P, INNER - P * c)
                last = pe.transpose(bank[2][0:w, P * c:P * (c + 1)], wqt[:, 6 * P + P * c:6 * P + P * c + w], ident[:, :])
            last.then_inc(wt_done, 1)
            pe.wait_ge(wT_done, 3)

            def gate_up(i, y):
                pe.wait_ge(staged, 2 * i + 2)
                pe.wait_ge(xT_done, 2 * i)
                pe.transpose(bank[0][:, 0:P], st_n[:, :], ident[:, :])
                pe.transpose(bank[0][:, P:2 * P], st_q[:, :], ident[:, :]).then_inc(x_turned, 1)
                pe.wait_ge(xT_done, 2 * i + 2)
                if not (isinstance(i, int) and i < 2):
                    pe.wait_ge(hid_done, i - 1)
                for n in range(2):
                    last = pe.matmul(bank[1 + 2 * y + n][:, 0:INNER], xqT[:, :],
                                     wguT[:, n, 0:INNER], start=True, stop=True)
                last.then_inc(gu_done, 1)

            def ffn_pe(i, more, y=None):
                y = i % 2 if y is None else y
                if more:
                    gate_up(i + 2, y)
                pe.wait_ge(hq_done, i + 1)
                pe.wait_ge(hT_done, 2 * i)
                for c in range(3):
                    w = min(P, INNER - P * c)
                    last = pe.transpose(bank[5][0:w, P * c:P * (c + 1)], hq[:, P * c:P * c + w], ident[:, :])
                last.then_inc(h_turned, 1)
                pe.wait_ge(hT_done, 2 * i + 2)
                if not (isinstance(i, int) and i < 2):
                    pe.wait_ge(ffn_added, i - 1)
                for c in range(3):
                    w = min(P, INNER - P * c)
                    last = pe.matmul(bank[6 + y][:, 0:D], hqT[0:w, c, :], wdT[0:w, c, :], start=(c == 0), stop=(c == 2))
                last.then_inc(down_done, 1)

            gate_up(0, 0)
            gate_up(1, 1)
            ffn_steps(pe, ffn_pe)
            end_phase(pe)
            pe.wait_ge(ld2, 128)
            for n in range(8):
                pe.matmul(bank[n][0:5 * H0, :], wgate[:, :], xnT[:, 512 * n:512 * n + 512], start=True, stop=True).then_inc(g_mm, 1)
            pe.wait_ge(sb_root, 1)
            for t in range(T):
                last = pe.matmul(bank[0][:, H0 * t:H0 * t + H0], sbeta[:, P * t:P * t + P], ident[0:H0, 0:H0], start=True, stop=True)
            last.then_inc(pb_turned, 1)
            pe.wait_ge(bias_set, 5)
            pe.wait_ge(sbt_set, 1)
            with pe.Fori(0, T // 2) as j:
                for y in range(2):
                    i = 2 * j + y
                    pe.wait_ge(p_staged, i + 1)
                    for n in range(8):
                        pe.wait_ge(p_silu, 8 * i + n + 1)
                        pe.matmul(bank[n], st_p[:, y, :], wproj[:, 512 * n:512 * n + 512], start=True, stop=False)
                        pe.matmul(bank[n], ones3[:, :], bias3[:, 512 * n:512 * n + 512], start=False, stop=True).then_inc(p_mm, 1)
            pe.wait_ge(p_silu, 8 * T + 8)
            pe.wait_ge(vv_set, T)
            for t in range(T):
                last = pe.transpose(bank[t // 4][0:H0, P * (t % 4):P * (t % 4) + P], vv[:, t, :], ident[:, :])
                if t % 4 == 3:
                    last.then_inc(vv_turned, 1)
            end_phase(pe)
            chunk_pe(pe)
            with capped(pe):
                pe.wait_ge(r_ready, 1)
                with pe.Fori(0, L // (2 * STEPS)) as i:
                    for s in range(2 * STEPS):
                        pe.wait_ge(updated, 2 * STEPS * i + s + 1)
                        for n in range(8):
                            last = pe.matmul(bank[n], mix[:, :], Snew[:, 512 * n:512 * n + 512], start=True, stop=True)
                        last.then_inc(mixed, 1)
                        if s % STEPS == STEPS - 1:
                            n = s // STEPS
                            pe.wait_ge(answered, 2 * i + n + 1)
                            pe.matmul(bank[0][0:B * H0, 0:STEPS * DK], pair_sum[:, :], ohalf[:, :, :].rearrange("p k d -> p (k d)"),
                                      start=True, stop=True).then_inc(summed, 1)
            end_phase(pe)
            pe.wait_ge(ld4, 160)
            with pe.Fori(0, T) as i:
                pe.wait_ge(og_set, i + 1)
                for c in range(8):
                    last = pe.transpose(bank[c // 4][:, P * (c % 4):P * (c % 4) + P], og[:, P * c:P * c + P], ident[:, :])
                last.then_inc(og_turned, 1)
                pe.wait_ge(ogT_set, 2 * i + 2)
                pe.wait_ge(o_added, i)
                for c in range(8):
                    pe.matmul(bank[2][:, 0:D], ogT[:, c, :], wout[:, c, :], start=(c == 0), stop=False)
                pe.matmul(bank[2][:, 0:D], ones_row[:, :], bout[:, :], start=False, stop=True).then_inc(o_mm, 1)
            end_phase(pe)
            pe.wait_ge(cleared, len(again))
            pe.drain()
            pe.wait_ge(ld5, 96)
            with pe.Fori(0, T) as i:
                pe.wait_ge(x1_staged, i + 1)
                pe.wait_ge(x1T_set, 2 * i)
                pe.transpose(bank[0][:, 0:P], st_x[:, :], ident[:, :]).then_inc(x1_turned, 1)
                pe.wait_ge(x1T_set, 2 * i + 2)
                pe.wait_ge(v_set, 2 * i)
                pe.matmul(bank[1][:, 0:D], xt_x[:, :], wv1[:, :], start=True, stop=True)
                pe.matmul(bank[2][:, 0:E1], xt_x[:, :], wg1[:, :], start=True, stop=True).then_inc(v_mm, 1)
            pe.wait_ge(c_set, 1)
            pe.wait_ge(v_set, 2 * T)
            with pe.Fori(0, B) as b:
                with pe.Fori(0, 4) as r:
                    i = b * 4 + r
                    pe.wait_ge(w_staged, 2 * i + 2)
                    for z in range(4):
                        w = (st_wq, st_wk)[z % 2]
                        if z == 1:
                            pe.wait_ge(o_norm, 4 * i)
                        if z >= 2:
                            pe.wait_ge(hi_set, 4 * i + z - 1)
                            pe.wait_ge(rest_set, 4 * i + z - 1)
                        for n in range(2):
                            last = pe.matmul(bank[4 + 2 * (z % 2) + n], w[:, z // 2, :], xnT1[:, ds(b * L + 512 * n, 512)], start=True, stop=True)
                        last.then_inc(pj_mm, 1)
                    pe.wait_ge(exp_done, 32 * i)

                    def turn_maxima(p):
                        pe.wait_ge(max_split, 2 * i + p + 1)
                        if p:
                            pe.wait_ge(qaug_set, 2 * i + 1)
                        for t in range(TB):
                            last = pe.matmul(bank[4 + t // 4][:, P * (t % 4):P * (t % 4) + P], mxz[:, p, t, :], ident_b[:, :], start=True, stop=True)
                        last.then_inc(mx_turned, 1)

                    def for_maxima(u):
                        g, t, at = u // TB, u % TB, 2 * buffer_a(u)
                        rows = slice(64 * (g % 2), 64 * (g % 2) + 64)
                        if u % 16 == 0:
                            pe.wait_ge(qk_set, 4 * i + 2 * (g // 2) + 2)
                        if u >= 16:
                            pe.wait_ge(mx_read, 32 * i + u)
                        elif u >= 2:
                            pe.wait_ge(mx_read, 32 * i + u - 1)
                        for n in range((t + 4) // 4):
                            w = min(512, (t + 1) * P - 512 * n)
                            pe.matmul(bank[at + n][:, 0:w], q_parts[rows, g // 2, t * P:t * P + P], k_parts[rows, g // 2, 512 * n:512 * n + w],
                                      start=True, stop=(n != t // 4))
                        pe.matmul(bank[at + t // 4][:, P * (t % 4):P * (t % 4) + P], ident_b[:, :], above[:, :],
                                  start=False, stop=True).then_inc(a_mm, 1)

                    def for_weights(u):
                        g, j, at = u // TB, u % TB, 2 * buffer_b(u)
                        rows = slice(64 * (g % 2), 64 * (g % 2) + 64)
                        if u % 16 == 0:
                            pe.wait_ge(qaug_set, 2 * i + g // 2 + 1)
                        if u == 17:
                            pe.wait_ge(mx_read, 32 * i + 32)
                        elif 1 <= u <= 16:
                            pe.wait_ge(exp_done, 32 * i + u)
                        elif u > 17:
                            pe.wait_ge(exp_done, 32 * i + u - 1)
                        wide = L - P * j
                        for n in range((wide + 511) // 512):
                            w = min(512, wide - 512 * n)
                            last = pe.matmul(bank[at + n][:, 0:w], k_parts[rows, g // 2, P * j:P * j + P],
                                             q_less[rows, g // 2, P * j + 512 * n:P * j + 512 * n + w], start=True, stop=(n > 0))
                            if n == 0:
                                last = pe.matmul(bank[at][:, 0:P], ident_b[:, :], below[:, :], start=False, stop=True)
                        last.then_inc(b_mm, 1)

                    def values(g, t):
                        if t == 0:
                            pe.wait_ge(exp_done, 32 * i + 8 * g + 8)
                            if g >= 2:
                                pe.wait_ge(o_norm, 4 * i + g - 1)
                        for j in range(t + 1):
                            at = sum(TB - x for x in range(j)) * P + (t - j) * P
                            last = pe.matmul(bank[6 + g % 2][:, SLOT * t:SLOT * t + SLOT], probs[:, g % 2, at:at + P],
                                             vaug[:, ds(b * TB + j, 1), ds(r * 4 + g, 1), :].rearrange("p a h d -> p (a h d)"),
                                             start=(j == 0), stop=(j == t))
                        if t == TB - 1:
                            last.then_inc(c_mm, 1)

                    for u in range(17):
                        for_maxima(u)
                    turn_maxima(0)
                    for u in range(16):
                        for_weights(u)
                        if u < 15:
                            for_maxima(17 + u)
                        if u >= TB:
                            values(0, u - TB)
                    for t in range(4):
                        values(1, t)
                    turn_maxima(1)
                    values(1, 4)
                    for u in range(16, 32):
                        for_weights(u)
                        if u in (16, 17, 18):
                            values(1, u - 11)
                        if u >= 24:
                            values(2, u - 24)
                    for t in range(TB):
                        values(3, t)
            end_phase(pe)
            pe.wait_ge(ld6, 16 * 13)
            with pe.Fori(0, T) as i:
                pe.wait_ge(o_staged, i + 1)
                pe.wait_ge(o1T_set, i)
                pe.transpose(bank[0][:, 0:P], st_o[:, :], ident[:, :]).then_inc(o1_turned, 1)
                pe.wait_ge(o1T_set, i + 1)
                pe.wait_ge(pr_added, i)
                pe.matmul(bank[1][:, 0:D], oT1[:, :], wp1[:, :], start=True, stop=False)
                pe.matmul(bank[1][:, 0:D], ones_row[:, :], bp1[:, :], start=False, stop=True).then_inc(pr_mm, 1)
            pe.wait_ge(pr_added, T)
            with pe.Fori(0, T // 4) as i:
                pe.wait_ge(r_staged, i + 1)
                for t in range(4):
                    last = pe.transpose(bank[6][0:E1, P * t:P * t + P], st_r[:, E1 * t:E1 * t + E1], ident[:, :])
                last.then_inc(r_turned, 1)
                pe.wait_ge(rT_set, i + 1)
                for t in range(4):
                    last = pe.matmul(bank[7][:, P * t:P * t + P], rT[:, P * t:P * t + P], b2[:, :], start=True, stop=True)
                last.then_inc(rb_mm, 1)

                def second(e):
                    pe.wait_ge(h_silu, 4 * E1 * i + 4 * e + 4)
                    if e >= 2:
                        pe.wait_ge(e_added, 4 * E1 * i + 4 * (e - 1))
                    for t in range(4):
                        for c in range(4):
                            last = pe.matmul(bank[4 + e % 2][:, P * t:P * t + P], hT1[:, e % 2, c, P * t:P * t + P], w2[:, e, c, :],
                                             start=(c == 0), stop=(c == 3))
                    last.then_inc(e_mm, 1)

                for e in range(E1):
                    for c in range(4):
                        if e or c:
                            pe.wait_ge(h_silu, 4 * E1 * i + max(4 * e + c - 3, 0))
                        pe.matmul(bank[c], w1[:, e, P * c:P * c + P], xnT1[:, ds(i * 512, 512)], start=True, stop=True).then_inc(h_mm, 1)
                    if e:
                        second(e - 1)
                second(E1 - 1)

        @block.scalar
        def _(act):
            act.wait_ge(var_done, 1)
            act.activation(stats[:, 0, :], stats[:, 1, :], ACT.Sqrt).then_inc(std_done, 1)
            act.wait_ge(norm_done, 1)
            act.activation(fa[:, :], xn[:, :, :].rearrange("p t d -> p (t d)"), ACT.Abs).then_inc(sign_done, 1)
            act.activation(fsg[:, :], xn[:, :, :].rearrange("p t d -> p (t d)"), ACT.Sign).then_inc(sign_done, 1)
            act.wait_ge(wt_done, 1)
            act.wait_ge(ld1, 112)
            for m in range(2):
                act.copy(wguT[:, m, :], bank[m][:, 0:3 * P]).then_inc(wT_done, 1)
            act.copy(wdT[:, 0:2, :], bank[2][:, 0:2 * P].rearrange("p (c d) -> p c d", c=2))
            act.copy(wdT[0:INNER - 2 * P, 2, :], bank[2][0:INNER - 2 * P, 2 * P:3 * P]).then_inc(wT_done, 1)

            def begin_tile(i, y):
                act.wait_ge(x_turned, i + 1)
                act.copy(xnT[:, ds(i * P, P)], bank[0][:, 0:P]).then_inc(xT_done, 1)
                act.wait_ge(gu_done, i)
                act.copy(xqT[:, :], bank[0][:, P:2 * P]).then_inc(xT_done, 1)
                act.wait_ge(gu_done, i + 1)
                if not (isinstance(i, int) and i < 2):
                    act.wait_ge(hid_done, i - 1)
                act.activation(silu_g[:, y, :], bank[1 + 2 * y][:, 0:INNER], ACT.Silu).then_inc(silu_done, 1)

            def signs(i, y):
                act.wait_ge(hid_done, i + 1)
                if not (isinstance(i, int) and i < 2):
                    act.wait_ge(hq_done, i - 1)
                act.activation(fa[:, INNER * y:INNER * y + INNER], hid[:, y, :], ACT.Abs).then_inc(hsign_done, 1)
                act.activation(fsg[:, INNER * y:INNER * y + INNER], hid[:, y, :], ACT.Sign).then_inc(hsign_done, 1)

            def ffn_act(i, more, y=None):
                y = i % 2 if y is None else y
                if more:
                    begin_tile(i + 2, y)
                act.wait_ge(h_turned, i + 1)
                act.wait_ge(down_done, i)
                act.copy(hqT[:, 0:2, :], bank[5][:, 0:2 * P].rearrange("p (c d) -> p c d", c=2)).then_inc(hT_done, 1)
                act.copy(hqT[0:INNER - 2 * P, 2, :], bank[5][0:INNER - 2 * P, 2 * P:3 * P]).then_inc(hT_done, 1)
                if more:
                    signs(i + 2, y)

            for y in range(2):
                begin_tile(y, y)
                signs(y, y)
            ffn_steps(act, ffn_act)
            end_phase(act)
            act.wait_ge(g_bias, 1)
            for n in range(8):
                act.wait_ge(g_mm, n + 1)
                act.activation(gates[:, 512 * n:512 * n + 512], bank[n][0:5 * H0, :], ACT.Sigmoid, bias=bgate[:, 2:3]).then_inc(g_done, 1)
            act.wait_ge(g_done, 8)
            act.activation(sbeta[:, :], gates[0:H0, :], ACT.Sqrt).then_inc(sb_root, 1)
            act.wait_ge(bias_set, 5)
            with act.Fori(0, T // 2) as j:
                for y in range(2):
                    i = 2 * j + y
                    act.wait_ge(p_stored[y], 16 * j)
                    for n in range(8):
                        act.wait_ge(p_mm, 8 * i + n + 9)
                        act.activation(prj[:, y, 512 * n:512 * n + 512], bank[n], ACT.Silu).then_inc(p_silu, 1)
                    act.wait_ge(p_var, i + 1)
                    act.activation(prj_n[:, 1, :], prj_n[:, 0, :], ACT.Sqrt).then_inc(p_std, 1)
            for n in range(8):
                act.wait_ge(vv_turned, n + 1)
                act.activation(vrow[:, 512 * n:512 * n + 512], bank[n][0:H0, :], ACT.Sqrt).then_inc(vrow_root, 1)
            end_phase(act)
            chunk_act(act)
            with capped(act):
                with act.Fori(0, L // (2 * STEPS)) as i:
                    for s in range(2 * STEPS):
                        at = 2 * STEPS * i + s + 1
                        act.wait_ge(mixed, at)
                        act.activation(junk[:, :], banks[:, :], ACT.Square, accum_out=cap[:, 0:1]).then_inc(squared, 1)
                        act.wait_ge(ratio_set, at)
                        act.activation(cap[:, 2:3], cap[:, 1:2], ACT.Sqrt).then_inc(ratio_root, 1)
                        act.wait_ge(lam_set, at)
                        act.activation(S[:, :, :].rearrange("p k v -> p (k v)"), banks[:, :], ACT.Copy, scale=cap[:, 5:6]).then_inc(state_set, 1)
            end_phase(act)
            with act.Fori(0, T) as i:
                act.wait_ge(o_var, i + 1)
                act.activation(orn[:, :], orn[:, :], ACT.Sqrt).then_inc(o_std, 1)
                act.wait_ge(og_turned, i + 1)
                for n in range(2):
                    act.copy(ogT[:, 4 * n:4 * n + 4, :].rearrange("p c d -> p (c d)"), bank[n]).then_inc(ogT_set, 1)
            end_phase(act)
            act.wait_ge(cleared, len(again))
            act.drain()
            act.wait_ge(var_done, 2)
            act.activation(stats[:, 0, :], stats[:, 1, :], ACT.Sqrt).then_inc(std_done, 1)
            act.wait_ge(norm_done, 2)
            act.activation(route[:, 0:1, :], stats[:, 0:1, 0:E1], ACT.Exp)
            with act.Fori(0, T) as i:
                act.wait_ge(x1_turned, i + 1)
                act.copy(xnT1[:, ds(i * P, P)], bank[0][:, 0:P]).then_inc(x1T_set, 1)
                act.wait_ge(v_mm, i)
                act.copy(xt_x[:, :], bank[0][:, 0:P]).then_inc(x1T_set, 1)
            act.wait_ge(r_ready1, 1)
            act.activation(rt[:, 1, :, :], rt[:, 0, :, :], ACT.Exp).then_inc(r_exp, 1)
            with act.Fori(0, B) as b:
                with act.Fori(0, 4) as r:
                    i = b * 4 + r
                    for z in range(4):
                        act.wait_ge(pj_mm, 4 * i + z + 1)
                        if z >= 2:
                            act.wait_ge(rest_set, 4 * i + z - 1)
                        source = banks[:, 2048 + 1024 * (z % 2):3072 + 1024 * (z % 2)]
                        if z % 2:
                            act.activation(hi[:, 1, :], source, ACT.Identity, bias=part[:, 4:5]).then_inc(hi_set, 1)
                            for w in (z - 1, z):
                                act.wait_ge(rest_set, 4 * i + w + 1)
                                if w >= 2:
                                    act.wait_ge(qk_set, 4 * i + w - 1)
                                act.copy(mid[:, w % 2, :], rest[:, w % 2, :]).then_inc(mid_set, 1)
                        else:
                            act.copy(hi[:, 0, :], source).then_inc(hi_set, 1)
                    for u in range(32):
                        g, j = u // TB, u % TB
                        if j == 0:
                            act.wait_ge(c_mm, 4 * i + max(g - 1, 0))
                        act.wait_ge(b_mm, 32 * i + u + 1)
                        at, w = sum(TB - x for x in range(j)) * P, L - P * j
                        act.activation(probs[:, g % 2, at:at + w], banks[:, 1024 * buffer_b(u):1024 * buffer_b(u) + w], ACT.Exp,
                                       scale=D1 ** -0.5).then_inc(exp_done, 1)
            end_phase(act)
            with act.Fori(0, T) as i:
                act.wait_ge(o1_turned, i + 1)
                act.wait_ge(pr_mm, i)
                act.copy(oT1[:, :], bank[0][:, 0:P]).then_inc(o1T_set, 1)
            act.wait_ge(ld6, 16 * 13)
            with act.Fori(0, T // 4) as i:
                act.wait_ge(r_turned, i + 1)
                act.copy(rT[:, :], bank[6][0:E1, :]).then_inc(rT_set, 1)
                for e in range(E1):
                    act.wait_ge(e_mm, i * E1 + max(e - 1, 0))
                    for c in range(4):
                        act.wait_ge(h_mm, 4 * E1 * i + 4 * e + c + 1)
                        act.activation(hT1[:, e % 2, c, :], bank[c], ACT.Silu, bias=b1[:, e, c:c + 1]).then_inc(h_silu, 1)

        @block.vector
        def _(dve):
            seq = Count(dve, v_seq)
            dve.wait_ge(ld, 64)
            layernorm(dve, seq, res, xn, xnT, 0)
            dve.tensor_copy(stats[:, 3, 0:1], stats[:, 2, 0:1]).then_inc(norm_done, 1)
            xf = xn[:, :, :].rearrange("p t d -> p (t d)")
            quantize(dve, seq, xf, T * D // BLOCK, fa[:, :], fc[:, :], fsg[:, :], fsc,
                     xq[:, :, :].rearrange("p t d -> p (t d)"),
                     lambda: dve.wait_ge(sign_done, 2)).then_inc(xq_done, 1)
            dve.wait_ge(ld1, 112)
            dve.wait_ge(xq_done, 1)
            wneg = fa[:, NW:2 * NW]
            seq.link(dve.tensor_scalar(wneg, wraw[:, :], 0.0, None, ALU.is_lt))
            seq.link(dve.scalar_tensor_tensor(out=fsg[:, 0:NW], in0=wraw[:, :], scalar=0.0, in1=wneg,
                                              op0=ALU.is_gt, op1=ALU.subtract))
            seq.link(dve.tensor_tensor(fa[:, 0:NW], wraw[:, :], fsg[:, 0:NW], ALU.mult))
            quantize(dve, seq, wraw[:, :], NW // BLOCK, fa[:, 0:NW], fc[:, 0:NW], fsg[:, 0:NW], fsc,
                     wqt[:, :], lambda: None).then_inc(wq_done, 1)
            dve.wait_ge(wq_done, 1)
            ffn = Count(dve, v_ffn, per=13)

            def hidden(i, y):
                dve.wait_ge(silu_done, i + 1)
                if not (isinstance(i, int) and i < 2):
                    dve.wait_ge(hsign_done, 2 * i - 2)
                dve.tensor_tensor(hid[:, y, :], silu_g[:, y, :], bank[2 + 2 * y][:, 0:INNER], ALU.mult).then_inc(hid_done, 1)

            def add_down(i, y):
                dve.wait_ge(down_done, i + 1)
                dve.tensor_tensor(tile(res, i), tile(res, i), bank[6 + y][:, 0:D], ALU.add).then_inc(ffn_added, 1)

            def ffn_dve(i, more, y=None):
                y = i % 2 if y is None else y
                ffn.start(i)
                dve.wait_ge(hid_done, i + 1)
                dve.wait_ge(hq_done, i)

                def sign_ready():
                    dve.wait_ge(hsign_done, 2 * i + 2)
                    dve.wait_ge(h_turned, i)
                quantize(dve, ffn, hid[:, y, :], INNER // BLOCK, fa[:, INNER * y:INNER * y + INNER], fc[:, 0:INNER],
                         fsg[:, INNER * y:INNER * y + INNER], fsc, hq[:, :], sign_ready).then_inc(hq_done, 1)
                ffn.end()
                if more:
                    hidden(i + 2, y)
                if not (isinstance(i, int) and i == 0):
                    add_down(i - 1, 1 - y)

            hidden(0, 0)
            hidden(1, 1)
            ffn_steps(dve, ffn_dve)
            add_down(T - 1, 1)
            end_phase(dve)
            dve.wait_ge(ld2, 128)
            dve.tensor_tensor(bgate[:, 2:3], bgate[:, 0:1], bgate[:, 1:2], ALU.add).then_inc(g_bias, 1)
            raw3, rest3 = prj[0:3, 0, :], prj[0:3, 1, :]
            dve.memset(ones3[:, :], 1.0).then_inc(bias_set, 1)
            bia = Count(dve, bias_set)
            bia.n = 1
            bia.link(dve.tensor_copy(bias_hi[:, :], raw3))
            bia.link(dve.scalar_tensor_tensor(out=rest3, in0=bias_hi[:, :], scalar=bias_part[:, 0:1], in1=raw3, op0=ALU.mult, op1=ALU.add))
            bia.link(dve.tensor_copy(bias_hi[:, :], rest3))
            bia.link(dve.scalar_tensor_tensor(out=bias3[:, :], in0=bias_hi[:, :], scalar=bias_part[:, 1:2], in1=rest3, op0=ALU.mult, op1=ALU.add))
            dve.wait_ge(pb_turned, 1)
            dve.tensor_copy(sb_tok[:, :, :].rearrange("p t h -> p (t h)"), bank[0]).then_inc(sbt_set, 1)
            dve.wait_ge(sbt_set, 1)
            prc = Count(dve, v_prj, per=5)
            with dve.Fori(0, T // 2) as j:
                for y in range(2):
                    i = 2 * j + y
                    prc.start(i)
                    dve.wait_ge(p_silu, 8 * i + 12)
                    qk = prj[:, y, 0:2 * HD].rearrange("p (h d) -> p h d", d=DK)
                    qk_sq = prj_sq[:, :].rearrange("p (h d) -> p h d", d=DK)
                    root = sb_tok[:, ds(i, 1), :].rearrange("p a h -> p (a h)")
                    prc.link(dve.tensor_tensor(qk_sq, qk, qk, ALU.mult))
                    prc.link(dve.tensor_reduce(prj_n[:, 0, :], qk_sq, AX, ALU.add))
                    dve.tensor_scalar(prj_n[:, 0, :], prj_n[:, 0, :], 1e-6, None, ALU.add).then_inc(p_var, 1)
                    dve.wait_ge(p_silu, 8 * i + 14)
                    val = prj[:, y, 2 * HD:3 * HD].rearrange("p (h d) -> p h d", d=DK)
                    dve.tensor_tensor(val, val, root.unsqueeze(2).to_broadcast([P, H0, DK]), ALU.mult).then_inc(p_normed, 1)
                    dve.wait_ge(p_normed, 2 * i + 1)
                    prc.link(dve.tensor_tensor(qk_sq[:, 0:H0, :], val, val, ALU.mult))
                    dve.tensor_reduce(vv[:, ds(i, 1), :], qk_sq[:, 0:H0, :], AX, ALU.add).then_inc(vv_set, 1)
                    dve.wait_ge(p_std, i + 1)
                    prc.link(dve.reciprocal(prj_n[:, 0, :], prj_n[:, 1, :]))
                    prc.link(dve.tensor_tensor(prj_n[:, 0, H0:2 * H0], prj_n[:, 0, H0:2 * H0], root, ALU.mult))
                    prc.end()
                    dve.wait_ge(vv_set, i + 1)
                    dve.tensor_tensor(qk, qk, prj_n[:, 0, :].unsqueeze(2).to_broadcast([P, 2 * H0, DK]), ALU.mult).then_inc(p_normed, 1)
                    dve.wait_ge(p_normed, 2 * i + 2)
            end_phase(dve)
            chunk_dve(dve, seq)
            with capped(dve):
                pre = Count(dve, v_pre)
                dve.wait_ge(ld3, 16 * 17)
                dve.wait_ge(swap_set, 3)
                pre.link(dve.tensor_tensor(pair_sum[:, :], ident[:, 0:B * H0], ident[:, B * H0:P], ALU.add))
                pre.link(dve.scalar_tensor_tensor(out=mix[:, :], in0=mix[:, :], scalar=rf_col[:, 0:1], in1=ident[:, :], op0=ALU.mult, op1=ALU.add))
                pre.link(dve.memset(S[:, :, :], 0.0))
                dve.tensor_scalar(gndec[:, :], gdec[:, :], -1.0, None, ALU.mult).then_inc(r_ready, 1)
                dve.wait_ge(r_ready, 1)
                PER = 3 + 2 * STEPS * 9
                rec = Count(dve, v_rec, per=PER)
                with dve.Fori(0, L // (2 * STEPS)) as i:
                    rec.start(i)
                    for n, g in enumerate((gdec, gndec, gout)):
                        rec.link(dve.tensor_copy(gcur[:, n, :], g[:, ds(i * (2 * STEPS), 2 * STEPS)]))
                    for s in range(2 * STEPS):
                        n, k = s // STEPS, s % STEPS
                        at = 2 * STEPS * i + s + 1
                        q_, k_, v_ = (qkv[:, n, w, k, :] for w in range(3))
                        if k == 0:
                            dve.wait_ge(qkv_in[n], 16 * 24 * (i + 1))
                            dve.wait_ge(o_stored[n], 64 * i)
                        if s:
                            dve.wait_ge(state_set, at - 1)
                        rec.link(dve.tensor_tensor(prod[:, :, :], S[:, :, :], k_.unsqueeze(2).to_broadcast([P, DK, DK]), ALU.mult))
                        rec.link(dve.tensor_reduce(small[:, 0, :], prod[:, :, :].rearrange("p k v -> p v k"), AX, ALU.add))
                        rec.link(dve.scalar_tensor_tensor(out=small[:, 1, :], in0=small[:, 0, :], scalar=gcur[:, 1, s:s + 1], in1=v_, op0=ALU.mult, op1=ALU.add))
                        rec.link(dve.tensor_tensor(outer[:, :, :], k_.unsqueeze(2).to_broadcast([P, DK, DK]),
                                                   small[:, 1, :].unsqueeze(1).to_broadcast([P, DK, DK]), ALU.mult))
                        dve.scalar_tensor_tensor(out=Snew[:, :], in0=S[:, :, :].rearrange("p k v -> p (k v)"), scalar=gcur[:, 0, s:s + 1],
                                                 in1=outer[:, :, :].rearrange("p k v -> p (k v)"), op0=ALU.mult, op1=ALU.add).then_inc(updated, 1)
                        dve.wait_ge(squared, at)
                        dve.tensor_scalar(cap[:, 1:2], cap[:, 0:1], 1.0 / (DK * DK), 1.0, ALU.mult, ALU.max).then_inc(ratio_set, 1)
                        rec.link(dve.tensor_scalar(cap[:, 3:4], cap[:, 0:1], float(DK * DK), None, ALU.is_gt))
                        dve.wait_ge(ratio_root, at)
                        rec.link(dve.reciprocal(cap[:, 4:5], cap[:, 2:3]))
                        rec.link(dve.scalar_tensor_tensor(out=cap[:, 4:5], in0=cap[:, 4:5], scalar=-1.0, in1=cap[:, 3:4], op0=ALU.add, op1=ALU.mult))
                        dve.tensor_scalar(cap[:, 5:6], cap[:, 4:5], 1.0, None, ALU.add).then_inc(lam_set, 1)
                        dve.wait_ge(state_set, at)
                        rec.link(dve.tensor_tensor(prod[:, :, :], S[:, :, :], q_.unsqueeze(2).to_broadcast([P, DK, DK]), ALU.mult))
                        rec.link(dve.tensor_reduce(small[:, 0, :], prod[:, :, :].rearrange("p k v -> p v k"), AX, ALU.add))
                        last = dve.tensor_scalar(ohalf[:, k, :], small[:, 0, :], gcur[:, 2, s:s + 1], None, ALU.mult)
                        if k == STEPS - 1:
                            last.then_inc(answered, 1)
                            dve.wait_ge(summed, 2 * i + n + 1)
                            dve.tensor_copy(obuf[:, n, :, :].rearrange("p k d -> p (k d)"), bank[0][0:B * H0, 0:STEPS * DK]).then_inc(stepped[n], 1)
                    rec.end()
            end_phase(dve)
            oc = Count(dve, v_out, per=5)
            dve.wait_ge(ld4, 160)
            with dve.Fori(0, T) as i:
                oc.start(i)
                dve.wait_ge(om_in, 32 * (i + 1))
                o_h = om[:, 0, :].rearrange("p (h d) -> p h d", d=DK)
                oc.link(dve.tensor_tensor(osq[:, :], om[:, 0, :], om[:, 0, :], ALU.mult))
                oc.link(dve.tensor_reduce(orn[:, :], osq[:, :].rearrange("p (h d) -> p h d", d=DK), AX, ALU.add))
                dve.tensor_scalar(orn[:, :], orn[:, :], 1.0 / DK, 1e-5, ALU.mult, ALU.add).then_inc(o_var, 1)
                dve.wait_ge(o_std, i + 1)
                oc.link(dve.reciprocal(orn[:, :], orn[:, :]))
                oc.link(dve.tensor_tensor(o_h, o_h, orn[:, :].unsqueeze(2).to_broadcast([P, H0, DK]), ALU.mult))
                oc.link(dve.tensor_tensor(o_h, o_h, onw[:, :].unsqueeze(1).to_broadcast([P, H0, DK]), ALU.mult))
                oc.end()
                dve.wait_ge(og_turned, i)
                dve.tensor_tensor(og[:, :], om[:, 0, :], om[:, 2, :], ALU.mult).then_inc(og_set, 1)
                dve.wait_ge(o_mm, i + 1)
                dve.tensor_tensor(tile(res, i), tile(res, i), bank[2][:, 0:D], ALU.add).then_inc(o_added, 1)
            end_phase(dve)
            dve.wait_ge(cleared, len(again))
            dve.drain()
            layernorm(dve, seq, res, xn1, xnT1, 1)
            dve.tensor_copy(stats[:, 3, 0:1], stats[:, 2, 0:1]).then_inc(norm_done, 1)
            dve.wait_ge(mask_set, 7)
            dve.tensor_copy(ident_b[:, :], ident[:, :]).then_inc(c_set, 1)
            seq.link(dve.tensor_copy(number[:, :], number_i[:, :]))
            dve.wait_ge(ld5, 96)
            with dve.Fori(0, T) as i:
                dve.wait_ge(v_mm, i + 1)
                dve.tensor_copy(vaug[:, ds(i, 1), :, 0:D1].rearrange("p a h d -> p (a h) d"),
                                bank[1][:, 0:D].rearrange("p (h d) -> p h d", d=D1)).then_inc(v_set, 1)
                dve.tensor_tensor(tile(logit, i), bank[2][:, 0:E1], bg1[:, :], ALU.add).then_inc(v_set, 1)
            dve.wait_ge(v_set, 2 * T)
            wide = [P, T, E1]
            top = rs[:, 0, :]
            seq.link(dve.tensor_reduce(top, logit[:, :, :], AX, ALU.max))
            dve.tensor_tensor(rt[:, 0, :, :], logit[:, :, :], top.unsqueeze(2).to_broadcast(wide), ALU.subtract).then_inc(r_ready1, 1)
            dve.wait_ge(r_exp, 1)
            share = rt[:, 1, :, :]
            seq.link(dve.tensor_reduce(rs[:, 1, :], share, AX, ALU.add))
            seq.link(dve.reciprocal(rs[:, 0, :], rs[:, 1, :]))
            seq.link(dve.tensor_tensor(share, share, rs[:, 0, :].unsqueeze(2).to_broadcast(wide), ALU.mult))
            seq.link(dve.tensor_reduce(top, share, AX, ALU.max))
            best, cand = rt[:, 0, :, :], rt[:, 2, :, :]
            numbers = number[:, :].unsqueeze(1).to_broadcast(wide)
            seq.link(dve.tensor_tensor(best, share, top.unsqueeze(2).to_broadcast(wide), ALU.is_ge))
            seq.link(dve.scalar_tensor_tensor(out=cand, in0=numbers, scalar=-float(E1), in1=best, op0=ALU.add, op1=ALU.mult))
            seq.link(dve.tensor_reduce(rs[:, 1, :], cand, AX, ALU.min))
            seq.link(dve.scalar_tensor_tensor(out=best, in0=numbers, scalar=-float(E1), in1=rs[:, 1, :].unsqueeze(2).to_broadcast(wide),
                                              op0=ALU.add, op1=ALU.is_equal))
            seq.link(dve.tensor_tensor(route[:, :, :], best, share, ALU.mult))
            onc = Count(dve, v_on, per=10)
            with dve.Fori(0, B) as b:
                with dve.Fori(0, 4) as r:
                    i = b * 4 + r
                    onc.start(i)
                    def take_rest(z):
                        keys = z % 2
                        dve.wait_ge(hi_set, 4 * i + z + 1)
                        if z >= 2:
                            dve.wait_ge(mid_set, 4 * i + z - 1)
                        dve.scalar_tensor_tensor(out=rest[:, keys, :], in0=hi[:, keys, :], scalar=part[:, 2 * keys:2 * keys + 1],
                                                 in1=banks[:, 2048 + 1024 * keys:3072 + 1024 * keys],
                                                 op0=ALU.mult, op1=ALU.add).then_inc(rest_set, 1)

                    def take_part(z):
                        keys = z % 2
                        dve.wait_ge(mid_set, 4 * i + z + 1)
                        dve.scalar_tensor_tensor(out=(q_parts, k_parts)[keys][:, z // 2, :], in0=mid[:, keys, :],
                                                 scalar=part[:, 2 * keys + 1:2 * keys + 2], in1=rest[:, keys, :],
                                                 op0=ALU.mult, op1=ALU.add).then_inc(qk_set, 1)

                    take_rest(0)
                    take_rest(1)
                    take_part(0)
                    take_part(1)

                    def split_maxima(p):
                        dve.wait_ge(mx_read, 32 * i + 16 * p + 16)
                        top3 = mx[:, 2 * p:2 * p + 2, :]
                        if p == 0:
                            dve.wait_ge(mx_turned, 2 * i)
                        at = [mxz[:, p, :, :].rearrange("p t (g c) -> p g t c", g=2)[:, :, :, c:c + 1].rearrange("p g t c -> p g (t c)")
                              for c in (48, 49, 50)]
                        onc.link(dve.tensor_copy(at[0], top3))
                        onc.link(dve.tensor_tensor(mx_rest[:, :, :], top3, at[0], ALU.subtract))
                        onc.link(dve.tensor_copy(at[1], mx_rest[:, :, :]))
                        dve.tensor_tensor(at[2], mx_rest[:, :, :], at[1], ALU.subtract).then_inc(max_split, 1)

                    def less_maxima(p):
                        dve.wait_ge(mx_turned, 2 * i + p + 1)
                        dve.tensor_tensor(q_less[:, p, :], q_parts[:, p, :], banks[:, 2048:3072], ALU.subtract).then_inc(qaug_set, 1)

                    for u in range(32):
                        g, t = u // TB, u % TB
                        dve.wait_ge(a_mm, 32 * i + u + 1)
                        dve.tensor_reduce(mx[:, g, t:t + 1], banks[:, 1024 * buffer_a(u):1024 * buffer_a(u) + (t + 1) * P],
                                          AX, ALU.max).then_inc(mx_read, 1)
                        if u in (1, 3):
                            take_rest(2 + u // 2)
                        if u in (5, 7):
                            take_part(u // 2)
                        if u == 15:
                            split_maxima(0)
                        if u == 16:
                            less_maxima(0)
                    split_maxima(1)
                    less_maxima(1)
                    for g in range(4):
                        dve.wait_ge(c_mm, 4 * i + g + 1)
                        o_ps = bank[6 + g % 2][:, 0:TB * SLOT].rearrange("p (t d) -> p t d", d=SLOT)
                        onc.link(dve.reciprocal(inv_o[:, g, :], o_ps[:, :, D1:SLOT].rearrange("p t a -> p (t a)")))
                        dve.tensor_tensor(o_all[:, ds(b * TB, TB), ds(r * (4 * D1) + g * D1, D1)], o_ps[:, :, 0:D1],
                                          inv_o[:, g, :].unsqueeze(2).to_broadcast([P, TB, D1]), ALU.mult).then_inc(o_norm, 1)
                    onc.end()
            end_phase(dve)
            with dve.Fori(0, T) as i:
                dve.wait_ge(pr_mm, i + 1)
                dve.tensor_tensor(tile(res, i), tile(res, i), bank[1][:, 0:D], ALU.add).then_inc(pr_added, 1)
            dve.wait_ge(pr_added, T)
            with dve.Fori(0, T // 4) as i:
                group = res[:, ds(4 * i, 4), :]
                dve.wait_ge(rb_mm, i + 1)
                dve.tensor_tensor(group, group, bank[7].rearrange("p (t d) -> p t d", d=D), ALU.add).then_inc(rb_added, 1)
                dve.wait_ge(rb_added, i + 1)
                for e in range(E1):
                    dve.wait_ge(e_mm, i * E1 + e + 1)
                    if e:
                        dve.wait_ge(e_added, i * (4 * E1) + 4 * e)
                    for t in range(4):
                        row = res[:, ds(4 * i + t, 1), :].rearrange("p a d -> p (a d)")
                        dve.scalar_tensor_tensor(out=row, in0=bank[4 + e % 2][:, P * t:P * t + P], scalar=st_r[:, E1 * t + e:E1 * t + e + 1],
                                                 in1=row, op0=ALU.mult, op1=ALU.add).then_inc(e_added, 1)


def kernel(**inputs):
    import concourse.bacc as bacc
    from concourse.bass_utils import run_bass_kernel_spmd

    n = {k: np.ascontiguousarray(v) for k, v in inputs.items()}
    arrays = {
        "x": n["L0_attn_hidden_states"].reshape(B * L, D),
        "w_gate": n["L0_ffn_w_gate"], "w_up": n["L0_ffn_w_up"], "w_down": n["L0_ffn_w_down"],
    }
    m = {k[8:]: v for k, v in n.items() if k.startswith("L0_attn_")}
    for w in ("Wq", "Wk", "Wv", "Wg", "Wo"):
        arrays[w] = m[w]
    arrays["bproj"] = np.concatenate([m["bq"], m["bk"], m["bv"], m["bg"]])[None]
    arrays["bias_part"] = np.array([[0, 0], [-1, 0], [-1, -1]], np.float32)
    arrays["wgate"] = np.concatenate([m["Wb"], m["Wfd"], m["Wsd"], m["Wfg"], m["Wsg"]], 1)
    none = np.zeros(H0, np.float32)
    arrays["bgate"] = np.stack([np.concatenate([m["bb"], m["bfd"], m["bsd"], m["bfg"], m["bsg"]]),
                                np.concatenate([none, m["fast_decay_bias"], m["slow_decay_bias"], none, none])], 1)
    arrays["rf"] = m["resonance_flux"].reshape(1)
    arrays["onorm_w"] = m["onorm_w"]
    arrays["bo"] = m["bo"][None]
    of_q, of_k = (1, 1, 2, 2, 1, 3), (1, 2, 1, 2, 3, 1)
    for w in ("Wq", "Wk"):
        padded = np.zeros((D, H1, 64), np.float32)
        for n6 in range(6):
            padded[:, :, n6 * D1:n6 * D1 + D1] = n["L1_attn_" + w].T.reshape(D, H1, D1)
        arrays["W1" + w[1]] = padded.reshape(D, H1 // 2, P)
    part = np.zeros((2, 64, 5), np.float32)
    for c, parts in ((0, of_q), (2, of_k)):
        for n6, level in enumerate(parts):
            part[:, n6 * D1:n6 * D1 + D1, c] = -(level >= 2)
            part[:, n6 * D1:n6 * D1 + D1, c + 1] = -(level == 3)
    part[:, 6 * D1:6 * D1 + 3, 2] = 1.0
    part[:, 6 * D1:6 * D1 + 3, 4] = 1.0
    arrays["part"] = part.reshape(P, 5)
    arrays["W1v"] = n["L1_attn_Wv"].T
    arrays["W1p"] = n["L1_attn_Wp"].T
    arrays["bp1"] = n["L1_attn_bp"][None]
    arrays["Wg1"] = n["L1_ffn_Wg"]
    arrays["bg1"] = n["L1_ffn_bg"]
    arrays["W1"] = n["L1_ffn_W1"]
    arrays["W2"] = n["L1_ffn_W2"]
    arrays["b1"] = n["L1_ffn_b1"].reshape(E1, HID // P, P).transpose(2, 0, 1)
    arrays["b2"] = n["L1_ffn_b2"]
    arrays = {k: np.ascontiguousarray(v) for k, v in arrays.items()}
    nc = bacc.Bacc("TRN2", target_bir_lowering=False, num_devices=1)
    a = {k: nc.dram_tensor("in_" + k, v.shape, F32, kind="ExternalInput").ap() for k, v in arrays.items()}
    out = nc.dram_tensor("out_0", (B * L, D), F32, kind="ExternalOutput").ap()
    layer_kernel(nc, a, out)
    r = run_bass_kernel_spmd(nc, [{"in_" + k: v for k, v in arrays.items()}], core_ids=[0])
    return r.results[0]["out_0"].reshape(B, L, D)
```
